# Optimizing a Trainium2 kernel written in Bass

```python
import numpy as np
import jax
import jax.numpy as jnp

def _softmax(x, axis=-1):
    return jax.nn.softmax(x, axis=axis)

def _gelu(x):
    return jax.nn.gelu(x, approximate=True)

def _silu(x):
    return jax.nn.silu(x)

def _sigmoid(x):
    return jax.nn.sigmoid(x)

def _layernorm(x, axis=-1, eps=1e-05):
    m = jnp.mean(x, axis=axis, keepdims=True)
    v = jnp.var(x, axis=axis, keepdims=True)
    return (x - m) / jnp.sqrt(v + eps)

def _scatter_add(tgt, idx, src, axis=0):
    return tgt.at[idx].add(src)

def _segment_sum(src, seg, n):
    return jax.ops.segment_sum(src, seg, n)
kernel_name = 'mk_vit_tower_cls_d2_tok_img1024_r4_761f64'

def setup_inputs(seed: int=0):
    np.random.seed(seed)
    _w = jnp.asarray

    def _rec_inputs():
        import jax
        import jax.numpy as jnp
        _rk = jax.random.key(seed)
        x = -0.00016672 + 0.999947 * jax.random.normal(jax.random.fold_in(_rk, 1), (16, 3, 96, 96), jnp.float32)
        cls_tok = 0.02 * jax.random.normal(jax.random.fold_in(_rk, 5), (1, 1, 256), jnp.float32)
        return (x, cls_tok)
    x, cls_tok = _rec_inputs()

    def _L0_tok_setup():
        import jax, jax.numpy as jnp
        import numpy as np
        P = 16
        EPS = 1e-05

        def _layernorm(x, g, b):
            mu = jnp.mean(x, axis=-1, keepdims=True)
            var = jnp.mean(jnp.square(x - mu), axis=-1, keepdims=True)
            return (x - mu) * jax.lax.rsqrt(var + EPS) * g + b
        key = jax.random.key(seed)
        ks = jax.random.split(key, 7)
        B, C, H, W = (64, 3, 96, 96)
        patch_dim = C * P * P
        out_dim = 256
        x = jax.random.normal(ks[0], (B, C, H, W), dtype=jnp.float32)
        Wp = jax.random.normal(ks[1], (patch_dim, out_dim), dtype=jnp.float32) * (1.0 / np.sqrt(patch_dim))
        bp = jax.random.normal(ks[2], (out_dim,), dtype=jnp.float32) * 0.01
        ln1_g = jnp.ones((patch_dim,), dtype=jnp.float32)
        ln1_b = jnp.zeros((patch_dim,), dtype=jnp.float32)
        ln2_g = jnp.ones((out_dim,), dtype=jnp.float32)
        ln2_b = jnp.zeros((out_dim,), dtype=jnp.float32)
        return {'x': x, 'Wp': Wp, 'bp': bp, 'ln1_g': ln1_g, 'ln1_b': ln1_b, 'ln2_g': ln2_g, 'ln2_b': ln2_b}
    _L0_tok_all = _L0_tok_setup()
    _L0_tok_in = {k: v for k, v in _L0_tok_all.items() if k in ('Wp', 'bp', 'ln1_g', 'ln1_b', 'ln2_g', 'ln2_b')}
    del _L0_tok_all

    def _L0_attn_setup():
        import jax, jax.numpy as jnp
        import numpy as np
        import math
        D_MODEL = 256
        NUM_HEADS = 16
        D_HEAD = D_MODEL // NUM_HEADS
        SEQ = 512
        BATCH = 2
        THETA = 10000.0
        SCALE = 1.0 / math.sqrt(D_HEAD)

        def rope_cos_sin(seq_len, d_head, theta):
            inv_freq = 1.0 / theta ** (jnp.arange(0, d_head, 2, dtype=jnp.float32) / d_head)
            t = jnp.arange(seq_len, dtype=jnp.float32)
            ang = jnp.outer(t, inv_freq)
            return (jnp.cos(ang), jnp.sin(ang))

        def apply_rope(x, cos, sin):
            B, S, H, Dh = x.shape
            xr = x.reshape(B, S, H, Dh // 2, 2)
            x0, x1 = (xr[..., 0], xr[..., 1])
            c = cos[None, :, None, :]
            s = sin[None, :, None, :]
            out = jnp.stack([x0 * c - x1 * s, x0 * s + x1 * c], axis=-1)
            return out.reshape(B, S, H, Dh)
        key = jax.random.key(seed)
        ks = jax.random.split(key, 9)
        w_std = 0.02
        return {'qkv': jax.random.normal(ks[0], (BATCH, SEQ, D_MODEL), jnp.float32), 'Wq': jax.random.normal(ks[1], (D_MODEL, D_MODEL), jnp.float32) * w_std, 'bq': jax.random.normal(ks[2], (D_MODEL,), jnp.float32) * w_std, 'Wk': jax.random.normal(ks[3], (D_MODEL, D_MODEL), jnp.float32) * w_std, 'bk': jax.random.normal(ks[4], (D_MODEL,), jnp.float32) * w_std, 'Wv': jax.random.normal(ks[5], (D_MODEL, D_MODEL), jnp.float32) * w_std, 'bv': jax.random.normal(ks[6], (D_MODEL,), jnp.float32) * w_std, 'Wo': jax.random.normal(ks[7], (D_MODEL, D_MODEL), jnp.float32) * w_std, 'bo': jax.random.normal(ks[8], (D_MODEL,), jnp.float32) * w_std}
    _L0_attn_all = _L0_attn_setup()
    _L0_attn_in = {k: v for k, v in _L0_attn_all.items() if k in ('Wq', 'bq', 'Wk', 'bk', 'Wv', 'bv', 'Wo', 'bo')}
    del _L0_attn_all

    def _L0_ffn_setup():
        import jax, jax.numpy as jnp
        import numpy as np
        E, D, F = (8, 256, 1024)
        B, S = (4, 512)

        def _layernorm(x, g, b, eps=1e-05):
            mu = jnp.mean(x, axis=-1, keepdims=True)
            var = jnp.var(x, axis=-1, keepdims=True)
            return (x - mu) * jax.lax.rsqrt(var + eps) * g + b
        key = jax.random.key(seed)
        ks = jax.random.split(key, 5)
        return {'input_features': jax.random.normal(ks[0], (B, S, D), jnp.float32), 'centroids': jax.random.normal(ks[1], (E, D), jnp.float32) * 0.1, 'ln_g': jnp.ones((E, D), jnp.float32), 'ln_b': jnp.zeros((E, D), jnp.float32), 'w1': jax.random.normal(ks[2], (E, F, D), jnp.float32) * (1.0 / np.sqrt(D).astype(np.float32)), 'b1': jnp.zeros((E, F), jnp.float32), 'w2': jax.random.normal(ks[3], (E, D, F), jnp.float32) * (1.0 / np.sqrt(F).astype(np.float32)), 'b2': jnp.zeros((E, D), jnp.float32)}
    _L0_ffn_all = _L0_ffn_setup()
    _L0_ffn_in = {k: v for k, v in _L0_ffn_all.items() if k in ('centroids', 'ln_g', 'ln_b', 'w1', 'b1', 'w2', 'b2')}
    del _L0_ffn_all

    def _L1_attn_setup():
        import jax, jax.numpy as jnp
        import numpy as np
        B, S, H, NH = (2, 512, 256, 16)
        HD = H // NH
        SCALE = HD ** (-0.5)
        EPS = 1e-05

        def _weight_quant(w):
            scale = 1.0 / jnp.clip(jnp.mean(jnp.abs(w)), 1e-05)
            wq = jnp.clip(jnp.round(w * scale), -1.0, 1.0) / scale
            return w + jax.lax.stop_gradient(wq - w)

        def _act_quant(x):
            scale = 127.0 / jnp.clip(jnp.max(jnp.abs(x), axis=-1, keepdims=True), 1e-05)
            y = jnp.clip(jnp.round(x * scale), -128.0, 127.0) / scale
            return x + jax.lax.stop_gradient(y - x)

        def _bitlinear(x, w):
            mu = jnp.mean(x, axis=(1, 2), keepdims=True)
            var = jnp.var(x, axis=(1, 2), keepdims=True)
            x_norm = (x - mu) * jax.lax.rsqrt(var + EPS)
            return _act_quant(x_norm) @ _weight_quant(w).T
        key = jax.random.key(seed)
        kx, k1, k2, k3, k4 = jax.random.split(key, 5)
        x = jax.random.normal(kx, (B, S, H), dtype=jnp.float32)
        init = 0.02
        w_q = jax.random.normal(k1, (H, H), dtype=jnp.float32) * init
        w_k = jax.random.normal(k2, (H, H), dtype=jnp.float32) * init
        w_v = jax.random.normal(k3, (H, H), dtype=jnp.float32) * init
        w_o = jax.random.normal(k4, (H, H), dtype=jnp.float32) * init
        return {'x': x, 'w_q': w_q, 'w_k': w_k, 'w_v': w_v, 'w_o': w_o}
    _L1_attn_all = _L1_attn_setup()
    _L1_attn_in = {k: v for k, v in _L1_attn_all.items() if k in ('w_q', 'w_k', 'w_v', 'w_o')}
    del _L1_attn_all

    def _L1_ffn_setup():
        import jax, jax.numpy as jnp
        import numpy as np
        B, S, DIM, FFN, E = (4, 512, 256, 1024, 8)
        key = jax.random.key(seed)
        k0, k1, k2, k3 = jax.random.split(key, 4)
        scale = 0.02
        return {'hidden_states': jax.random.normal(k0, (B, S, DIM), jnp.float32), 'router_w': jax.random.normal(k1, (DIM, E), jnp.float32) * scale, 'router_b': jnp.zeros((E,), jnp.float32), 'w1': jax.random.normal(k2, (E, DIM, 2 * FFN), jnp.float32) * scale, 'w2': jax.random.normal(k3, (E, FFN, DIM), jnp.float32) * scale}
    _L1_ffn_all = _L1_ffn_setup()
    _L1_ffn_in = {k: v for k, v in _L1_ffn_all.items() if k in ('router_w', 'router_b', 'w1', 'w2')}
    del _L1_ffn_all
    return {'x': x, 'cls_tok': cls_tok, 'L0_tok_Wp': _L0_tok_in['Wp'], 'L0_tok_bp': _L0_tok_in['bp'], 'L0_tok_ln1_g': _L0_tok_in['ln1_g'], 'L0_tok_ln1_b': _L0_tok_in['ln1_b'], 'L0_tok_ln2_g': _L0_tok_in['ln2_g'], 'L0_tok_ln2_b': _L0_tok_in['ln2_b'], 'L0_attn_Wq': _L0_attn_in['Wq'], 'L0_attn_bq': _L0_attn_in['bq'], 'L0_attn_Wk': _L0_attn_in['Wk'], 'L0_attn_bk': _L0_attn_in['bk'], 'L0_attn_Wv': _L0_attn_in['Wv'], 'L0_attn_bv': _L0_attn_in['bv'], 'L0_attn_Wo': _L0_attn_in['Wo'], 'L0_attn_bo': _L0_attn_in['bo'], 'L0_ffn_centroids': _L0_ffn_in['centroids'], 'L0_ffn_ln_g': _L0_ffn_in['ln_g'], 'L0_ffn_ln_b': _L0_ffn_in['ln_b'], 'L0_ffn_w1': _L0_ffn_in['w1'], 'L0_ffn_b1': _L0_ffn_in['b1'], 'L0_ffn_w2': _L0_ffn_in['w2'], 'L0_ffn_b2': _L0_ffn_in['b2'], 'L1_attn_w_q': _L1_attn_in['w_q'], 'L1_attn_w_k': _L1_attn_in['w_k'], 'L1_attn_w_v': _L1_attn_in['w_v'], 'L1_attn_w_o': _L1_attn_in['w_o'], 'L1_ffn_router_w': _L1_ffn_in['router_w'], 'L1_ffn_router_b': _L1_ffn_in['router_b'], 'L1_ffn_w1': _L1_ffn_in['w1'], 'L1_ffn_w2': _L1_ffn_in['w2']}

def reference(x, cls_tok, L0_tok_Wp, L0_tok_bp, L0_tok_ln1_g, L0_tok_ln1_b, L0_tok_ln2_g, L0_tok_ln2_b, L0_attn_Wq, L0_attn_bq, L0_attn_Wk, L0_attn_bk, L0_attn_Wv, L0_attn_bv, L0_attn_Wo, L0_attn_bo, L0_ffn_centroids, L0_ffn_ln_g, L0_ffn_ln_b, L0_ffn_w1, L0_ffn_b1, L0_ffn_w2, L0_ffn_b2, L1_attn_w_q, L1_attn_w_k, L1_attn_w_v, L1_attn_w_o, L1_ffn_router_w, L1_ffn_router_b, L1_ffn_w1, L1_ffn_w2):
    import jax
    import jax.numpy as jnp

    def _L0_tok_ref(x, Wp, bp, ln1_g, ln1_b, ln2_g, ln2_b):
        import jax, jax.numpy as jnp
        import numpy as np
        P = 16
        EPS = 1e-05

        def _layernorm(x, g, b):
            mu = jnp.mean(x, axis=-1, keepdims=True)
            var = jnp.mean(jnp.square(x - mu), axis=-1, keepdims=True)
            return (x - mu) * jax.lax.rsqrt(var + EPS) * g + b
        B, C, H, W = x.shape
        h, w = (H // P, W // P)
        patches = x.reshape(B, C, h, P, w, P)
        patches = jnp.transpose(patches, (0, 2, 4, 3, 5, 1))
        patches = patches.reshape(B, h * w, P * P * C)
        y = _layernorm(patches, ln1_g, ln1_b)
        y = jnp.einsum('bnd,de->bne', y, Wp) + bp
        y = _layernorm(y, ln2_g, ln2_b)
        return y

    def _L0_attn_ref(qkv, Wq, bq, Wk, bk, Wv, bv, Wo, bo):
        import jax, jax.numpy as jnp
        import numpy as np
        import math
        D_MODEL = 256
        NUM_HEADS = 16
        D_HEAD = D_MODEL // NUM_HEADS
        SEQ = 512
        BATCH = 2
        THETA = 10000.0
        SCALE = 1.0 / math.sqrt(D_HEAD)

        def rope_cos_sin(seq_len, d_head, theta):
            inv_freq = 1.0 / theta ** (jnp.arange(0, d_head, 2, dtype=jnp.float32) / d_head)
            t = jnp.arange(seq_len, dtype=jnp.float32)
            ang = jnp.outer(t, inv_freq)
            return (jnp.cos(ang), jnp.sin(ang))

        def apply_rope(x, cos, sin):
            B, S, H, Dh = x.shape
            xr = x.reshape(B, S, H, Dh // 2, 2)
            x0, x1 = (xr[..., 0], xr[..., 1])
            c = cos[None, :, None, :]
            s = sin[None, :, None, :]
            out = jnp.stack([x0 * c - x1 * s, x0 * s + x1 * c], axis=-1)
            return out.reshape(B, S, H, Dh)
        B, S, D = qkv.shape
        cos, sin = rope_cos_sin(S, D_HEAD, THETA)
        q = (qkv @ Wq.T + bq).reshape(B, S, NUM_HEADS, D_HEAD)
        k = (qkv @ Wk.T + bk).reshape(B, S, NUM_HEADS, D_HEAD)
        v = (qkv @ Wv.T + bv).reshape(B, S, NUM_HEADS, D_HEAD)
        q = apply_rope(q, cos, sin)
        k = apply_rope(k, cos, sin)
        scores = jnp.einsum('bqhd,bkhd->bhqk', q, k) * SCALE
        causal = jnp.triu(jnp.ones((S, S), dtype=bool), k=1)
        scores = jnp.where(causal[None, None], -1e+30, scores)
        attn = jax.nn.softmax(scores, axis=-1)
        out = jnp.einsum('bhqk,bkhd->bqhd', attn, v).reshape(B, S, D)
        return out @ Wo.T + bo

    def _L0_ffn_ref(input_features, centroids, ln_g, ln_b, w1, b1, w2, b2):
        import jax, jax.numpy as jnp
        import numpy as np
        E, D, F = (8, 256, 1024)
        B, S = (4, 512)

        def _layernorm(x, g, b, eps=1e-05):
            mu = jnp.mean(x, axis=-1, keepdims=True)
            var = jnp.var(x, axis=-1, keepdims=True)
            return (x - mu) * jax.lax.rsqrt(var + eps) * g + b
        Bf, Sf, Df = input_features.shape
        x = input_features.reshape(-1, Df)
        aff = x @ centroids.T
        assign = jnp.argmax(aff, axis=1)
        order = jnp.argsort(assign)
        xs = x[order]
        es = assign[order]
        alpha = jax.nn.sigmoid(jnp.take_along_axis(aff[order], es[:, None], axis=1))
        nE = centroids.shape[0]
        y = jnp.zeros_like(xs)
        for e in range(nE):
            h = _layernorm(xs, ln_g[e], ln_b[e])
            h = jax.nn.relu(h @ w1[e].T + b1[e])
            ye = xs + h @ w2[e].T + b2[e]
            y = y + jnp.where((es == e)[:, None], ye, 0.0)
        out_sorted = alpha * y + (1.0 - alpha) * xs
        inv = jnp.argsort(order)
        return out_sorted[inv].reshape(Bf, Sf, Df)

    def _L1_attn_ref(x, w_q, w_k, w_v, w_o):
        import jax, jax.numpy as jnp
        import numpy as np
        B, S, H, NH = (2, 512, 256, 16)
        HD = H // NH
        SCALE = HD ** (-0.5)
        EPS = 1e-05

        def _weight_quant(w):
            scale = 1.0 / jnp.clip(jnp.mean(jnp.abs(w)), 1e-05)
            wq = jnp.clip(jnp.round(w * scale), -1.0, 1.0) / scale
            return w + jax.lax.stop_gradient(wq - w)

        def _act_quant(x):
            scale = 127.0 / jnp.clip(jnp.max(jnp.abs(x), axis=-1, keepdims=True), 1e-05)
            y = jnp.clip(jnp.round(x * scale), -128.0, 127.0) / scale
            return x + jax.lax.stop_gradient(y - x)

        def _bitlinear(x, w):
            mu = jnp.mean(x, axis=(1, 2), keepdims=True)
            var = jnp.var(x, axis=(1, 2), keepdims=True)
            x_norm = (x - mu) * jax.lax.rsqrt(var + EPS)
            return _act_quant(x_norm) @ _weight_quant(w).T
        bsz, seq_len, hidden = x.shape
        q = _bitlinear(x, w_q).reshape(bsz, seq_len, NH, HD).transpose(0, 2, 1, 3)
        k = _bitlinear(x, w_k).reshape(bsz, seq_len, NH, HD).transpose(0, 2, 1, 3)
        v = _bitlinear(x, w_v).reshape(bsz, seq_len, NH, HD).transpose(0, 2, 1, 3)
        scores = jnp.einsum('bhqd,bhkd->bhqk', q, k) * SCALE
        attn = jax.nn.softmax(scores, axis=-1)
        out = jnp.einsum('bhqk,bhkd->bhqd', attn, v)
        out = out.transpose(0, 2, 1, 3).reshape(bsz, seq_len, hidden)
        return _bitlinear(out, w_o)

    def _L1_ffn_ref(hidden_states, router_w, router_b, w1, w2):
        import jax, jax.numpy as jnp
        import numpy as np
        B, S, DIM, FFN, E = (4, 512, 256, 1024, 8)
        b, s, d = hidden_states.shape
        x = hidden_states.reshape(-1, d)
        logits = x @ router_w + router_b
        route = jax.nn.softmax(logits, axis=1)
        max_prob = jnp.max(route, axis=1, keepdims=True)
        max_ind = jnp.argmax(route, axis=1)
        out = jnp.zeros_like(x)
        num_experts = w1.shape[0]
        for e in range(num_experts):
            h = x @ w1[e]
            a, g = jnp.split(h, 2, axis=1)
            y = jax.nn.silu(a) * g @ w2[e]
            out = jnp.where((max_ind == e)[:, None], y, out)
        out = out * max_prob
        return out.reshape(b, s, d)
    h = _L0_tok_ref(x, L0_tok_Wp, L0_tok_bp, L0_tok_ln1_g, L0_tok_ln1_b, L0_tok_ln2_g, L0_tok_ln2_b)
    h = jnp.concatenate([jnp.broadcast_to(cls_tok, (h.shape[0], 1, h.shape[2])), h], axis=1)
    h = h + _L0_attn_ref(_layernorm(h, axis=-1), L0_attn_Wq, L0_attn_bq, L0_attn_Wk, L0_attn_bk, L0_attn_Wv, L0_attn_bv, L0_attn_Wo, L0_attn_bo)
    h = h + _L0_ffn_ref(_layernorm(h, axis=-1), L0_ffn_centroids, L0_ffn_ln_g, L0_ffn_ln_b, L0_ffn_w1, L0_ffn_b1, L0_ffn_w2, L0_ffn_b2)
    h = h + _L1_attn_ref(_layernorm(h, axis=-1), L1_attn_w_q, L1_attn_w_k, L1_attn_w_v, L1_attn_w_o)
    h = h + _L1_ffn_ref(_layernorm(h, axis=-1), L1_ffn_router_w, L1_ffn_router_b, L1_ffn_w1, L1_ffn_w2)
    return h

_drawn_inputs = setup_inputs


def setup_inputs(seed=0):
    import zlib

    import numpy as np

    out = dict(_drawn_inputs(seed))
    spreads = {'L0_tok_ln1_g': (1.0, 0.2),
     'L0_tok_ln1_b': (0.0, 0.1),
     'L0_tok_ln2_g': (1.0, 0.2),
     'L0_tok_ln2_b': (0.0, 0.1),
     'L0_ffn_ln_g': (1.0, 0.2),
     'L0_ffn_ln_b': (0.0, 0.267),
     'L0_ffn_b1': (0.0, 0.1),
     'L0_ffn_b2': (0.0, 0.1),
     'L1_ffn_router_b': (0.0, 0.8)}
    factors = {'L0_attn_bq': 31.591,
     'L0_attn_bk': 34.648,
     'L1_attn_w_q': 8.0,
     'L1_attn_w_k': 8.0,
     'L1_ffn_router_w': 8.0,
     'L1_ffn_w1': 8.0,
     'L1_ffn_w2': 8.0}
    for name, (base, spread) in spreads.items():
        noise = np.random.default_rng([zlib.crc32(name.encode()), seed]).standard_normal(out[name].shape)
        drawn = base * np.exp(spread * noise) if base else spread * noise
        out[name] = jnp.asarray(drawn.astype(out[name].dtype))
    for name, factor in factors.items():
        out[name] = (out[name] * factor).astype(out[name].dtype)
    return out
```

```python
from contextlib import ExitStack

import numpy as np

import concourse.bass as bass
from concourse import mybir

P = 128
IMAGES, CHANNELS, SIDE, PATCH = 16, 3, 96, 16
GRID = SIDE // PATCH
SEQ = GRID * GRID + 1
TOKENS = IMAGES * SEQ
TILES = -(-TOKENS // P)
ROWS = TILES * P
D = 256
DC = D // P
PD = PATCH * PATCH * CHANNELS
PC = PD // P
HEADS, HD = 16, 16
PAIRS = IMAGES // 2
PW = 2 * SEQ
QPAD = 64
EXPERTS, FF = 8, 1024
FC = FF // P
WIN = P
WINDOWS = (TOKENS - EXPERTS) // WIN + EXPERTS
MIN_WINDOWS = -(-TOKENS // WIN)
DUMP = WINDOWS * WIN
SLOTS = DUMP + P
EPS = 1e-5
SCALE = HD ** -0.5
NEG = -1e30
HALF_EVEN = 12582912.0

F32 = mybir.dt.float32
BF16 = mybir.dt.bfloat16
I32 = mybir.dt.int32
ALU = mybir.AluOpType
ACT = mybir.ActivationFunctionType
AX = mybir.AxisListType


def constant_columns():
    p = np.arange(P)[:, None]
    token = np.arange(ROWS).reshape(TILES, P).T
    inv_freq = 1.0 / 10000.0 ** (np.arange(0, HD, 2, dtype=np.float32) / HD)
    angle = np.outer(np.arange(SEQ, dtype=np.float32), inv_freq.astype(np.float32))
    freq = (np.arange(P) % HD) // 2
    sign = np.where(np.arange(P) % 2 == 0, -1.0, 1.0)[:, None]
    q = np.arange(P) % QPAD
    causal = np.where(np.arange(SEQ)[None, :] > q[:, None], NEG, 0.0)
    valid = (token < TOKENS)
    image = np.where(valid, token // SEQ, -1)
    is_patch = valid & (token % SEQ != 0)
    flat = np.arange(ROWS)
    tables = {
        "ident": np.eye(P),
        "cos": np.cos(angle).T[freq],
        "sin": sign * np.sin(angle).T[freq],
        "causal": np.tile(causal, (1, 8)),
        "head4": ((p // HD) % 4 == np.arange(4)[None, :]),
        "head2": ((p // SEQ) == (np.arange(D)[None, :] // HD) % 2),
        "of_image": (image[:, :, None] == np.arange(IMAGES)).reshape(P, -1),
        "image_of": np.pad((flat // SEQ)[None, :] == np.arange(IMAGES)[:, None], ((0, P - IMAGES), (0, 0))),
        "patch_row": np.pad(np.stack([(flat % SEQ == 0), (flat % SEQ != 0)]), ((0, P - 2), (0, 0))),
        "is_patch": is_patch,
        "valid": valid,
        "pad_slot": np.where(valid, 0, DUMP + token - TOKENS),
        "earlier": np.triu(np.ones((P, P)), 1),
        "ones": np.ones((P, P)),
        "first": np.broadcast_to(EXPERTS - np.arange(EXPERTS), (P, EXPERTS)),
        "full": np.broadcast_to(WIN * np.arange(TILES), (P, TILES)),
        "upto": np.broadcast_to(np.tril(np.ones((EXPERTS, EXPERTS))).reshape(-1), (P, EXPERTS * EXPERTS)),
        "window": np.broadcast_to(np.arange(WINDOWS), (P, WINDOWS)),
        "minus_half": np.full((P, TILES), -0.5),
    }
    where, at = {}, 0
    for name, table in tables.items():
        where[name] = (at, at + table.shape[1])
        at += table.shape[1]
    return np.concatenate([np.asarray(t, np.float32) for t in tables.values()], 1), where


CONST, CONST_AT = constant_columns()


def vit_tower(nc, xp, cls_ln2b, Wp, ln1, bp, ln2_g, const, wa0, ba0, wo0, bo0, cent, w1_0, w2_0, par_0, b2_0,
              wa1, router, router_b, w1_1, w2_1, out):
    with ExitStack() as ctx:
        def sb(name, shape, dt=F32):
            return ctx.enter_context(nc.sbuf_tensor(name, shape, dt))

        def sem(name):
            return ctx.enter_context(nc.semaphore(name))

        slots_in = nc.dram_tensor("slots_in", [SLOTS, D], F32)
        slots_out = nc.dram_tensor("slots_out", [SLOTS, D], F32)

        cst = sb("cst", [P, CONST.shape[1]])

        def table(name, rows=P):
            a, b = CONST_AT[name]
            return cst[0:rows, a:b]

        ident = table("ident")
        identb = sb("identb", [P, P], BF16)
        patches = sb("patches", [P, TILES, PD])
        patchT = sb("patchT", [P, PC, ROWS])
        wp_s = sb("wp_s", [P, PC, D])
        ln1_s = sb("ln1_s", [P, 2, PC])
        bp_s = sb("bp_s", [P, D])
        ln2g_s = sb("ln2g_s", [P, D])
        cls_s = sb("cls_s", [2, D])
        wa0_s = sb("wa0_s", [P, DC, 5, D])
        ba0_s = sb("ba0_s", [P, 5, DC])
        wo0_s = sb("wo0_s", [P, DC, D])
        bo0_s = sb("bo0_s", [P, D])
        cent_s = sb("cent_s", [P, DC, EXPERTS])
        wa1_s = sb("wa1_s", [P, DC, 4, D])
        wq1_s = sb("wq1_s", [P, DC, 4, D], BF16)
        router_s = sb("router_s", [P, DC, EXPERTS])
        routerb_s = sb("routerb_s", [P, EXPERTS])

        h = sb("h", [P, TILES, D])
        x = sb("x", [P, TILES, D])
        xd = sb("xd", [P, TILES, D])
        z = sb("z", [P, TILES, D])
        xT = sb("xT", [P, DC, ROWS])
        oT = sb("oT", [P, DC, ROWS])
        xqb = sb("xqb", [P, TILES, D], BF16)
        xTb = sb("xTb", [P, DC, ROWS], BF16)
        stats = sb("stats", [P, TILES, 3, 6])
        mv = sb("mv", [P, TILES, 2])
        veps = sb("veps", [P, TILES])
        rstd = sb("rstd", [P, TILES])
        stat2 = sb("stat2", [P, TILES, 3])
        img = sb("img", [IMAGES, 8])
        tokstat = sb("tokstat", [P, TILES, 2])
        amax = sb("amax", [P, TILES])
        inv_s = sb("inv_s", [P, TILES])
        act_s = sb("act_s", [P, TILES])
        spread = sb("spread", [P, TILES, P])
        invT = sb("invT", [P, ROWS])
        wsum = sb("wsum", [P, 4])
        wmean = sb("wmean", [P, 4])
        wscale = sb("wscale", [P, 4])
        qk_scale = sb("qk_scale", [P, 1])

        rope_bias = sb("rope_bias", [P, 4, SEQ])
        rope_c = sb("rope_c", [P, 8, SEQ])
        rope_s = sb("rope_s", [P, 8, SEQ])
        qT = sb("qT", [P, 2, DC, 2, QPAD])
        kT = sb("kT", [P, DC, PW])
        kM = sb("kM", [P, 2, DC, 2, 4, SEQ])
        vR = sb("vR", [P, DC, 2, 2, SEQ])
        vM = sb("vM", [PW, 2, 2, D])
        sc = sb("sc", [P, 2, 8 * SEQ])
        prob = sb("prob", [P, HEADS, SEQ])
        smax = sb("smax", [P, HEADS])
        ssum = sb("ssum", [P, HEADS])
        srec = sb("srec", [P, HEADS])
        pT = sb("pT", [PW, 8, P])

        lg = sb("lg", [P, TILES, EXPERTS])
        lmax = sb("lmax", [P, TILES])
        lexp = sb("lexp", [P, TILES, EXPERTS])
        gate = sb("gate", [P, TILES])
        r1 = sb("r1", [P, TILES, EXPERTS])
        rsmall = sb("rsmall", [P, TILES])
        hot = sb("hot", [P, TILES, EXPERTS])
        total = sb("total", [P, TILES, EXPERTS])
        before = sb("before", [P, TILES + 1, EXPERTS])
        rank = sb("rank", [P, TILES, EXPERTS])
        cmp = sb("cmp", [P, WINDOWS * EXPERTS])
        nwin = sb("nwin", [P, EXPERTS])
        wend = sb("wend", [P, EXPERTS])
        wbeg = sb("wbeg", [P, EXPERTS])
        winexp = sb("winexp", [P, WINDOWS + 3])
        winexp_i = sb("winexp_i", [P, WINDOWS + 3], I32)
        slot_f = sb("slot_f", [P, TILES])
        slot_i = sb("slot_i", [P, TILES], I32)

        zero = sb("zero", [P, D])
        stored = sb("stored", [1, 1])
        w1_s = sb("w1_s", [P, 2, DC * 2 * FF])
        w2_s = sb("w2_s", [P, 2, FC, D])
        par_s = sb("par_s", [P, 2, 2 * DC + FC])
        b2_s = sb("b2_s", [P, 2, D])
        xw = sb("xw", [P, 2, D])
        xwT = sb("xwT", [P, DC, WIN])
        hid = sb("hid", [P, FC, WIN])
        act_a = sb("act_a", [P, 2, WIN])
        zw = sb("zw", [P, 2, D])

        psum = ctx.enter_context(nc.psum_tensor("psum", [P, 8, 512], F32))

        block = None
        S = {}

        def s(name):
            if name not in S:
                S[name] = sem(name)
            return S[name]

        class Chain:

            def __init__(self, eng, name):
                self.eng, self.sem, self.n, self.base = eng, s(name), 0, 0

            def __call__(self, ins):
                ins.then_inc(self.sem, 1)
                self.n += 1
                self.eng.wait_ge(self.sem, self.base + self.n)

            def loop(self, index, per):
                self.start, self.per = self.n, per
                self.base = index * per

            def again(self, offset):
                self.n = self.start + offset

            def end(self, count):
                self.base, self.n = 0, self.start + count

        for name in ("dve_own", "act_own", "pool_own"):
            s(name)

        def loads(sp):
            sp.dma_start(cst[:], const[:]).then_inc(s("in_const"), 16)
            for i in range(TILES):
                sp.dma_start(patches[:, i, :], xp[:, i, :]).then_inc(s(f"in_patch{i}"), 16)
            sp.dma_start(ln1_s[:], ln1[:]).then_inc(s("in_embed"), 16)
            sp.dma_start(wp_s[:], Wp[:]).then_inc(s("in_embed"), 16)
            for dst, src in ((bp_s, bp), (ln2g_s, ln2_g)):
                sp.dma_start(dst[:], src.rearrange("(a d) -> a d", a=1).to_broadcast([P, D])).then_inc(s("in_embed"), 16)
            sp.dma_start(cls_s[:], cls_ln2b[:]).then_inc(s("in_embed"), 16)
            sp.dma_start(wa0_s[:], wa0[:]).then_inc(s("in_attn0"), 16)
            sp.dma_start(ba0_s[:], ba0[:]).then_inc(s("in_attn0"), 16)
            sp.dma_start(wo0_s[:], wo0[:]).then_inc(s("in_attn0"), 16)
            sp.dma_start(bo0_s[:], bo0.rearrange("(a d) -> a d", a=1).to_broadcast([P, D])).then_inc(s("in_attn0"), 16)
            sp.dma_start(cent_s[:], cent[:]).then_inc(s("in_moe0"), 16)
            sp.dma_start(wa1_s[:], wa1[:]).then_inc(s("in_attn1"), 16)
            sp.dma_start(router_s[:], router[:]).then_inc(s("in_moe1"), 16)
            sp.dma_start(routerb_s[:], router_b.rearrange("(a d) -> a d", a=1).to_broadcast([P, EXPERTS])).then_inc(s("in_moe1"), 16)
            sp.wait_ge(s("zeros"), 1)
            for slots in (slots_in, slots_out):
                sp.dma_start(slots[:, :].rearrange("(w p) d -> p w d", p=P),
                             zero[:].rearrange("p (o d) -> p o d", o=1).to_broadcast([P, SLOTS // P, D])).then_inc(s("slots_zeroed"), 16)

        ZEROED = 32

        def norm_vector(dve, do, src, dst, tag, eps_done, mask=None, groups=1, width=D, tile_ready=None):
            for i in range(TILES):
                if tile_ready is not None:
                    tile_ready(i)
                for g in range(groups):
                    last = nc.vector.bn_stats(stats[:, i, g, :], src[:, i, g * (width // groups):(g + 1) * (width // groups)])
                    do(last)
            for i in range(TILES):
                do(nc.vector.bn_aggr(mv[:, i, :], stats[:, i, 0:groups, :]))
            nc.vector.tensor_scalar(veps[:], mv[:, :, 1], EPS, None, ALU.add).then_inc(s("veps_ready"), 1)
            dve.wait_ge(s("rstd_ready"), eps_done)
            if mask is not None:
                do(nc.vector.tensor_tensor(rstd[:], rstd[:], mask, ALU.mult))
            for i in range(TILES):
                last = nc.vector.tensor_scalar(dst[:, i, :], src[:, i, :], mv[:, i, 0:1], rstd[:, i:i + 1],
                                               ALU.subtract, ALU.mult)
                if i < TILES - 1:
                    do(last)
            last.then_inc(s(tag), 1)
            dve.wait_ge(s(tag), 1)

        POWERS = 8

        def embed_vector(dve, do):
            nc.vector.memset(zero[:], 0.0).then_inc(s("zeros"), 1)
            do(nc.vector.memset(oT[:], 0.0))
            do(nc.vector.memset(qT[:], 0.0))
            norm_vector(dve, do, patches, patches, "patches_normed", 1, groups=3, width=PD,
                        tile_ready=lambda i: dve.wait_ge(s(f"in_patch{i}"), 16))
            dve.wait_ge(s("in_embed"), 80)
            dve.wait_ge(s("in_const"), 16)
            for c in range(0, PC, 2):
                dve.wait_ge(s("patchT_ps"), c + 1)
                nc.vector.tensor_scalar(patchT[:, c, :], two_banks(c), ln1_s[:, 0, c:c + 1], ln1_s[:, 1, c:c + 1],
                                        ALU.mult, ALU.add).then_inc(s("patchT_even"), 1)
            for i in range(TILES):
                dve.wait_ge(s("y_ps"), min(TILES, (i | 1) + 1))
                do(nc.vector.tensor_tensor(x[:, i, :], tile_bank(4, i), bp_s[:], ALU.add))
            norm_vector(dve, do, x, x, "y_normed", 2, mask=table("is_patch"))
            for i in range(TILES):
                do(nc.vector.tensor_tensor(xd[:, i, :], x[:, i, :], ln2g_s[:], ALU.mult))
            dve.wait_ge(s("cls_ps"), 1)
            for i in range(TILES):
                do(nc.vector.tensor_tensor(h[:, i, :], xd[:, i, :], tile_bank(0, i), ALU.add))
            norm_vector(dve, do, h, x, "x_attn0", 3)

        def two_banks(c):
            b = 2 * (c % 2)
            return psum[:, b:b + 2, :].rearrange("p b n -> p (b n)")[:, 0:ROWS]

        def tile_bank(first, i):
            return psum[:, first + i // 2, (i % 2) * D:(i % 2) * D + D]

        def embed_scalar(act, do):
            act.wait_ge(s("in_const"), 16)
            nc.scalar.activation(identb[:], ident, ACT.Copy).then_inc(s("identb_ready"), 1)
            act.wait_ge(s("in_embed"), 80)
            for c in range(1, PC, 2):
                act.wait_ge(s("patchT_ps"), c + 1)
                nc.scalar.activation(patchT[:, c, :], two_banks(c), ACT.Identity, bias=ln1_s[:, 1, c:c + 1],
                                     scale=ln1_s[:, 0, c:c + 1]).then_inc(s("patchT_odd"), 1)

        def embed_tensor(pe):
            pe.wait_ge(s("in_const"), 16)
            pe.wait_ge(s("patches_normed"), 1)
            for c in range(PC):
                if c >= 2:
                    pe.wait_ge(s("patchT_odd" if c % 2 else "patchT_even"), c // 2)
                for i in range(TILES):
                    last = nc.tensor.transpose(two_banks(c)[:, i * P:(i + 1) * P], patches[:, i, c * P:(c + 1) * P], ident)
                last.then_inc(s("patchT_ps"), 1)
            pe.wait_ge(s("patchT_even"), PC // 2)
            pe.wait_ge(s("patchT_odd"), PC // 2)
            pe.wait_ge(s("in_embed"), 80)
            for i in range(TILES):
                for c in range(PC):
                    last = nc.tensor.matmul(tile_bank(4, i), patchT[:, c, i * P:(i + 1) * P], wp_s[:, c, :],
                                            start=(c == 0), stop=(c == PC - 1))
                last.then_inc(s("y_ps"), 1)
            for i in range(TILES):
                last = nc.tensor.matmul(tile_bank(0, i), table("patch_row", 2)[:, i * P:(i + 1) * P], cls_s[:],
                                        start=True, stop=True)
            last.then_inc(s("cls_ps"), 1)

        def turn_tensor(pe, src, ready, n, tag):
            pe.wait_ge(s(ready), n)
            for c in range(DC):
                for i in range(TILES):
                    last = nc.tensor.transpose(two_banks(c)[:, i * P:(i + 1) * P], src[:, i, c * P:(c + 1) * P], ident)
                last.then_inc(s(tag + "_ps"), 1)

        def turn_scalar(act, dst, tag):
            for c in range(DC):
                act.wait_ge(s(tag + "_ps"), c + 1)
                nc.scalar.activation(dst[:, c, :], two_banks(c), ACT.Copy).then_inc(s(tag), 1)

        def bank(b, parts=P):
            return psum[0:parts, b, :]

        def reused(engine, semaphore, count):
            if not (isinstance(count, int) and count <= 0):
                engine.wait_ge(semaphore, count)

        def attention(layer):
            done = layer * PAIRS
            src = xT if layer == 0 else xTb
            v_at = 2 if layer == 0 else 1
            v_col = 0

            def v_psum():
                return bank(2)[:, DC * PW:2 * DC * PW] if layer == 0 else bank(1)[:, 0:DC * PW]

            def o_psum():
                return bank(2)[:, 0:DC * PW]

            if layer == 0:
                weights, groups = wa0_s, [(0, 0, 0), (1, 0, 1), (2, 1, 0), (3, 1, 1), (4, 2, 1)]
            else:
                weights, groups = wq1_s, [(0, 0, 0), (1, 0, 1), (2, 1, 0)]

            def project_tensor(pe, p):
                if layer == 0:
                    reused(pe, s("qk_read"), done + p)
                reused(pe, s("vR_ready"), done + p)
                for g, b, col in groups:
                    if g == 4 and not is_first(p):
                        reused(pe, s("o_read"), done + p - 1)
                    for c in range(DC):
                        dst = bank(b)[:, (col * DC + c) * PW:(col * DC + c + 1) * PW]
                        for k in range(DC):
                            last = nc.tensor.matmul(dst, weights[:, k, g, c * P:(c + 1) * P], src[:, k, bass.ds(p * PW, PW)],
                                                    start=(k == 0), stop=(k == DC - 1))
                last.then_inc(s("proj"), 1)

            def is_first(p):
                return isinstance(p, int) and p == 0

            def values_tensor(pe, p):
                pe.wait_ge(s("vR_ready"), done + p + 1)
                reused(pe, s("vM_ready"), done + p)
                for j in range(2):
                    for c in range(DC):
                        last = nc.tensor.transpose(bank(3, PW)[:, j * D + c * P:j * D + (c + 1) * P],
                                                   vR[:, c, j, :, :].rearrange("p r k -> p (r k)"), ident)
                last.then_inc(s("v_ps"), 1)

            def scores_tensor(pe, p, buf):
                pe.wait_ge(s("in_const"), 16)
                pe.wait_ge(s("qT_ready"), done + p + 1)
                pe.wait_ge(s("kM_ready"), done + p + 1)
                reused(pe, s("sc_read"), done + p)
                for c in range(DC):
                    for j in range(2):
                        for r in range(2):
                            last = nc.tensor.matmul(bank(4 + r)[64 * j:64 * j + QPAD, c * 4 * SEQ:(c + 1) * 4 * SEQ],
                                                    qT[64 * r:64 * r + 64, buf, c, j, :],
                                                    kM[64 * r:64 * r + 64, buf, c, j, :, :].rearrange("p a k -> p (a k)"),
                                                    start=True, stop=True)
                last.then_inc(s("sc_ps"), 1)

            def turn_probs_tensor(pe, p):
                pe.wait_ge(s("prob"), done + p + 1)
                reused(pe, s("pT_ready"), done + p)
                for g in range(8):
                    last = nc.tensor.transpose(bank(6 + g // 4, PW)[:, (g % 4) * P:(g % 4 + 1) * P],
                                               prob[:, 2 * g:2 * g + 2, :].rearrange("p a k -> p (a k)"), ident)
                last.then_inc(s("pT_ps"), 1)

            def output_tensor(pe, p, buf):
                pe.wait_ge(s("pT_ready"), done + p + 1)
                pe.wait_ge(s("vM_ready"), done + p + 1)
                reused(pe, s("o_read"), done + p)
                for g in range(8):
                    r, c, hp = g // 4, (g // 2) % 2, g % 2
                    row = 64 * r + 32 * hp
                    for j in range(2):
                        last = nc.tensor.matmul(o_psum()[row:row + 32, c * PW + j * SEQ:c * PW + (j + 1) * SEQ],
                                                vM[:, buf, j, c * P + row:c * P + row + 32],
                                                pT[:, g, 64 * j:64 * j + SEQ], start=True, stop=True,
                                                tile_position=(0, row))
                last.then_inc(s("o_ps"), 1)

            def tensor(pe):
                def step(p, buf):
                    project_tensor(pe, p)
                    values_tensor(pe, p)
                    turn_probs_tensor(pe, p - 1)
                    scores_tensor(pe, p, buf)
                    output_tensor(pe, p - 1, 1 - buf)
                project_tensor(pe, 0)
                values_tensor(pe, 0)
                scores_tensor(pe, 0, 0)
                step(1, 1)
                with pe.Fori(1, PAIRS // 2) as u:
                    p = u * 2
                    step(p, 0)
                    step(p + 1, 1)
                turn_probs_tensor(pe, PAIRS - 1)
                output_tensor(pe, PAIRS - 1, 1)

            def qk_vector(dve, do, p, buf):
                dve.wait_ge(s("proj"), done + p + 1)
                qk = bank(0)[:, 0:2 * DC * PW]
                if layer == 0:
                    a = sc[:, 0, :]
                    b = sc[:, 1, :]
                    do(nc.vector.tensor_tensor(a.rearrange("p (n k) -> p n k", k=SEQ), qk.rearrange("p (n k) -> p n k", k=SEQ),
                                               rope_c[:], ALU.mult))
                    nc.vector.tensor_tensor(b.rearrange("p (n k) -> p n k", k=SEQ),
                                            bank(1)[:, 0:2 * DC * PW].rearrange("p (n k) -> p n k", k=SEQ),
                                            rope_s[:], ALU.mult).then_inc(s("qk_read"), 1)
                    dve.wait_ge(s("qk_read"), done + p + 1)
                    do(nc.vector.tensor_tensor(a, a, b, ALU.add))
                    bias = rope_bias[:].rearrange("p (g o) k -> p g o k", o=1).to_broadcast([P, 4, 2, SEQ])
                    av = a.rearrange("p (g j k) -> p g j k", j=2, k=SEQ)
                    nc.vector.tensor_tensor(qT[:, buf, :, :, 0:SEQ], av[:, 0:2], bias[:, 0:2], ALU.add).then_inc(s("qT_ready"), 1)
                    if not is_first(p):
                        reused(dve, s("kM_ready"), done + p)
                    nc.vector.tensor_tensor(kT[:].rearrange("p c (j k) -> p c j k", k=SEQ), av[:, 2:4], bias[:, 2:4],
                                            ALU.add).then_inc(s("kT_ready"), 1)
                else:
                    inv = invT[:, bass.ds(p * PW, PW)].rearrange("p (o n) -> p o n", o=1).to_broadcast([P, DC, PW])
                    qkv = qk.rearrange("p (g n) -> p g n", n=PW)
                    for c in range(DC):
                        last = nc.vector.tensor_tensor(qT[:, buf, c, :, 0:SEQ], qkv[:, c, :].rearrange("p (j k) -> p j k", k=SEQ),
                                                       invT[:, bass.ds(p * PW, PW)].rearrange("p (j k) -> p j k", k=SEQ), ALU.mult)
                        if c == 0:
                            do(last)
                    last.then_inc(s("qT_ready"), 1)
                    dve.wait_ge(s("qT_ready"), done + p + 1)
                    if not is_first(p):
                        reused(dve, s("kM_ready"), done + p)
                    nc.vector.tensor_tensor(kT[:], qkv[:, DC:2 * DC, :], inv, ALU.mult).then_inc(s("kT_ready"), 1)
                    dve.wait_ge(s("kT_ready"), done + p + 1)
                    reused(dve, s("v_ps"), done + p)
                    for c in range(DC):
                        for r in range(2):
                            last = nc.vector.tensor_tensor(vR[:, c, :, r, :],
                                                           v_psum()[:, c * PW:(c + 1) * PW].rearrange("p (j k) -> p j k", k=SEQ),
                                                           invT[:, bass.ds(p * PW, PW)].rearrange("p (j k) -> p j k", k=SEQ),
                                                           ALU.mult)
                            if (c, r) != (DC - 1, 1):
                                do(last)
                    last.then_inc(s("vR_ready"), 1)
                    dve.wait_ge(s("vR_ready"), done + p + 1)

            def mask_values_vector(dve, do, p, buf):
                dve.wait_ge(s("v_ps"), done + p + 1)
                if not is_first(p):
                    reused(dve, s("o_ps"), done + p - 1)
                nc.vector.tensor_tensor(vM[:, buf, :, :], bank(3, PW)[:, 0:2 * D].rearrange("p (j d) -> p j d", d=D),
                                        table("head2", PW).rearrange("p (o d) -> p o d", o=1).to_broadcast([PW, 2, D]),
                                        ALU.mult).then_inc(s("vM_ready"), 1)

            def softmax_vector(dve, do, p):
                scores = psum[:, 4:6, 0:8 * SEQ]
                flat = sc[:].rearrange("p r (n k) -> p (r n) k", k=SEQ)
                dve.wait_ge(s("sc_ps"), done + p + 1)
                if layer == 0:
                    nc.vector.scalar_tensor_tensor(out=sc[:], in0=scores, scalar=SCALE,
                                                   in1=table("causal").rearrange("p (o n) -> p o n", o=1).to_broadcast([P, 2, 8 * SEQ]),
                                                   op0=ALU.mult, op1=ALU.add).then_inc(s("sc_read"), 1)
                else:
                    nc.vector.tensor_copy(sc[:], scores).then_inc(s("sc_read"), 1)
                dve.wait_ge(s("sc_read"), done + p + 1)
                do(nc.vector.reduce_max(smax[:], flat, AX.X))
                nc.vector.tensor_tensor(flat, flat, smax[:].rearrange("p (n o) -> p n o", o=1).to_broadcast([P, HEADS, SEQ]),
                                        ALU.subtract).then_inc(s("sc_shift"), 1)
                dve.wait_ge(s("exp"), done + p + 1)
                do(nc.vector.reduce_sum(ssum[:], flat, AX.X))
                do(nc.vector.reciprocal(srec[:], ssum[:]))
                if not is_first(p):
                    reused(dve, s("pT_ps"), done + p)
                nc.vector.tensor_tensor(prob[:], flat, srec[:].rearrange("p (n o) -> p n o", o=1).to_broadcast([P, HEADS, SEQ]),
                                        ALU.mult).then_inc(s("prob"), 1)
                dve.wait_ge(s("prob"), done + p + 1)

            def vector(dve, do):
                def step(p, buf):
                    qk_vector(dve, do, p, buf)
                    mask_values_vector(dve, do, p, buf)
                    softmax_vector(dve, do, p)
                start = do.n
                step(0, 0)
                per = do.n - start
                step(1, 1)
                do.loop(0, per)
                with dve.Fori(1, PAIRS // 2) as u:
                    p = u * 2
                    do.base = (u - 1) * (2 * per)
                    step(p, 0)
                    step(p + 1, 1)
                do.end((PAIRS - 2) * per)

            def spread_keys_gpsimd(pool, p, buf):
                pool.wait_ge(s("kT_ready"), done + p + 1)
                if not is_first(p):
                    reused(pool, s("sc_ps"), done + p - 1)
                nc.gpsimd.tensor_tensor(kM[:, buf, :, :, :, :].rearrange("p c j a k -> p (c j) a k"),
                                        kT[:].rearrange("p c (j o k) -> p (c j) o k", o=1, k=SEQ).to_broadcast([P, 2 * DC, 4, SEQ]),
                                        table("head4").rearrange("p (o a u) -> p o a u", o=1, u=1).to_broadcast([P, 2 * DC, 4, SEQ]),
                                        ALU.mult).then_inc(s("kM_ready"), 1)

            def gpsimd(pool):
                spread_keys_gpsimd(pool, 0, 0)
                spread_keys_gpsimd(pool, 1, 1)
                with pool.Fori(1, PAIRS // 2) as u:
                    p = u * 2
                    spread_keys_gpsimd(pool, p, 0)
                    spread_keys_gpsimd(pool, p + 1, 1)

            def scalar(act, do):
                def copy_values(p):
                    act.wait_ge(s("proj"), done + p + 1)
                    reused(act, s("v_ps"), done + p)
                    for c in range(DC):
                        for r in range(2):
                            last = nc.scalar.activation(vR[:, c, :, r, :],
                                                        v_psum()[:, c * PW:(c + 1) * PW].rearrange("p (j k) -> p j k", k=SEQ),
                                                        ACT.Identity, bias=ba0_s[:, 4, c:c + 1])
                            if (c, r) != (DC - 1, 1):
                                do(last)
                    last.then_inc(s("vR_ready"), 1)

                def exponent(p):
                    act.wait_ge(s("sc_shift"), done + p + 1)
                    nc.scalar.activation(sc[:], sc[:], ACT.Exp, scale=1.0 if layer == 0 else qk_scale[:, 0:1]).then_inc(s("exp"), 1)

                def copy_probs(p):
                    act.wait_ge(s("pT_ps"), done + p + 1)
                    if not is_first(p):
                        reused(act, s("o_ps"), done + p)
                    nc.scalar.activation(pT[:], psum[0:PW, 6:8, :].rearrange("p b (g n) -> p (b g) n", n=P),
                                         ACT.Copy).then_inc(s("pT_ready"), 1)

                def copy_output(p):
                    act.wait_ge(s("o_ps"), done + p + 1)
                    nc.scalar.activation(oT[:, :, bass.ds(p * PW, PW)], o_psum().rearrange("p (c n) -> p c n", n=PW), ACT.Copy,
                                         scale=1.0 if layer == 0 else wmean[:, 2:3]).then_inc(s("o_read"), 1)

                def step(p):
                    if layer == 0:
                        copy_values(p)
                    copy_probs(p - 1)
                    exponent(p)
                    copy_output(p - 1)

                start = do.n
                if layer == 0:
                    copy_values(0)
                per = do.n - start
                exponent(0)
                step(1)
                do.loop(0, per)
                with act.Fori(1, PAIRS // 2) as u:
                    p = u * 2
                    do.base = (u - 1) * (2 * per)
                    step(p)
                    step(p + 1)
                do.end((PAIRS - 2) * per)
                copy_probs(PAIRS - 1)
                copy_output(PAIRS - 1)

            return tensor, vector, gpsimd, scalar

        attn0 = attention(0)
        attn1 = attention(1)

        def rope_tables_vector(dve, do):
            dve.wait_ge(s("in_attn0"), 64)
            one = lambda a: a.rearrange("p (o k) -> p o k", o=1).to_broadcast([P, 8, SEQ])
            do(nc.vector.tensor_copy(rope_c[:], one(table("cos"))))
            do(nc.vector.tensor_copy(rope_s[:], one(table("sin"))))
            for g in range(2):
                for c in range(DC):
                    dst = rope_bias[:, g * DC + c, :]
                    do(nc.vector.tensor_scalar(dst, table("cos"), ba0_s[:, g, c:c + 1], None, ALU.mult))
                    do(nc.vector.scalar_tensor_tensor(out=dst, in0=table("sin"), scalar=ba0_s[:, 2 + g, c:c + 1], in1=dst,
                                                      op0=ALU.mult, op1=ALU.add))

        def moe(layer):
            L = f"_m{layer}"
            F1 = FF * (1 + layer)
            w1, w2 = (w1_0, w2_0) if layer == 0 else (w1_1, w2_1)
            logit_w = cent_s if layer == 0 else router_s
            HC = F1 // P

            def load_count(engine):
                return engine.value_load(winexp_i[0:1, WINDOWS:WINDOWS + 1], min_val=MIN_WINDOWS, max_val=WINDOWS)

            def load_pairs(engine):
                return engine.value_load(winexp_i[0:1, WINDOWS + 1:WINDOWS + 2], min_val=-(-MIN_WINDOWS // 2), max_val=WINDOWS // 2)

            def load_seconds(engine):
                return engine.value_load(winexp_i[0:1, WINDOWS + 2:WINDOWS + 3], min_val=MIN_WINDOWS // 2, max_val=WINDOWS // 2)

            def windows(engine, body):
                engine.wait_ge(s("table" + L), 1)
                count = load_count(engine)
                pairs = load_pairs(engine)
                body(0, 0)
                body(0, 1)
                with engine.Fori(1, pairs) as u:
                    body(u, 0)
                    with engine.If(u * 2 + 1 < count):
                        body(u, 1)
                return count

            def logits_tensor(pe):
                pe.wait_ge(s("turned" + L), DC)
                pe.wait_ge(s("in_moe0" if layer == 0 else "in_moe1"), 16 if layer == 0 else 32)
                for i in range(TILES):
                    for c in range(DC):
                        last = nc.tensor.matmul(bank(4)[:, i * EXPERTS:(i + 1) * EXPERTS], xT[:, c, i * P:(i + 1) * P],
                                                logit_w[:, c, :], start=(c == 0), stop=(c == DC - 1))
                last.then_inc(s("logits" + L), 1)
                pe.wait_ge(s("hot" + L), 1)
                nc.tensor.matmul(bank(5)[:, 0:TILES * EXPERTS], table("earlier"), hot[:].rearrange("p t e -> p (t e)"), start=True, stop=True)
                nc.tensor.matmul(bank(6)[:, 0:TILES * EXPERTS], table("ones"), hot[:].rearrange("p t e -> p (t e)"),
                                 start=True, stop=True).then_inc(s("ranks" + L), 1)

            def route_vector(dve, do):
                T8 = [P, TILES, EXPERTS]
                per_expert = lambda a: a.rearrange("p (o e) -> p o e", o=1).to_broadcast(T8)
                per_row = lambda a: a.rearrange("p (t o) -> p t o", o=1).to_broadcast(T8)
                dve.wait_ge(s("logits" + L), 1)
                logits = bank(4)[:, 0:TILES * EXPERTS].rearrange("p (t e) -> p t e", e=EXPERTS)
                if layer == 0:
                    do(nc.vector.tensor_copy(lg[:], logits))
                else:
                    do(nc.vector.tensor_tensor(lg[:], logits, per_expert(routerb_s[:]), ALU.add))
                do(nc.vector.reduce_max(lmax[:], lg[:], AX.X))
                if layer == 0:
                    do(nc.vector.tensor_copy(lexp[:, :, 0], lmax[:]))
                    s_ready = nc.vector.tensor_copy(gate[:], lmax[:])
                    s_ready.then_inc(s("gate_in" + L), 1)
                    dve.wait_ge(s("gate_exp" + L), 1)
                    do(nc.vector.tensor_scalar(gate[:], gate[:], 1.0, None, ALU.add))
                    do(nc.vector.reciprocal(gate[:], gate[:]))
                    ranked, top = lg, lmax
                else:
                    nc.vector.tensor_tensor(lexp[:], lg[:], per_row(lmax[:]), ALU.subtract).then_inc(s("gate_in" + L), 1)
                    dve.wait_ge(s("gate_exp" + L), 1)
                    do(nc.vector.reduce_sum(gate[:], lexp[:], AX.X))
                    do(nc.vector.reciprocal(gate[:], gate[:]))
                    do(nc.vector.reduce_max(lmax[:], lexp[:], AX.X))
                    ranked, top = lexp, lmax
                do(nc.vector.tensor_tensor(r1[:], ranked[:], per_row(top[:]), ALU.is_equal))
                do(nc.vector.tensor_tensor(r1[:], r1[:], per_expert(table("first")), ALU.mult))
                do(nc.vector.reduce_max(rsmall[:], r1[:], AX.X))
                do(nc.vector.tensor_tensor(hot[:], r1[:], per_row(rsmall[:]), ALU.is_equal))
                nc.vector.tensor_tensor(hot[:], hot[:], per_row(table("valid")), ALU.mult).then_inc(s("hot" + L), 1)
                dve.wait_ge(s("ranks" + L), 1)
                do(nc.vector.tensor_copy(total[:], bank(6)[:, 0:TILES * EXPERTS].rearrange("p (t e) -> p t e", e=EXPERTS)))
                do(nc.vector.memset(before[:, 0, :], 0.0))
                for i in range(TILES):
                    do(nc.vector.tensor_tensor(before[:, i + 1, :], before[:, i, :], total[:, i, :], ALU.add))
                do(nc.vector.tensor_tensor(rank[:], bank(5)[:, 0:TILES * EXPERTS].rearrange("p (t e) -> p t e", e=EXPERTS),
                                           before[:, 0:TILES, :], ALU.add))
                c5 = cmp[:, 0:EXPERTS * TILES].rearrange("p (e t) -> p e t", t=TILES)
                do(nc.vector.tensor_tensor(c5, before[:, TILES, :].rearrange("p (e o) -> p e o", o=1).to_broadcast([P, EXPERTS, TILES]),
                                           table("full").rearrange("p (o t) -> p o t", o=1).to_broadcast([P, EXPERTS, TILES]), ALU.is_gt))
                do(nc.vector.reduce_sum(nwin[:], c5, AX.X))
                c8 = cmp[:, 0:EXPERTS * EXPERTS].rearrange("p (e f) -> p e f", f=EXPERTS)
                do(nc.vector.tensor_tensor(c8, table("upto").rearrange("p (e f) -> p e f", f=EXPERTS),
                                           nwin[:].rearrange("p (o f) -> p o f", o=1).to_broadcast([P, EXPERTS, EXPERTS]), ALU.mult))
                do(nc.vector.reduce_sum(wend[:], c8, AX.X))
                do(nc.vector.tensor_tensor(wbeg[:], wend[:], nwin[:], ALU.subtract))
                cw = cmp[:].rearrange("p (w e) -> p w e", e=EXPERTS)
                do(nc.vector.tensor_tensor(cw, wend[:].rearrange("p (o e) -> p o e", o=1).to_broadcast([P, WINDOWS, EXPERTS]),
                                           table("window").rearrange("p (w o) -> p w o", o=1).to_broadcast([P, WINDOWS, EXPERTS]), ALU.is_le))
                do(nc.vector.reduce_sum(winexp[:, 0:WINDOWS], cw, AX.X))
                do(nc.vector.tensor_scalar(winexp[:, 0:WINDOWS], winexp[:, 0:WINDOWS], float(EXPERTS - 1), None, ALU.min))
                do(nc.vector.tensor_copy(winexp[:, WINDOWS:WINDOWS + 1], wend[:, EXPERTS - 1:EXPERTS]))
                do(nc.vector.tensor_scalar(cmp[:, 0:1], wend[:, EXPERTS - 1:EXPERTS], 0.5, 0.25, ALU.mult, ALU.add))
                do(nc.vector.tensor_scalar(winexp[:, WINDOWS + 1:WINDOWS + 2], cmp[:, 0:1], HALF_EVEN, HALF_EVEN, ALU.add, ALU.subtract))
                do(nc.vector.tensor_tensor(winexp[:, WINDOWS + 2:WINDOWS + 3], winexp[:, WINDOWS:WINDOWS + 1],
                                           winexp[:, WINDOWS + 1:WINDOWS + 2], ALU.subtract))
                nc.vector.tensor_copy(winexp_i[:], winexp[:]).then_inc(s("table" + L), 1)
                do(nc.vector.scalar_tensor_tensor(out=rank[:], in0=per_expert(wbeg[:]), scalar=float(WIN), in1=rank[:],
                                                  op0=ALU.mult, op1=ALU.add))
                do(nc.vector.tensor_tensor(rank[:], rank[:], hot[:], ALU.mult))
                do(nc.vector.reduce_sum(slot_f[:], rank[:], AX.X))
                do(nc.vector.tensor_tensor(slot_f[:], slot_f[:], table("pad_slot"), ALU.add))
                nc.vector.tensor_copy(slot_i[:], slot_f[:]).then_inc(s("slots" + L), 1)

            def route_scalar(act):
                act.wait_ge(s("gate_in" + L), 1)
                if layer == 0:
                    nc.scalar.activation(gate[:], gate[:], ACT.Exp, scale=-1.0).then_inc(s("gate_exp" + L), 1)
                else:
                    nc.scalar.activation(lexp[:], lexp[:], ACT.Exp).then_inc(s("gate_exp" + L), 1)

            def dispatch_gpsimd(pool):
                rows = xd if layer == 0 else x
                pool.wait_ge(s("slots_zeroed"), ZEROED)
                pool.wait_ge(s("slots" + L), 1)
                if layer == 0:
                    pool.wait_ge(s("inner_normed"), 1)
                for i in range(TILES):
                    pool.indirect_dma_start(out=slots_in[:, :], out_offset=bass.IndirectOffsetOnAxis(ap=slot_i[:, i:i + 1], axis=0),
                                            in_=rows[:, i, :], in_offset=None).then_inc(s("dispatched" + L), 16)

                def store(u, b):
                    pool.wait_ge(s(f"z_ready{b}" + L), u + 1)
                    pool.dma_start(slots_out[bass.ds((u * 2 + b) * WIN, WIN), :], zw[:, b, :]).then_inc(s(f"z_stored{b}" + L), 16)
                windows(pool, store)
                pairs, seconds = load_pairs(pool), load_seconds(pool)
                pool.wait_ge(s("z_stored0" + L), pairs * 16)
                pool.wait_ge(s("z_stored1" + L), seconds * 16)
                nc.gpsimd.tensor_tensor(stored[:], table("ones")[0:1, 0:1], table("ones")[0:1, 0:1], ALU.mult).then_inc(s("all_stored"), 1)
                pool.wait_ge(s("all_stored"), layer + 1)
                for i in range(TILES):
                    pool.indirect_dma_start(out=z[:, i, :], out_offset=None, in_=slots_out[:, :],
                                            in_offset=bass.IndirectOffsetOnAxis(ap=slot_i[:, i:i + 1], axis=0)).then_inc(s(f"z_back{i}"), 16)

            def weights_sync(sp):
                def load(u, b):
                    e = sp.value_load(winexp_i[0:1, bass.ds(u * 2 + b, 1)], min_val=0, max_val=EXPERTS - 1)
                    reused(sp, s(f"w2_used{b}" + L), u)
                    sp.dma_start(w1_s[:, b, 0:DC * F1], w1[bass.ds(e, 1), :, :].rearrange("e p n -> (e p) n")).then_inc(s(f"w1_in{b}" + L), 16)
                    if layer == 0:
                        sp.dma_start(par_s[:, b, :], par_0[bass.ds(e, 1), :, :].rearrange("e p n -> (e p) n")).then_inc(s(f"w1_in{b}" + L), 16)
                    sp.dma_start(w2_s[:, b, :, :].rearrange("p f n -> p (f n)"), w2[bass.ds(e, 1), :, :].rearrange("e p n -> (e p) n")).then_inc(s(f"w2_in{b}" + L), 16)
                    if layer == 0:
                        reused(sp, s(f"z_ready{b}" + L), u)
                        sp.dma_start(b2_s[:, b, :], b2_0[bass.ds(e, 1), :].to_broadcast([P, D])).then_inc(s(f"b2_in{b}" + L), 16)
                    sp.wait_ge(s("dispatched" + L), 16 * TILES)
                    reused(sp, s(f"xw_used{b}" + L), u)
                    sp.dma_start(xw[:, b, :], slots_in[bass.ds((u * 2 + b) * WIN, WIN), :]).then_inc(s(f"xw_in{b}" + L), 16)
                windows(sp, load)

            def expert_tensor(pe):
                def window(u, b):
                    w = u * 2 + b
                    pe.wait_ge(s(f"xw_in{b}" + L), u * 16 + 16)
                    reused(pe, s("xwT_ready" + L), w)
                    for c in range(DC):
                        last = nc.tensor.transpose(bank(0)[:, c * P:(c + 1) * P], xw[:, b, c * P:(c + 1) * P], ident)
                    last.then_inc(s(f"xw_used{b}" + L), 1)
                    n1 = 32 if layer == 0 else 16
                    pe.wait_ge(s(f"w1_in{b}" + L), u * n1 + n1)
                    pe.wait_ge(s("xwT_ready" + L), w + 1)
                    w1v = w1_s[:, b, 0:DC * F1].rearrange("p (k f) -> p k f", f=F1)
                    for f in range(FC):
                        reused(pe, s("hid_ready" + L), w * FC + max(f - 3, 0))
                        for part in range(1 + layer):
                            for k in range(DC):
                                last = nc.tensor.matmul(bank(1 + f % 4)[:, part * WIN:(part + 1) * WIN],
                                                        w1v[:, k, part * FF + f * P:part * FF + (f + 1) * P], xwT[:, k, :],
                                                        start=(k == 0), stop=(k == DC - 1))
                        last.then_inc(s("hid_ps" + L), 1)
                    pe.wait_ge(s(f"w2_in{b}" + L), u * 16 + 16)
                    reused(pe, s(f"z_ready{b}" + L), u)
                    for f in range(FC):
                        pe.wait_ge(s("hid_ready" + L), w * FC + f + 1)
                        last = nc.tensor.matmul(bank(5 + b)[:, 0:D], hid[:, f, :], w2_s[:, b, f, :], start=(f == 0), stop=(f == FC - 1))
                    last.then_inc(s(f"w2_used{b}" + L), 1)
                windows(pe, window)

            def expert_vector(dve, do):
                def window(u, b):
                    w = u * 2 + b
                    dve.wait_ge(s(f"xw_used{b}" + L), u + 1)
                    turned = bank(0)[:, 0:DC * P].rearrange("p (c n) -> p c n", n=P)
                    if layer == 0:
                        dve.wait_ge(s(f"w1_in{b}" + L), u * 32 + 32)
                        nc.vector.tensor_scalar(xwT[:, 0, :], turned[:, 0, :], par_s[:, b, 0:1], par_s[:, b, DC:DC + 1], ALU.mult, ALU.add)
                        nc.vector.tensor_scalar(xwT[:, 1, :], turned[:, 1, :], par_s[:, b, 1:2], par_s[:, b, DC + 1:DC + 2], ALU.mult,
                                                ALU.add).then_inc(s("xwT_ready" + L), 1)
                    else:
                        nc.vector.tensor_copy(xwT[:], turned).then_inc(s("xwT_ready" + L), 1)
                        for f in range(FC):
                            dve.wait_ge(s("act_ready" + L), w * FC + f + 1)
                            nc.vector.tensor_tensor(hid[:, f, :], bank(1 + f % 4)[:, WIN:2 * WIN], act_a[:, f % 2, :],
                                                    ALU.mult).then_inc(s("hid_ready" + L), 1)
                    dve.wait_ge(s(f"w2_used{b}" + L), u + 1)
                    reused(dve, s(f"z_stored{b}" + L), u * 16)
                    if layer == 0:
                        dve.wait_ge(s(f"b2_in{b}" + L), u * 16 + 16)
                        nc.vector.tensor_tensor(zw[:, b, :], bank(5 + b)[:, 0:D], b2_s[:, b, :], ALU.add).then_inc(s(f"z_ready{b}" + L), 1)
                    else:
                        nc.vector.tensor_copy(zw[:, b, :], bank(5 + b)[:, 0:D]).then_inc(s(f"z_ready{b}" + L), 1)
                windows(dve, window)

            def expert_scalar(act):
                def window(u, b):
                    w = u * 2 + b
                    for f in range(FC):
                        act.wait_ge(s("hid_ps" + L), w * FC + f + 1)
                        src = bank(1 + f % 4)[:, 0:WIN]
                        if layer == 0:
                            if f == 0:
                                reused(act, s(f"w2_used{1 - b}" + L), u + b)
                            last = nc.scalar.activation(hid[:, f, :], src, ACT.Relu, bias=par_s[:, b, 2 * DC + f:2 * DC + f + 1])
                            last.then_inc(s("hid_ready" + L), 1)
                        else:
                            reused(act, s("hid_ready" + L), w * FC + max(f - 1, 0))
                            nc.scalar.activation(act_a[:, f % 2, :], src, ACT.Silu).then_inc(s("act_ready" + L), 1)
                windows(act, window)

            return logits_tensor, route_vector, route_scalar, dispatch_gpsimd, weights_sync, expert_tensor, expert_vector, expert_scalar

        moe0 = moe(0)
        moe1 = moe(1)

        def quant_weights_scalar(act):
            act.wait_ge(s("in_attn1"), 16)
            for g in range(4):
                last = nc.scalar.activation(z[:, g, :].rearrange("p (k n) -> p k n", k=DC)[:, :, 0:P], wa1_s[:, :, g, 0:P], ACT.Abs,
                                            accum_out=stat2[:, g, 0:1])
            return last

        def quant_weights_vector(dve, do):
            dve.wait_ge(s("in_attn1"), 16)
            ab = wscaleabs().rearrange("p (k g n) -> p k g n", k=DC, g=4)
            for g in range(4):
                do(nc.vector.tensor_reduce(wsum[:, g:g + 1], wa1_s[:, :, g, :], AX.XY, ALU.add, apply_absolute_value=True))
            nc.vector.tensor_copy(wscale[:], wsum[:]).then_inc(s("wsum_ready"), 1)
            dve.wait_ge(s("wsum_ps"), 1)
            do(nc.vector.tensor_scalar(wmean[:], bank(7)[:, 0:4], 1.0 / (D * D), 1e-5, ALU.mult, ALU.max))
            do(nc.vector.reciprocal(wscale[:], wmean[:]))
            do(nc.vector.tensor_tensor(qk_scale[:], wmean[:, 0:1], wmean[:, 1:2], ALU.mult))
            do(nc.vector.tensor_scalar(qk_scale[:], qk_scale[:], SCALE, None, ALU.mult))
            for g in range(4):
                dst = ab[:, :, g, :]
                do(nc.vector.tensor_scalar(dst, wa1_s[:, :, g, :], wscale[:, g:g + 1], HALF_EVEN, ALU.mult, ALU.add))
                do(nc.vector.tensor_scalar(dst, dst, HALF_EVEN, 1.0, ALU.subtract, ALU.min))
                last = nc.vector.tensor_scalar(wq1_s[:, :, g, :], dst, -1.0, None, ALU.max)
                if g < 3:
                    do(last)
            last.then_inc(s("wq1_ready"), 1)

        def wscaleabs():
            return patchT[:].rearrange("p c n -> p (c n)")[:, 0:DC * 4 * D]

        def quant_weights_tensor(pe):
            pe.wait_ge(s("wsum_ready"), 1)
            nc.tensor.matmul(bank(7)[:, 0:4], table("ones"), wscale[:], start=True, stop=True).then_inc(s("wsum_ps"), 1)

        def quant_vector(dve, do, src, tag, power):
            for i in range(TILES):
                do(nc.vector.bn_stats(stats[:, i, 0, :], src[:, i, :]))
            for i in range(TILES):
                do(nc.vector.bn_aggr(mv[:, i, :], stats[:, i, 0:1, :]))
            do(nc.vector.tensor_copy(stat2[:, :, 0:2], mv[:]))
            nc.vector.tensor_tensor(stat2[:, :, 2], mv[:, :, 0], mv[:, :, 0], ALU.mult).then_inc(s("stat" + tag), 1)
            dve.wait_ge(s("img_ps" + tag), 1)
            do(nc.vector.tensor_scalar(img[:, 0:3], bank(6)[0:IMAGES, 0:3], 1.0 / SEQ, None, ALU.mult))
            do(nc.vector.tensor_tensor(img[:, 3:4], img[:, 0:1], img[:, 0:1], ALU.mult))
            do(nc.vector.tensor_tensor(img[:, 4:5], img[:, 1:2], img[:, 2:3], ALU.add))
            do(nc.vector.tensor_tensor(img[:, 4:5], img[:, 4:5], img[:, 3:4], ALU.subtract))
            do(nc.vector.tensor_scalar(img[:, 4:5], img[:, 4:5], 0.0, None, ALU.max))
            nc.vector.tensor_copy(img[:, 1:2], img[:, 4:5]).then_inc(s("img" + tag), 1)
            dve.wait_ge(s("tok_ps" + tag), 1)
            do(nc.vector.tensor_copy(tokstat[:], bank(7)[:, 0:2 * TILES].rearrange("p (t a) -> p t a", a=2)))
            nc.vector.tensor_scalar(veps[:], tokstat[:, :, 1], EPS, None, ALU.add).then_inc(s("veps_ready"), 1)
            dve.wait_ge(s("rstd_ready"), power)
            for i in range(TILES):
                do(nc.vector.tensor_scalar(z[:, i, :], src[:, i, :], tokstat[:, i, 0:1], rstd[:, i:i + 1], ALU.subtract, ALU.mult))
            do(nc.vector.tensor_reduce(amax[:], z[:], AX.X, ALU.max, apply_absolute_value=True))
            do(nc.vector.tensor_scalar(amax[:], amax[:], 1e-5, None, ALU.max))
            do(nc.vector.tensor_scalar(inv_s[:], amax[:], 1.0 / 127.0, None, ALU.mult))
            do(nc.vector.reciprocal(act_s[:], amax[:]))
            do(nc.vector.tensor_scalar(act_s[:], act_s[:], 127.0, None, ALU.mult))
            for i in range(TILES):
                do(nc.vector.tensor_scalar(z[:, i, :], z[:, i, :], act_s[:, i:i + 1], HALF_EVEN, ALU.mult, ALU.add))
                do(nc.vector.tensor_scalar(z[:, i, :], z[:, i, :], HALF_EVEN, 127.0, ALU.subtract, ALU.min))
                last = nc.vector.tensor_scalar(xqb[:, i, :], z[:, i, :], -128.0, None, ALU.max)
                if i < TILES - 1:
                    do(last)
            last.then_inc(s("xq" + tag), 1)

        def quant_tensor(pe, tag):
            pe.wait_ge(s("stat" + tag), 1)
            for i in range(TILES):
                last = nc.tensor.matmul(bank(6)[0:IMAGES, 0:3], table("of_image")[:, i * IMAGES:(i + 1) * IMAGES], stat2[:, i, :],
                                        start=(i == 0), stop=(i == TILES - 1))
            last.then_inc(s("img_ps" + tag), 1)
            pe.wait_ge(s("img" + tag), 1)
            for i in range(TILES):
                last = nc.tensor.matmul(bank(7)[:, 2 * i:2 * i + 2], table("image_of", IMAGES)[:, i * P:(i + 1) * P], img[:, 0:2],
                                        start=True, stop=True)
            last.then_inc(s("tok_ps" + tag), 1)
            pe.wait_ge(s("xq" + tag), 1)
            pe.wait_ge(s("identb_ready"), 1)
            for c in range(DC):
                for i in range(TILES):
                    last = nc.tensor.transpose(turned_bf16(c)[:, i * P:(i + 1) * P], xqb[:, i, c * P:(c + 1) * P], identb[:])
                last.then_inc(s("xqT_ps" + tag), 1)

        def turned_bf16(c):
            return psum[:, 4 + c, :].bitcast(BF16)[:, 0:ROWS]

        def quant_scalar(act, tag):
            for c in range(DC):
                act.wait_ge(s("xqT_ps" + tag), c + 1)
                nc.scalar.activation(xTb[:, c, :], turned_bf16(c), ACT.Copy).then_inc(s("xqT" + tag), 1)

        block = ctx.enter_context(nc.Block())

        @block.sync
        def _(sp):
            loads(sp)
            moe0[4](sp)
            moe1[4](sp)
            for i in range(TILES):
                n = min(P, TOKENS - i * P)
                sp.wait_ge(s("out_ready"), i + 1)
                sp.dma_start(out[i * P:i * P + n, :], h[0:n, i, :]).then_inc(s("out_stored"), 16)
            sp.wait_ge(s("out_stored"), 16 * TILES)

        @block.gpsimd
        def _(pool):
            powers = [0]

            def power():
                pool.wait_ge(s("veps_ready"), powers[0] + 1)
                nc.gpsimd.tensor_tensor(rstd[:], veps[:], table("minus_half"), ALU.pow).then_inc(s("rstd_ready"), 1)
                powers[0] += 1

            pool.wait_ge(s("in_const"), 16)
            power()
            power()
            power()
            attn0[2](pool)
            power()
            power()
            moe0[3](pool)
            power()
            power()
            attn1[2](pool)
            power()
            power()
            moe1[3](pool)

        @block.scalar
        def _(act):
            do = Chain(act, "act_own")
            embed_scalar(act, do)
            turn_scalar(act, xT, "turn_a0")
            attn0[3](act, do)
            turn_scalar(act, xT, "turned_m0")
            moe0[2](act)
            moe0[7](act)
            quant_scalar(act, "_x1")
            attn1[3](act, do)
            quant_scalar(act, "_o1")
            turn_scalar(act, xT, "turned_m1")
            moe1[2](act)
            moe1[7](act)

        @block.tensor
        def _(pe):
            embed_tensor(pe)
            pe.wait_ge(s("y_normed"), 1)
            turn_tensor(pe, x, "x_attn0", 1, "turn_a0")
            pe.wait_ge(s("turn_a0"), DC)
            pe.wait_ge(s("in_attn0"), 64)
            quant_weights_tensor(pe)
            pe.wait_ge(s("wq1_ready"), 1)
            attn0[0](pe)
            pe.wait_ge(s("o_read"), PAIRS)
            for i in range(TILES):
                for c in range(DC):
                    last = nc.tensor.matmul(tile_bank(0, i), oT[:, c, i * P:(i + 1) * P], wo0_s[:, c, :], start=(c == 0), stop=(c == DC - 1))
                last.then_inc(s("y_attn0"), 1)
            turn_tensor(pe, x, "x_moe0", 1, "turned_m0")
            moe0[0](pe)
            moe0[5](pe)
            quant_tensor(pe, "_x1")
            pe.wait_ge(s("spread"), 1)
            for i in range(TILES):
                last = nc.tensor.transpose(two_banks(0)[:, i * P:(i + 1) * P], spread[:, i, :], ident)
            last.then_inc(s("invT_ps"), 1)
            pe.wait_ge(s("invT_ready"), 1)
            pe.wait_ge(s("xqT_x1"), DC)
            attn1[0](pe)
            pe.wait_ge(s("o_read"), 2 * PAIRS)
            for c in range(DC):
                for i in range(TILES):
                    last = nc.tensor.transpose(psum[:, (i // 2), (i % 2) * D + c * P:(i % 2) * D + (c + 1) * P], oT[:, c, i * P:(i + 1) * P], ident)
            last.then_inc(s("o_rows_ps"), 1)
            quant_tensor(pe, "_o1")
            pe.wait_ge(s("xqT_o1"), DC)
            for i in range(TILES):
                for c in range(DC):
                    last = nc.tensor.matmul(tile_bank(0, i), xTb[:, c, i * P:(i + 1) * P], wq1_s[:, c, 3, :], start=(c == 0), stop=(c == DC - 1))
                last.then_inc(s("y_attn1"), 1)
            turn_tensor(pe, x, "x_moe1", 1, "turned_m1")
            moe1[0](pe)
            moe1[5](pe)

        @block.vector
        def _(dve):
            do = Chain(dve, "dve_own")
            embed_vector(dve, do)
            rope_tables_vector(dve, do)
            quant_weights_vector(dve, do)
            attn0[1](dve, do)
            for i in range(TILES):
                do(nc.vector.tensor_tensor(h[:, i, :], h[:, i, :], bo0_s[:], ALU.add))
            for i in range(TILES):
                dve.wait_ge(s("y_attn0"), i + 1)
            for i in range(TILES):
                do(nc.vector.tensor_tensor(h[:, i, :], tile_bank(0, i), h[:, i, :], ALU.add))
            norm_vector(dve, do, h, x, "x_moe0", 4)
            norm_vector(dve, do, x, xd, "inner_normed", 5)
            moe0[1](dve, do)
            moe0[6](dve, do)
            for i in range(TILES):
                do(nc.vector.tensor_tensor(h[:, i, :], h[:, i, :], x[:, i, :], ALU.add))
            for i in range(TILES):
                dve.wait_ge(s(f"z_back{i}"), 16)
                do(nc.vector.scalar_tensor_tensor(out=h[:, i, :], in0=z[:, i, :], scalar=gate[:, i:i + 1], in1=h[:, i, :],
                                                  op0=ALU.mult, op1=ALU.add))
            norm_vector(dve, do, h, x, "x_attn1", 6)
            quant_vector(dve, do, x, "_x1", 7)
            do(nc.vector.tensor_copy(veps[:], inv_s[:]))
            nc.vector.tensor_copy(spread[:], inv_s[:].rearrange("p (t o) -> p t o", o=1).to_broadcast([P, TILES, P])).then_inc(s("spread"), 1)
            dve.wait_ge(s("invT_ps"), 1)
            nc.vector.tensor_copy(invT[:], two_banks(0)).then_inc(s("invT_ready"), 1)
            dve.wait_ge(s("invT_ready"), 1)
            attn1[1](dve, do)
            dve.wait_ge(s("o_rows_ps"), 1)
            for i in range(TILES):
                do(nc.vector.tensor_copy(xd[:, i, :], tile_bank(0, i)))
            quant_vector(dve, do, xd, "_o1", 8)
            do(nc.vector.tensor_scalar(rsmall[:], inv_s[:], wmean[:, 3:4], None, ALU.mult))
            for i in range(TILES):
                dve.wait_ge(s("y_attn1"), i + 1)
            for i in range(TILES):
                do(nc.vector.scalar_tensor_tensor(out=h[:, i, :], in0=tile_bank(0, i), scalar=rsmall[:, i:i + 1], in1=h[:, i, :],
                                                  op0=ALU.mult, op1=ALU.add))
            norm_vector(dve, do, h, x, "x_moe1", 9)
            moe1[1](dve, do)
            moe1[6](dve, do)
            for i in range(TILES):
                dve.wait_ge(s(f"z_back{i}"), 32)
                nc.vector.scalar_tensor_tensor(out=h[:, i, :], in0=z[:, i, :], scalar=gate[:, i:i + 1], in1=h[:, i, :],
                                               op0=ALU.mult, op1=ALU.add).then_inc(s("out_ready"), 1)


def kernel(**inputs):
    import concourse.bacc as bacc
    from concourse.bass_utils import run_bass_kernel_spmd

    a = {k: np.asarray(v) for k, v in inputs.items()}

    def rows(w):
        return w.reshape(w.shape[0] // P, P, *w.shape[1:]).swapaxes(0, 1)

    def col(v):
        return v.reshape(-1, P).T

    patches = a["x"].reshape(IMAGES, CHANNELS, GRID, PATCH, GRID, PATCH).transpose(0, 2, 4, 3, 5, 1).reshape(IMAGES, SEQ - 1, PD)
    xp = np.zeros((ROWS, PD), np.float32)
    xp[:TOKENS].reshape(IMAGES, SEQ, PD)[:, 1:] = patches
    partner = np.arange(D) ^ 1
    wq, wk, wv = a["L0_attn_Wq"], a["L0_attn_Wk"], a["L0_attn_Wv"]
    bq, bk, bv = a["L0_attn_bq"], a["L0_attn_bk"], a["L0_attn_bv"]
    e1 = a["L0_ffn_w1"].transpose(0, 2, 1).reshape(EXPERTS, DC, P, FF).transpose(0, 2, 1, 3)
    e2 = a["L0_ffn_w2"].transpose(0, 2, 1).reshape(EXPERTS, FC, P, D).transpose(0, 2, 1, 3)
    f1 = a["L1_ffn_w1"].reshape(EXPERTS, DC, P, 2 * FF).transpose(0, 2, 1, 3)
    f2 = a["L1_ffn_w2"].reshape(EXPERTS, FC, P, D).transpose(0, 2, 1, 3)
    by_expert = lambda v: v.reshape(EXPERTS, -1, P).transpose(0, 2, 1)
    arrays = {
        "xp": rows(xp),
        "cls_ln2b": np.stack([a["cls_tok"].reshape(D), a["L0_tok_ln2_b"]]),
        "Wp": rows(a["L0_tok_Wp"]),
        "ln1": np.stack([col(a["L0_tok_ln1_g"]), col(a["L0_tok_ln1_b"])], 1),
        "bp": a["L0_tok_bp"],
        "ln2_g": a["L0_tok_ln2_g"],
        "const": CONST,
        "wa0": np.stack([rows(w.T) for w in (wq, wk, wq[partner], wk[partner], wv)], 2),
        "ba0": np.stack([col(b) for b in (bq, bk, bq[partner], bk[partner], bv)], 1),
        "wo0": rows(a["L0_attn_Wo"].T),
        "bo0": a["L0_attn_bo"],
        "cent": rows(a["L0_ffn_centroids"].T),
        "w1_0": e1.reshape(EXPERTS, P, DC * FF),
        "w2_0": e2.reshape(EXPERTS, P, FC * D),
        "par_0": np.concatenate([by_expert(a["L0_ffn_ln_g"]), by_expert(a["L0_ffn_ln_b"]), by_expert(a["L0_ffn_b1"])], 2),
        "b2_0": a["L0_ffn_b2"],
        "wa1": np.stack([rows(a[f"L1_attn_w_{n}"].T) for n in "qkvo"], 2),
        "router": rows(a["L1_ffn_router_w"]),
        "router_b": a["L1_ffn_router_b"],
        "w1_1": f1.reshape(EXPERTS, P, DC * 2 * FF),
        "w2_1": f2.reshape(EXPERTS, P, FC * D),
    }
    nc = bacc.Bacc("TRN2", target_bir_lowering=False, num_devices=1)
    args = {}
    for name, array in arrays.items():
        array = np.ascontiguousarray(array)
        arrays[name] = array
        args[name] = nc.dram_tensor(name, array.shape, mybir.dt.from_np(array.dtype), kind="ExternalInput").ap()
    out = nc.dram_tensor("out", (TOKENS, D), F32, kind="ExternalOutput").ap()
    vit_tower(nc, *args.values(), out)
    got = run_bass_kernel_spmd(nc, [arrays], core_ids=[0])
    return got.results[0]["out"].reshape(IMAGES, SEQ, D)
```

```python
from contextlib import ExitStack

import numpy as np

import concourse.bass as bass
from concourse import mybir

P = 128
IMAGES, CHANNELS, SIDE, PATCH = 16, 3, 96, 16
GRID = SIDE // PATCH
SEQ = GRID * GRID + 1
TOKENS = IMAGES * SEQ
TILES = -(-TOKENS // P)
ROWS = TILES * P
D = 256
DC = D // P
PD = PATCH * PATCH * CHANNELS
PC = PD // P
HEADS, HD = 16, 16
PAIRS = IMAGES // 2
PW = 2 * SEQ
HALF = TOKENS // 2
QPAD = 64
EXPERTS, FF = 8, 1024
FC = FF // P
WIN = P
WINDOWS = (TOKENS - EXPERTS) // WIN + EXPERTS
MIN_WINDOWS = -(-TOKENS // WIN)
DUMP = WINDOWS * WIN
SLOTS = DUMP + P
EPS = 1e-5
SCALE = HD ** -0.5
NEG = -1e30
HALF_EVEN = 12582912.0

F32 = mybir.dt.float32
BF16 = mybir.dt.bfloat16
I32 = mybir.dt.int32
ALU = mybir.AluOpType
ACT = mybir.ActivationFunctionType
AX = mybir.AxisListType


def constant_columns():
    p = np.arange(P)[:, None]
    token = np.arange(ROWS).reshape(TILES, P).T
    inv_freq = 1.0 / 10000.0 ** (np.arange(0, HD, 2, dtype=np.float32) / HD)
    angle = np.outer(np.arange(SEQ, dtype=np.float32), inv_freq.astype(np.float32))
    freq = (np.arange(P) % HD) // 2
    sign = np.where(np.arange(P) % 2 == 0, -1.0, 1.0)[:, None]
    q = np.arange(P) % QPAD
    causal = np.where(np.arange(SEQ)[None, :] > q[:, None], NEG, 0.0)
    valid = (token < TOKENS)
    image = np.where(valid, token // SEQ, -1)
    is_patch = valid & (token % SEQ != 0)
    flat = np.arange(ROWS)
    tables = {
        "ident": np.eye(P),
        "minus_half": np.full((P, TILES), -0.5),
        "cos": np.cos(angle).T[freq],
        "sin": sign * np.sin(angle).T[freq],
        "causal": np.tile(causal, (1, 8)),
        "head4": ((p // HD) % 4 == np.arange(4)[None, :]),
        "head2": ((p // SEQ) == (np.arange(D)[None, :] // HD) % 2),
        "of_image": (image[:, :, None] == np.arange(IMAGES)).reshape(P, -1),
        "is_patch": is_patch,
        "valid": valid,
        "pad_slot": np.where(valid, 0, DUMP + token - TOKENS),
        "earlier": np.triu(np.ones((P, P)), 1),
        "ones": np.ones((P, P)),
        "first": np.broadcast_to(EXPERTS - np.arange(EXPERTS), (P, EXPERTS)),
        "full": np.broadcast_to(WIN * np.arange(TILES), (P, TILES)),
        "upto": np.broadcast_to(np.tril(np.ones((EXPERTS, EXPERTS))).reshape(-1), (P, EXPERTS * EXPERTS)),
        "window": np.broadcast_to(np.arange(WINDOWS + 1), (P, WINDOWS + 1)),
        "tiles_before": np.broadcast_to(np.tril(np.ones((TILES, TILES)), -1).reshape(-1), (P, TILES * TILES)),
    }
    row_tables = {
        "image_of": (flat // SEQ)[None, :] == np.arange(IMAGES)[:, None],
        "patch_row": np.pad(np.stack([(flat % SEQ == 0), (flat % SEQ != 0)]), ((0, IMAGES - 2), (0, 0))),
    }
    where, at = {}, 0
    for name, table in tables.items():
        where[name] = (at, at + table.shape[1])
        at += table.shape[1]
    join = lambda ts: np.concatenate([np.asarray(t, np.float32) for t in ts.values()], 1)
    return join(tables), join(row_tables), where


CONST, CONST_ROWS, CONST_AT = constant_columns()
CONST_FIRST = P + TILES


def vit_tower(nc, xp, cls_ln2b, Wp, ln1, bp, ln2_g, const, const_rows, wa0, ba0, wo0, bo0, cent, w1_0, w2_0, par_0, b2_0,
              wa1, router, router_b, w1_1, w2_1, out):
    with ExitStack() as ctx:
        def sb(name, shape, dt=F32):
            return ctx.enter_context(nc.sbuf_tensor(name, shape, dt))

        def sem(name):
            return ctx.enter_context(nc.semaphore(name))

        slots_in = nc.dram_tensor("slots_in", [SLOTS, D], F32)
        slots_out = nc.dram_tensor("slots_out", [SLOTS, D], F32)

        cst = sb("cst", [P, CONST.shape[1]])

        def table(name, rows=P):
            a, b = CONST_AT[name]
            return cst[0:rows, a:b]

        cst_rows = sb("cst_rows", CONST_ROWS.shape)
        image_of, patch_row = cst_rows[:, 0:ROWS], cst_rows[0:2, ROWS:2 * ROWS]

        ident = table("ident")
        identb = sb("identb", [P, P], BF16)
        causal_b = sb("causal_b", [P, 8 * SEQ], BF16)
        patches = sb("patches", [P, TILES, PD])
        wide = sb("wide", [P, IMAGES * D])
        patchT = wide[:, 0:PC * ROWS].rearrange("p (c n) -> p c n", n=ROWS)
        vD = wide[0:PW].rearrange("p (i d) -> p i d", d=D)
        wp_s = sb("wp_s", [P, PC, D])
        ln1_s = sb("ln1_s", [P, 2, PC])
        bp_s = sb("bp_s", [P, D])
        ln2g_s = sb("ln2g_s", [P, D])
        cls_s = sb("cls_s", [2, D])
        wa0_s = sb("wa0_s", [P, DC, 5, D])
        ba0_s = sb("ba0_s", [P, 5, DC])
        wo0_s = sb("wo0_s", [P, DC, D])
        bo0_s = sb("bo0_s", [P, D])
        cent_s = sb("cent_s", [P, DC, EXPERTS])
        wa1_s = sb("wa1_s", [P, DC, 4, D])
        wq1_s = sb("wq1_s", [P, DC, 4, D], BF16)
        router_s = sb("router_s", [P, DC, EXPERTS])
        routerb_s = sb("routerb_s", [P, EXPERTS])

        h = sb("h", [P, TILES, D])
        x = sb("x", [P, TILES, D])
        xd_z = sb("xd_z", [P, 2, TILES, D])
        xd, z = xd_z[:, 0], xd_z[:, 1]
        vT = xd_z[:].rearrange("p a t d -> p (a t d)")[:, 0:DC * IMAGES * 2 * SEQ].rearrange(
            "p (c i o k) -> p c i o k", c=DC, i=IMAGES, o=2)
        xT = sb("xT", [P, DC, ROWS])
        oT = sb("oT", [P, DC, ROWS])
        xqb = sb("xqb", [P, TILES, D], BF16)
        xTb = sb("xTb", [P, DC, ROWS], BF16)
        mv3 = sb("mv3", [P, 3, TILES, 2])
        veps3 = sb("veps3", [P, 3, TILES])
        rstd3 = sb("rstd3", [P, 3, TILES])
        stats = sb("stats", [P, TILES, 3, 6])
        mv = sb("mv", [P, TILES, 2])
        veps = sb("veps", [P, TILES])
        rstd = sb("rstd", [P, TILES])
        stat2 = sb("stat2", [P, TILES, 3])
        img = sb("img", [IMAGES, 8])
        tokstat = sb("tokstat", [P, TILES, 2])
        amax = sb("amax", [P, TILES])
        inv_s = sb("inv_s", [P, TILES])
        act_s = sb("act_s", [P, TILES])
        spread = sb("spread", [P, TILES, P])
        invT = sb("invT", [P, ROWS])
        wsum = sb("wsum", [P, 4])
        wmean = sb("wmean", [P, 4])
        wscale = sb("wscale", [P, 4])
        qk_scale = sb("qk_scale", [P, 1])

        qr, kr = (patches[:].rearrange("p t d -> p (t d)")[:, i * DC * ROWS:(i + 1) * DC * ROWS].rearrange("p (c n) -> p c n", n=ROWS)
                  for i in range(2))
        qW = sb("qW", [P, 2, DC, 2, QPAD])
        kM = sb("kM", [P, 2, DC, 2, 4, SEQ])
        vM = sb("vM", [PW, 2, 2, D])
        sc = sb("sc", [P, 2, 2, 8 * SEQ])
        prob = sb("prob", [P, 2, HEADS, SEQ])
        smax = sb("smax", [P, 2, 2, 8])
        srec = sb("srec", [P, DC * PW])
        pT = sb("pT", [PW, 2, 8, P])

        lg = sb("lg", [P, TILES, EXPERTS])
        lmax = sb("lmax", [P, TILES])
        lexp = sb("lexp", [P, TILES, EXPERTS])
        gate = sb("gate", [P, TILES])
        r1 = sb("r1", [P, TILES, EXPERTS])
        rsmall = sb("rsmall", [P, TILES])
        hot = sb("hot", [P, TILES, EXPERTS])
        mine = sb("mine", [P, EXPERTS])
        rank = sb("rank", [P, TILES, EXPERTS])
        cmp = sb("cmp", [P, TILES * EXPERTS * TILES])
        nwin = sb("nwin", [P, EXPERTS])
        wend = sb("wend", [P, EXPERTS])
        wbeg = sb("wbeg", [P, EXPERTS])
        winexp = sb("winexp", [P, WINDOWS + 4])
        winexp_i = sb("winexp_i", [P, WINDOWS + 4], I32)
        slot_f = sb("slot_f", [P, TILES])
        slot_i = sb("slot_i", [P, TILES], I32)

        zero = sb("zero", [P, D])
        stored = sb("stored", [1, 1])
        w1_s = sb("w1_s", [P, 2, DC * 2 * FF])
        wpg_s = w1_s[:, 0, 0:PC * D].rearrange("p (c n) -> p c n", n=D)
        ln1b_s = w1_s[:, 1, 0:PC * P].rearrange("p (c n) -> p c n", n=P)
        w2_s = sb("w2_s", [P, 2, FC, D])
        par_s = sb("par_s", [P, 2, 2 * DC + FC])
        b2_s = sb("b2_s", [P, 2, D])
        xw = sb("xw", [P, 2, D])
        xwT = sb("xwT", [P, 2, DC, WIN])
        hid = patches[:].rearrange("p t d -> p (t d)")[:, 2 * DC * ROWS:2 * DC * ROWS + FC * WIN].rearrange("p (f n) -> p f n", n=WIN)
        act_a = sb("act_a", [P, 2, WIN])
        zw = sb("zw", [P, 2, D])

        psum = ctx.enter_context(nc.psum_tensor("psum", [P, 8, 512], F32))

        block = None
        S = {}

        def s(name):
            if name not in S:
                S[name] = sem(name)
            return S[name]

        class Chain:

            def __init__(self, eng, name):
                self.eng, self.sem, self.n, self.base = eng, s(name), 0, 0

            def __call__(self, ins):
                ins.then_inc(self.sem, 1)
                self.n += 1
                self.eng.wait_ge(self.sem, self.base + self.n)

            def post(self, ins):
                ins.then_inc(self.sem, 1)
                self.n += 1
                return self.n

            def until(self, ticket):
                self.eng.wait_ge(self.sem, ticket)

            def loop(self, index, per):
                self.start, self.per = self.n, per
                self.base = index * per

            def again(self, offset):
                self.n = self.start + offset

            def end(self, count):
                self.base, self.n = 0, self.start + count

        for name in ("dve_own", "act_own", "pool_own"):
            s(name)

        def loads(sp):
            sp.dma_start(patches[:, 0, :], xp[:, 0, :]).then_inc(s("in_patch0"), 16)
            sp.dma_start(cst[:, 0:CONST_FIRST], const[:, 0:CONST_FIRST]).then_inc(s("in_first"), 16)
            sp.dma_start(patches[:, 1, :], xp[:, 1, :]).then_inc(s("in_patch1"), 16)
            sp.dma_start(ln1_s[:], ln1[:]).then_inc(s("in_embed"), 16)
            sp.dma_start(wp_s[:], Wp[:]).then_inc(s("in_embed"), 16)
            for i in range(2, TILES):
                sp.dma_start(patches[:, i, :], xp[:, i, :]).then_inc(s(f"in_patch{i}"), 16)
            for dst, src in ((bp_s, bp), (ln2g_s, ln2_g)):
                sp.dma_start(dst[:], src.rearrange("(a d) -> a d", a=1).to_broadcast([P, D])).then_inc(s("in_rows"), 16)
            sp.dma_start(cls_s[:], cls_ln2b[:]).then_inc(s("in_rows"), 16)
            sp.dma_start(cst[:, CONST_FIRST:], const[:, CONST_FIRST:]).then_inc(s("in_const"), 16)
            sp.dma_start(cst_rows[:], const_rows[:]).then_inc(s("in_const"), 16)
            sp.dma_start(wa0_s[:], wa0[:]).then_inc(s("in_attn0"), 16)
            sp.dma_start(ba0_s[:], ba0[:]).then_inc(s("in_attn0"), 16)
            sp.dma_start(wo0_s[:], wo0[:]).then_inc(s("in_attn0"), 16)
            sp.dma_start(bo0_s[:], bo0.rearrange("(a d) -> a d", a=1).to_broadcast([P, D])).then_inc(s("in_attn0"), 16)
            sp.dma_start(cent_s[:], cent[:]).then_inc(s("in_moe0"), 16)
            sp.dma_start(wa1_s[:], wa1[:]).then_inc(s("in_attn1"), 16)
            sp.dma_start(router_s[:], router[:]).then_inc(s("in_moe1"), 16)
            sp.dma_start(routerb_s[:], router_b.rearrange("(a d) -> a d", a=1).to_broadcast([P, EXPERTS])).then_inc(s("in_moe1"), 16)
            sp.wait_ge(s("zeros"), 1)
            for slots in (slots_in, slots_out):
                sp.dma_start(slots[:, :].rearrange("(w p) d -> p w d", p=P),
                             zero[:].rearrange("p (o d) -> p o d", o=1).to_broadcast([P, SLOTS // P, D])).then_inc(s("slots_zeroed"), 16)

        ZEROED = 32

        def norm_vector(dve, do, src, dst, tag, eps_done, prepare=None):
            made, counted = {}, {}
            for i in range(TILES + 2):
                if i < TILES and prepare is not None:
                    made[i] = do.post(prepare(i))
                if 1 <= i <= TILES:
                    if prepare is not None:
                        do.until(made[i - 1])
                    counted[i - 1] = do.post(nc.vector.bn_stats(stats[:, i - 1, 0, :], src[:, i - 1, :]))
                if i >= 2:
                    do.until(counted[i - 2])
                    last = do.post(nc.vector.bn_aggr(mv[:, i - 2, :], stats[:, i - 2, 0:1, :]))
            do.until(last)
            nc.vector.tensor_scalar(veps[:], mv[:, :, 1], EPS, None, ALU.add).then_inc(s("veps_ready"), 1)
            dve.wait_ge(s("rstd_ready"), eps_done)
            for i in range(TILES):
                nc.vector.tensor_scalar(dst[:, i, :], src[:, i, :], mv[:, i, 0:1], rstd[:, i:i + 1],
                                        ALU.subtract, ALU.mult).then_inc(s(tag), 1)

        EMBED_STAGES = ([("patch", 0), ("patch", 1), ("patch_norm", 0), ("patch", 2), ("patch_norm", 1), ("patch", 3),
                         ("patch_norm", 2), ("patch", 4), ("patch_norm", 3), ("patch_norm", 4)]
                        + [("y", 0), ("h", 0), ("y", 1), ("x", 0), ("h", 1), ("y", 2), ("x", 1), ("h", 2), ("y", 3), ("x", 2),
                           ("h", 3), ("y", 4), ("x", 3), ("h", 4), ("x", 4)])
        POWERS_OF = {"patch": 0, "y": 1, "h": 2}
        NORMS = 3 * TILES
        EMBED_POWERS = [stage for stage in EMBED_STAGES if stage[0] in POWERS_OF]

        def embed_vector(dve, do):
            nc.vector.memset(zero[:], 0.0).then_inc(s("zeros"), 1)
            do(nc.vector.memset(oT[:], 0.0))
            do(nc.vector.memset(qW[:], 0.0))

            def mean_of(kind, i):
                return mv3[:, POWERS_OF[kind], i, 0:1]

            def rstd_of(kind, i):
                return rstd3[:, POWERS_OF[kind], i:i + 1]

            def statistics(kind, i, src, groups=1):
                width = src.shape[-1] // groups
                for g in range(groups):
                    counted = do.post(nc.vector.bn_stats(stats[:, i, g, :], src[:, g * width:(g + 1) * width]))
                do.until(counted)
                do(nc.vector.bn_aggr(mv3[:, POWERS_OF[kind], i, :], stats[:, i, 0:groups, :]))
                nc.vector.tensor_scalar(veps3[:, POWERS_OF[kind], i:i + 1], mv3[:, POWERS_OF[kind], i, 1:2], EPS, None,
                                        ALU.add).then_inc(s("veps_ready"), 1)

            def power_done(kind, i):
                dve.wait_ge(s("rstd_ready"), EMBED_POWERS.index((kind, i)) + 1)

            for stage, i in EMBED_STAGES:
                if stage == "patch":
                    dve.wait_ge(s(f"in_patch{i}"), 16)
                    statistics("patch", i, patches[:, i, :], groups=3)
                elif stage == "patch_norm":
                    power_done("patch", i)
                    nc.vector.tensor_scalar(patches[:, i, :], patches[:, i, :], mean_of("patch", i), rstd_of("patch", i),
                                            ALU.subtract, ALU.mult).then_inc(s("patch_normed"), 1)
                elif stage == "y":
                    if i == 0:
                        dve.wait_ge(s("in_rows"), 48)
                        dve.wait_ge(s("bias_ps"), 1)
                        nc.vector.tensor_tensor(bp_s[:], psum[:, 7, 0:D], bp_s[:], ALU.add).then_inc(s("bias_row"), 1)
                        dve.wait_ge(s("bias_row"), 1)
                    dve.wait_ge(s("y_ps"), i + 1)
                    nc.vector.tensor_tensor(x[:, i, :], psum[:, 4 + i % 2, 0:D], bp_s[:], ALU.add).then_inc(s("y_read"), 1)
                    dve.wait_ge(s("y_read"), i + 1)
                    statistics("y", i, x[:, i, :])
                elif stage == "h":
                    if i == 0:
                        dve.wait_ge(s("in_const"), 32)
                    power_done("y", i)
                    do(nc.vector.tensor_tensor(rstd_of("y", i), rstd_of("y", i), table("is_patch")[:, i:i + 1], ALU.mult))
                    do(nc.vector.scalar_tensor_tensor(out=xd[:, i, :], in0=x[:, i, :], scalar=mean_of("y", i), in1=ln2g_s[:],
                                                      op0=ALU.subtract, op1=ALU.mult))
                    dve.wait_ge(s("cls_ps"), i + 1)
                    nc.vector.scalar_tensor_tensor(out=h[:, i, :], in0=xd[:, i, :], scalar=rstd_of("y", i), in1=psum[:, 6 + i % 2, 0:D],
                                                   op0=ALU.mult, op1=ALU.add).then_inc(s("h_made"), 1)
                    dve.wait_ge(s("h_made"), i + 1)
                    statistics("h", i, h[:, i, :])
                else:
                    power_done("h", i)
                    nc.vector.tensor_scalar(x[:, i, :], h[:, i, :], mean_of("h", i), rstd_of("h", i),
                                            ALU.subtract, ALU.mult).then_inc(s("x_attn0"), 1)
            dve.wait_ge(s("in_attn0"), 64)
            dve.wait_ge(s("x_attn0"), TILES)
            for i in range(TILES):
                last = do.post(nc.vector.tensor_tensor(h[:, i, :], h[:, i, :], bo0_s[:], ALU.add))
            do.until(last)

        def embed_gpsimd(pool):
            pool.wait_ge(s("in_first"), 16)
            for n, (kind, i) in enumerate(EMBED_POWERS):
                k = POWERS_OF[kind]
                pool.wait_ge(s("veps_ready"), n + 1)
                nc.gpsimd.tensor_tensor(rstd3[:, k, i:i + 1], veps3[:, k, i:i + 1], table("minus_half")[:, 0:1],
                                        ALU.pow).then_inc(s("rstd_ready"), 1)

        def two_banks(c):
            b = 2 * (c % 2)
            return psum[:, b:b + 2, :].rearrange("p b n -> p (b n)")[:, 0:ROWS]

        def patch_banks(i):
            b = 2 * (i % 2)
            return psum[:, b:b + 2, :].rearrange("p b n -> p (b n)")[:, 0:PD]

        def tile_bank(i):
            return psum[:, i, 0:D]

        def embed_scalar(act, do):
            act.wait_ge(s("in_embed"), 32)
            for c in range(PC):
                nc.scalar.activation(wpg_s[:, c, :], wp_s[:, c, :], ACT.Copy, scale=ln1_s[:, 0, c:c + 1]).then_inc(s("wpg_ready"), 1)
            act.wait_ge(s("in_first"), 16)
            nc.scalar.activation(identb[:], ident, ACT.Copy)
            for i in range(TILES):
                if i == 1:
                    for c in range(PC):
                        nc.scalar.activation(ln1b_s[:, c, :], ident, ACT.Identity, scale=0.0,
                                             bias=ln1_s[:, 1, c:c + 1]).then_inc(s("ln1b_ready"), 1)
                act.wait_ge(s("patchT_ps"), i + 1)
                nc.scalar.activation(patchT[:, :, i * P:(i + 1) * P], patch_banks(i).rearrange("p (c n) -> p c n", n=P),
                                     ACT.Copy).then_inc(s("patchT"), 1)
            act.wait_ge(s("in_const"), 32)
            nc.scalar.activation(causal_b[:], table("causal"), ACT.Copy).then_inc(s("identb_ready"), 1)

        def embed_tensor(pe):
            def turn(i):
                pe.wait_ge(s("patch_normed"), i + 1)
                if i >= 2:
                    pe.wait_ge(s("patchT"), i - 1)
                for c in range(PC):
                    last = nc.tensor.transpose(patch_banks(i)[:, c * P:(c + 1) * P], patches[:, i, c * P:(c + 1) * P], ident)
                last.then_inc(s("patchT_ps"), 1)

            def embed(i):
                pe.wait_ge(s("patchT"), i + 1)
                if i == 0:
                    pe.wait_ge(s("wpg_ready"), PC)
                if i >= 2:
                    pe.wait_ge(s("y_read"), i - 1)
                for c in range(PC):
                    last = nc.tensor.matmul(psum[:, 4 + i % 2, 0:D], patchT[:, c, i * P:(i + 1) * P], wpg_s[:, c, :],
                                            start=(c == 0), stop=(c == PC - 1))
                last.then_inc(s("y_ps"), 1)

            def row_constants(i):
                if i >= 2:
                    pe.wait_ge(s("h_made"), i - 1)
                nc.tensor.matmul(psum[:, 6 + i % 2, 0:D], patch_row[:, i * P:(i + 1) * P], cls_s[:],
                                 start=True, stop=True).then_inc(s("cls_ps"), 1)
            pe.wait_ge(s("in_first"), 16)
            turn(0)
            turn(1)
            pe.wait_ge(s("in_embed"), 32)
            pe.wait_ge(s("ln1b_ready"), PC)
            for c in range(PC):
                last = nc.tensor.matmul(psum[:, 7, 0:D], ln1b_s[:, c, :], wp_s[:, c, :], start=(c == 0), stop=(c == PC - 1))
            last.then_inc(s("bias_ps"), 1)
            embed(0)
            turn(2)
            pe.wait_ge(s("in_const"), 32)
            pe.wait_ge(s("in_rows"), 48)
            row_constants(0)
            pe.wait_ge(s("bias_row"), 1)
            row_constants(1)
            for i in range(1, TILES):
                embed(i)
                if i + 2 < TILES:
                    turn(i + 2)
                if i >= 2:
                    row_constants(i)
            turn_tensor(pe, x, "x_attn0", "turn_a0")

        def turn_tensor(pe, src, ready, tag):
            for i in range(TILES):
                pe.wait_ge(s(ready), i + 1)
                for c in range(DC):
                    last = nc.tensor.transpose(psum[:, i, c * P:(c + 1) * P], src[:, i, c * P:(c + 1) * P], ident)
                last.then_inc(s(tag + "_ps"), 1)

        def turn_scalar(act, dst, tag):
            for i in range(TILES):
                act.wait_ge(s(tag + "_ps"), i + 1)
                nc.scalar.activation(dst[:, :, i * P:(i + 1) * P], psum[:, i, 0:DC * P].rearrange("p (c n) -> p c n", n=P),
                                     ACT.Copy).then_inc(s(tag), 1)

        def bank(b, parts=P):
            return psum[0:parts, b, :]

        def reused(engine, semaphore, count):
            if not (isinstance(count, int) and count <= 0):
                engine.wait_ge(semaphore, count)

        def attention(layer):
            done = layer * PAIRS
            L = f"_a{layer}"
            src = xT if layer == 0 else xTb
            weights = wa0_s if layer == 0 else wq1_s
            Q, K, V = (0, 1, 4) if layer == 0 else (0, 1, 2)
            halves = range(2)
            values = [("v", V, c, half) for half in halves for c in range(DC)]

            def queries_keys(half):
                groups = (Q, Q + 2, K, K + 2) if layer == 0 else (Q, K)
                return [("qk", g, c, half) for c in range(DC) for g in groups]
            by_key = [("t", p) for p in range(PAIRS)]
            units = values + queries_keys(0) + by_key + queries_keys(1)

            def read_count(upto, kind):
                return sum(unit[0] == kind for unit in units[:upto + 1])

            def unit_psum(n, parts=P):
                return psum[0:parts, n % 8, :]

            def project_tensor(pe):
                for n, unit in enumerate(units):
                    if n >= 8:
                        kind = units[n - 8][0]
                        pe.wait_ge(s(f"{kind}_read" + L), read_count(n - 8, kind))
                    if unit[0] == "t":
                        p = unit[1]
                        pe.wait_ge(s("v_read" + L), DC * (p // (PAIRS // 2) + 1))
                        for j in range(2):
                            for c in range(DC):
                                last = nc.tensor.transpose(
                                    unit_psum(n, PW)[:, j * D + c * P:j * D + (c + 1) * P],
                                    vT[:, c, 2 * p + j, :, :].rearrange("p o k -> p (o k)"), ident)
                    else:
                        _, g, c, half = unit
                        for k in range(DC):
                            last = nc.tensor.matmul(unit_psum(n)[:, 0:HALF], weights[:, k, g, c * P:(c + 1) * P],
                                                    src[:, k, half * HALF:(half + 1) * HALF], start=(k == 0), stop=(k == DC - 1))
                    last.then_inc(s("unit" + L), 1)

            def values_twice(c, half):
                return vT[:, c, half * IMAGES // 2:(half + 1) * IMAGES // 2, :, :]

            def twice(tokens):
                return tokens.rearrange("p (i o k) -> p i o k", o=1, k=SEQ).to_broadcast([P, IMAGES // 2, 2, SEQ])

            def project_vector(dve):
                count = 0
                for n, unit in enumerate(units):
                    if unit[0] == "v" and layer == 1:
                        _, g, c, half = unit
                        dve.wait_ge(s("unit" + L), n + 1)
                        nc.vector.tensor_tensor(values_twice(c, half), twice(unit_psum(n)[:, 0:HALF]),
                                                twice(invT[:, half * HALF:(half + 1) * HALF]), ALU.mult).then_inc(s("v_read" + L), 1)
                    if unit[0] != "qk":
                        continue
                    _, g, c, half = unit
                    dve.wait_ge(s("unit" + L), n + 1)
                    if layer == 0:
                        turn, part = count // 2, count % 2
                        reused(dve, s("rotated"), turn - 1)
                        images = lambda a: a.rearrange("p (i k) -> p i k", k=SEQ)
                        nc.vector.scalar_tensor_tensor(
                            out=images(sc[:, turn % 2, part, :]), in0=images(unit_psum(n)[:, 0:HALF]), scalar=ba0_s[:, g, c:c + 1],
                            in1=table("sin" if part else "cos").rearrange("p (o k) -> p o k", o=1).to_broadcast([P, IMAGES // 2, SEQ]),
                            op0=ALU.add, op1=ALU.mult).then_inc(s("qk_read" + L), 1)
                    else:
                        dst = qr if g == Q else kr
                        nc.vector.tensor_tensor(dst[:, c, half * HALF:(half + 1) * HALF], unit_psum(n)[:, 0:HALF],
                                                invT[:, half * HALF:(half + 1) * HALF], ALU.mult).then_inc(s("qk_read" + L), 1)
                    count += 1

            def project_gpsimd(pool):
                if layer == 0:
                    turn = 0
                    for unit in units:
                        if unit[0] == "qk" and unit[1] in (Q, K):
                            _, g, c, half = unit
                            dst = qr if g == Q else kr
                            pool.wait_ge(s("qk_read" + L), 2 * turn + 2)
                            nc.gpsimd.tensor_tensor(dst[:, c, half * HALF:(half + 1) * HALF], sc[:, turn % 2, 0, :],
                                                    sc[:, turn % 2, 1, :], ALU.add).then_inc(s("rotated"), 1)
                            turn += 1
                            if turn == 2 * DC:
                                first_spreads(pool)

            def first_spreads(pool):
                pool.wait_ge(s("rotated") if layer == 0 else s("qk_read" + L), 2 * DC)
                spread_gpsimd(pool, 0, 0)
                spread_gpsimd(pool, 1, 1)

            def project_scalar(act):
                for n, unit in enumerate(units):
                    if unit[0] == "v" and layer == 0:
                        _, g, c, half = unit
                        act.wait_ge(s("unit" + L), n + 1)
                        nc.scalar.activation(values_twice(c, half), twice(unit_psum(n)[:, 0:HALF]), ACT.Identity,
                                             bias=ba0_s[:, 4, c:c + 1]).then_inc(s("v_read" + L), 1)
                    if unit[0] == "t":
                        p = unit[1]
                        act.wait_ge(s("unit" + L), n + 1)
                        nc.scalar.activation(vD[:, 2 * p:2 * p + 2, :], unit_psum(n, PW).rearrange("p (j d) -> p j d", d=D),
                                             ACT.Copy).then_inc(s("t_read" + L), 1)

            def scores_psum(buf):
                return psum[:, 2 * buf:2 * buf + 2, 0:8 * SEQ]

            def scores_tensor(pe, p, buf):
                pe.wait_ge(s("kM_ready"), done + p + 1)
                if not early(p):
                    pe.wait_ge(s("sc_read"), done + p - 1)
                if layer == 1:
                    nc.tensor.matmul(bank(2 * buf)[:, 511:512], identb[:], identb[:, 0:1], start=True, stop=True)
                for c in range(DC):
                    columns = slice(c * 4 * SEQ, (c + 1) * 4 * SEQ)
                    for j in range(2):
                        rows = slice(64 * j, 64 * j + QPAD)
                        for r in range(2):
                            if layer == 0:
                                nc.tensor.matmul(bank(2 * buf + r)[rows, columns], identb[:, rows], causal_b[:, columns],
                                                 start=True, stop=False)
                            last = nc.tensor.matmul(bank(2 * buf + r)[rows, columns], qW[64 * r:64 * r + 64, buf, c, j, :],
                                                    kM[64 * r:64 * r + 64, buf, c, j, :, :].rearrange("p a k -> p (a k)"),
                                                    start=(layer == 1), stop=True)
                last.then_inc(s("sc_ps"), 1)

            def early(p):
                return isinstance(p, int) and p < 2

            def turn_probs_tensor(pe, p, buf):
                pe.wait_ge(s("exp"), done + p + 1)
                if not (isinstance(p, int) and p == 0):
                    pe.wait_ge(s("pT_ready"), done + p)
                for g in range(8):
                    last = nc.tensor.transpose(bank(4 + g // 4, PW)[:, (g % 4) * P:(g % 4 + 1) * P],
                                               prob[:, buf, 2 * g:2 * g + 2, :].rearrange("p a k -> p (a k)"), ident)
                last.then_inc(s("pT_ps"), 1)

            def output_tensor(pe, p, buf):
                pe.wait_ge(s("pT_ready"), done + p + 1)
                pe.wait_ge(s("vM_ready"), done + p + 1)
                dst = bank(6 + buf)
                for g in range(8):
                    r, c, hp = g // 4, (g // 2) % 2, g % 2
                    row = 64 * r + 32 * hp
                    for j in range(2):
                        nc.tensor.matmul(dst[row:row + 32, c * PW + j * SEQ:c * PW + (j + 1) * SEQ],
                                         vM[:, buf, j, c * P + row:c * P + row + 32],
                                         pT[:, buf, g, 64 * j:64 * j + SEQ], start=True, stop=True, tile_position=(0, row))
                    last = nc.tensor.matmul(dst[row:row + 32, (DC + c) * PW:(DC + c + 1) * PW], table("head2", PW)[:, 0:2 * HD],
                                            pT[:, buf, g, :].rearrange("p (j q) -> p j q", j=2)[:, :, 0:SEQ],
                                            start=True, stop=True, tile_position=(0, row))
                last.then_inc(s("o_ps"), 1)

            def tensor(pe):
                pe.wait_ge(s("identb_ready"), 1)
                project_tensor(pe)
                for kind in ("qk", "t", "v"):
                    pe.wait_ge(s(f"{kind}_read" + L), read_count(len(units), kind))
                scores_tensor(pe, 0, 0)
                scores_tensor(pe, 1, 1)
                turn_probs_tensor(pe, 0, 0)
                with pe.Fori(1, PAIRS // 2) as u:
                    for b in range(2):
                        p = u * 2 + b
                        scores_tensor(pe, p, b)
                        turn_probs_tensor(pe, p - 1, 1 - b)
                        output_tensor(pe, p - 2, b)
                turn_probs_tensor(pe, PAIRS - 1, 1)

                def finish(i):
                    pe.wait_ge(s("o_read"), done + min(PAIRS, -(-(i + 1) * P // PW)))
                    if i == TILES - 1:
                        pe.wait_ge(s("pT_ready"), done + PAIRS)
                    for c in range(DC):
                        if layer == 0:
                            last = nc.tensor.matmul(tile_bank(i), oT[:, c, i * P:(i + 1) * P], wo0_s[:, c, :], start=(c == 0), stop=(c == DC - 1))
                        else:
                            last = nc.tensor.transpose(tile_bank(i)[:, c * P:(c + 1) * P], oT[:, c, i * P:(i + 1) * P], ident)
                    last.then_inc(s("finished" + L), 1)
                output_tensor(pe, PAIRS - 2, 0)
                finish(0)
                finish(1)
                finish(2)
                output_tensor(pe, PAIRS - 1, 1)
                finish(3)
                finish(4)

            def softmax_vector(dve, p, buf):
                heads = lambda a: a.rearrange("p r (n k) -> p r n k", k=SEQ)
                dve.wait_ge(s("sc_ps"), done + p + 1)
                nc.vector.reduce_max(smax[:, buf], heads(scores_psum(buf)), AX.X).then_inc(s("smax"), 1)
                dve.wait_ge(s("smax"), done + p + 1)
                if not early(p):
                    dve.wait_ge(s("exp"), done + p - 1)
                nc.vector.tensor_tensor(heads(sc[:, buf]), heads(scores_psum(buf)),
                                        smax[:, buf].rearrange("p r (n o) -> p r n o", o=1).to_broadcast([P, 2, 8, SEQ]),
                                        ALU.subtract).then_inc(s("sc_read"), 1)

            def mask_values_vector(dve, p, buf):
                if not early(p):
                    dve.wait_ge(s("o_ps"), done + p - 1)
                nc.vector.tensor_tensor(vM[:, buf, :, :], vD[:, bass.ds(p * 2, 2), :],
                                        table("head2", PW).rearrange("p (o d) -> p o d", o=1).to_broadcast([PW, 2, D]),
                                        ALU.mult).then_inc(s("vM_ready"), 1)

            def output_vector(dve, p, buf):
                dve.wait_ge(s("o_ps"), done + p + 1)
                nc.vector.reciprocal(srec[:], bank(6 + buf)[:, DC * PW:2 * DC * PW]).then_inc(s("srec"), 1)
                dve.wait_ge(s("srec"), done + p + 1)
                dst = oT[:, :, bass.ds(p * PW, PW)]
                raw = bank(6 + buf)[:, 0:DC * PW].rearrange("p (c n) -> p c n", n=PW)
                rec = srec[:].rearrange("p (c n) -> p c n", n=PW)
                if layer == 0:
                    nc.vector.tensor_tensor(dst, raw, rec, ALU.mult).then_inc(s("o_read"), 1)
                else:
                    nc.vector.scalar_tensor_tensor(out=dst, in0=raw, scalar=wmean[:, 2:3], in1=rec, op0=ALU.mult,
                                                   op1=ALU.mult).then_inc(s("o_read"), 1)
                dve.wait_ge(s("o_read"), done + p + 1)

            def vector(dve, do):
                project_vector(dve)
                if layer == 0:
                    dve.wait_ge(s("rotated"), 4 * DC)
                for p in range(2):
                    softmax_vector(dve, p, p)
                    if p == 0:
                        dve.wait_ge(s("t_read" + L), PAIRS)
                    mask_values_vector(dve, p, p)
                with dve.Fori(1, PAIRS // 2) as u:
                    for b in range(2):
                        p = u * 2 + b
                        softmax_vector(dve, p, b)
                        output_vector(dve, p - 2, b)
                        mask_values_vector(dve, p, b)
                output_vector(dve, PAIRS - 2, 0)
                output_vector(dve, PAIRS - 1, 1)

            def spread_gpsimd(pool, p, buf):
                if not early(p):
                    pool.wait_ge(s("sc_ps"), done + p - 1)
                pair = lambda a: a[:, :, bass.ds(p * PW, PW)].rearrange("p c (j k) -> p c j k", k=SEQ)
                nc.gpsimd.tensor_copy(qW[:, buf, :, :, 0:SEQ], pair(qr))
                for c in range(DC):
                    last = nc.gpsimd.tensor_tensor(
                        kM[:, buf, c, :, :, :],
                        kr[:, c, bass.ds(p * PW, PW)].rearrange("p (j o k) -> p j o k", o=1, k=SEQ).to_broadcast([P, 2, 4, SEQ]),
                        table("head4").rearrange("p (o a u) -> p o a u", o=1, u=1).to_broadcast([P, 2, 4, SEQ]), ALU.mult)
                last.then_inc(s("kM_ready"), 1)

            def gpsimd(pool):
                project_gpsimd(pool)
                if layer == 1:
                    first_spreads(pool)
                pool.wait_ge(s("rotated") if layer == 0 else s("qk_read" + L), 4 * DC)
                with pool.Fori(1, PAIRS // 2) as u:
                    for b in range(2):
                        p = u * 2 + b
                        spread_gpsimd(pool, p, b)

            def scalar(act):
                def step(p, buf):
                    act.wait_ge(s("sc_read"), done + p + 1)
                    if not early(p):
                        act.wait_ge(s("pT_ps"), done + p - 1)
                    nc.scalar.activation(prob[:, buf].rearrange("p n k -> p (n k)"), sc[:, buf].rearrange("p r n -> p (r n)"), ACT.Exp,
                                         scale=SCALE if layer == 0 else qk_scale[:, 0:1]).then_inc(s("exp"), 1)
                    act.wait_ge(s("pT_ps"), done + p + 1)
                    if not early(p):
                        act.wait_ge(s("o_ps"), done + p - 1)
                    nc.scalar.activation(pT[:, buf], psum[0:PW, 4:6, :].rearrange("p b (g n) -> p (b g) n", n=P),
                                         ACT.Copy).then_inc(s("pT_ready"), 1)
                project_scalar(act)
                step(0, 0)
                step(1, 1)
                with act.Fori(1, PAIRS // 2) as u:
                    for b in range(2):
                        step(u * 2 + b, b)

            return tensor, vector, gpsimd, scalar

        attn0 = attention(0)
        attn1 = attention(1)

        def moe(layer):
            L = f"_m{layer}"
            F1 = FF * (1 + layer)
            w1, w2 = (w1_0, w2_0) if layer == 0 else (w1_1, w2_1)
            logit_w = cent_s if layer == 0 else router_s
            HC = F1 // P

            def load_count(engine):
                return engine.value_load(winexp_i[0:1, WINDOWS + 1:WINDOWS + 2], min_val=MIN_WINDOWS, max_val=WINDOWS)

            def load_pairs(engine):
                return engine.value_load(winexp_i[0:1, WINDOWS + 2:WINDOWS + 3], min_val=-(-MIN_WINDOWS // 2), max_val=WINDOWS // 2)

            def load_seconds(engine):
                return engine.value_load(winexp_i[0:1, WINDOWS + 3:WINDOWS + 4], min_val=MIN_WINDOWS // 2, max_val=WINDOWS // 2)

            def windows(engine, body, before=None):
                engine.wait_ge(s("table" + L), 1)
                count = load_count(engine)
                pairs = load_pairs(engine)
                if before is not None:
                    before()
                body(0, 0)
                body(0, 1)
                with engine.Fori(1, pairs) as u:
                    body(u, 0)
                    with engine.If(u * 2 + 1 < count):
                        body(u, 1)
                return count

            def logits_tensor(pe):
                pe.wait_ge(s("in_moe0" if layer == 0 else "in_moe1"), 16 if layer == 0 else 32)
                for i in range(TILES):
                    pe.wait_ge(s("turned" + L), i + 1)
                    for c in range(DC):
                        last = nc.tensor.matmul(bank(7)[:, i * EXPERTS:(i + 1) * EXPERTS], xT[:, c, i * P:(i + 1) * P],
                                                logit_w[:, c, :], start=(c == 0), stop=(c == DC - 1))
                last.then_inc(s("logits" + L), 1)
                pe.wait_ge(s("hot" + L), 1)
                nc.tensor.matmul(bank(5)[:, 0:EXPERTS], table("earlier"), mine[:], start=True, stop=True)
                nc.tensor.matmul(bank(6)[:, 0:EXPERTS], table("ones"), mine[:], start=True, stop=True).then_inc(s("ranks" + L), 1)

            def route_vector(dve, do):
                T8 = [P, TILES, EXPERTS]
                per_expert = lambda a: a.rearrange("p (o e) -> p o e", o=1).to_broadcast(T8)
                per_row = lambda a: a.rearrange("p (t o) -> p t o", o=1).to_broadcast(T8)
                dve.wait_ge(s("logits" + L), 1)
                logits = bank(7)[:, 0:TILES * EXPERTS].rearrange("p (t e) -> p t e", e=EXPERTS)
                if layer == 0:
                    do(nc.vector.reduce_max(lmax[:], logits, AX.X))
                    ranked, top = logits, lmax
                    nc.vector.tensor_copy(gate[:], lmax[:]).then_inc(s("gate_in" + L), 1)
                else:
                    do(nc.vector.tensor_tensor(lg[:], logits, per_expert(routerb_s[:]), ALU.add))
                    do(nc.vector.reduce_max(lmax[:], lg[:], AX.X))
                    nc.vector.tensor_tensor(lexp[:], lg[:], per_row(lmax[:]), ALU.subtract).then_inc(s("gate_in" + L), 1)
                    dve.wait_ge(s("gate_exp" + L), 1)
                    do(nc.vector.reduce_max(lmax[:], lexp[:], AX.X))
                    ranked, top = lexp[:], lmax
                do(nc.vector.tensor_tensor(r1[:], ranked, per_row(top[:]), ALU.is_equal))
                do(nc.vector.tensor_tensor(r1[:], r1[:], per_expert(table("first")), ALU.mult))
                do(nc.vector.reduce_max(rsmall[:], r1[:], AX.X))
                do(nc.vector.tensor_tensor(hot[:], r1[:], per_row(rsmall[:]), ALU.is_equal))
                do(nc.vector.tensor_tensor(hot[:], hot[:], per_row(table("valid")), ALU.mult))
                nc.vector.reduce_sum(mine[:], hot[:].rearrange("p t e -> p e t"), AX.X).then_inc(s("hot" + L), 1)
                ct = cmp[:].rearrange("p (t e u) -> p t e u", e=EXPERTS, u=TILES)
                for i in range(TILES):
                    last = do.post(nc.vector.tensor_tensor(
                        ct[:, i], hot[:].rearrange("p u e -> p e u"),
                        table("tiles_before")[:, i * TILES:(i + 1) * TILES].rearrange("p (o u) -> p o u", o=1).to_broadcast([P, EXPERTS, TILES]),
                        ALU.mult))
                do.until(last)
                last = do.post(nc.vector.reduce_sum(rank[:], ct, AX.X))
                if layer == 0:
                    do(nc.vector.tensor_tensor(tokstat[:, :, 0], rstd[:], rstd[:], ALU.mult))
                    do(nc.vector.tensor_tensor(tokstat[:, :, 1], tokstat[:, :, 0], mv[:, :, 1], ALU.mult))
                    nc.vector.tensor_scalar(veps[:], tokstat[:, :, 1], EPS, None, ALU.add).then_inc(s("veps_ready"), 1)
                dve.wait_ge(s("ranks" + L), 1)
                do.until(last)
                c5 = cmp[:, 0:EXPERTS * TILES].rearrange("p (e t) -> p e t", t=TILES)
                do(nc.vector.tensor_tensor(c5, bank(6)[:, 0:EXPERTS].rearrange("p (e o) -> p e o", o=1).to_broadcast([P, EXPERTS, TILES]),
                                           table("full").rearrange("p (o t) -> p o t", o=1).to_broadcast([P, EXPERTS, TILES]), ALU.is_gt))
                ranked_in = do.post(nc.vector.tensor_tensor(rank[:], rank[:], per_expert(bank(5)[:, 0:EXPERTS]), ALU.add))
                do(nc.vector.reduce_sum(nwin[:], c5, AX.X))
                c8 = cmp[:, EXPERTS * TILES:EXPERTS * (TILES + EXPERTS)].rearrange("p (e f) -> p e f", f=EXPERTS)
                do(nc.vector.tensor_tensor(c8, table("upto").rearrange("p (e f) -> p e f", f=EXPERTS),
                                           nwin[:].rearrange("p (o f) -> p o f", o=1).to_broadcast([P, EXPERTS, EXPERTS]), ALU.mult))
                do(nc.vector.reduce_sum(wend[:], c8, AX.X))
                do(nc.vector.tensor_tensor(wbeg[:], wend[:], nwin[:], ALU.subtract))
                do.until(ranked_in)
                do(nc.vector.scalar_tensor_tensor(out=rank[:], in0=per_expert(wbeg[:]), scalar=float(WIN), in1=rank[:],
                                                  op0=ALU.mult, op1=ALU.add))
                do(nc.vector.tensor_tensor(rank[:], rank[:], hot[:], ALU.mult))
                do(nc.vector.reduce_sum(slot_f[:], rank[:], AX.X))
                nc.vector.tensor_tensor(slot_i[:], slot_f[:], table("pad_slot"), ALU.add).then_inc(s("slots" + L), 1)
                cw = cmp[:, 0:(WINDOWS + 1) * EXPERTS].rearrange("p (w e) -> p w e", e=EXPERTS)
                do(nc.vector.tensor_tensor(cw, wend[:].rearrange("p (o e) -> p o e", o=1).to_broadcast([P, WINDOWS + 1, EXPERTS]),
                                           table("window").rearrange("p (w o) -> p w o", o=1).to_broadcast([P, WINDOWS + 1, EXPERTS]), ALU.is_le))
                do(nc.vector.reduce_sum(winexp[:, 0:WINDOWS + 1], cw, AX.X))
                clipped = do.post(nc.vector.tensor_scalar(winexp_i[:, 0:WINDOWS + 1], winexp[:, 0:WINDOWS + 1], float(EXPERTS - 1), None, ALU.min))
                count = wend[:, EXPERTS - 1:EXPERTS]
                do.post(nc.vector.tensor_copy(winexp_i[:, WINDOWS + 1:WINDOWS + 2], count))
                do(nc.vector.tensor_scalar(cmp[:, 0:1], count, 0.5, 0.25, ALU.mult, ALU.add))
                do(nc.vector.tensor_scalar(winexp[:, WINDOWS + 2:WINDOWS + 3], cmp[:, 0:1], HALF_EVEN, HALF_EVEN, ALU.add, ALU.subtract))
                do.post(nc.vector.tensor_copy(winexp_i[:, WINDOWS + 2:WINDOWS + 3], winexp[:, WINDOWS + 2:WINDOWS + 3]))
                nc.vector.tensor_tensor(winexp_i[:, WINDOWS + 3:WINDOWS + 4], count,
                                        winexp[:, WINDOWS + 2:WINDOWS + 3], ALU.subtract).then_inc(s("table" + L), 1)
                if layer == 0:
                    dve.wait_ge(s("gate_exp" + L), 1)
                    do(nc.vector.tensor_scalar(gate[:], gate[:], 1.0, None, ALU.add))
                else:
                    do(nc.vector.reduce_sum(gate[:], lexp[:], AX.X))
                do(nc.vector.reciprocal(gate[:], gate[:]))

            def route_scalar(act):
                act.wait_ge(s("gate_in" + L), 1)
                if layer == 0:
                    nc.scalar.activation(gate[:], gate[:], ACT.Exp, scale=-1.0).then_inc(s("gate_exp" + L), 1)
                    act.wait_ge(s("rstd_ready"), NORMS + 2)
                    for i in range(TILES):
                        nc.scalar.activation(xd[:, i, :], x[:, i, :], ACT.Copy, scale=rstd[:, i:i + 1]).then_inc(s("inner_normed"), 1)
                else:
                    nc.scalar.activation(lexp[:], lexp[:], ACT.Exp).then_inc(s("gate_exp" + L), 1)

            def dispatch_gpsimd(pool):
                rows = xd if layer == 0 else x
                pool.wait_ge(s("slots_zeroed"), ZEROED)
                pool.wait_ge(s("slots" + L), 1)
                if layer == 0:
                    pool.wait_ge(s("inner_normed"), TILES)
                for i in range(TILES):
                    pool.indirect_dma_start(out=slots_in[:, :], out_offset=bass.IndirectOffsetOnAxis(ap=slot_i[:, i:i + 1], axis=0),
                                            in_=rows[:, i, :], in_offset=None).then_inc(s("dispatched" + L), 16)

                def store(u, b):
                    pool.wait_ge(s(f"z_ready{b}" + L), u + 1)
                    pool.dma_start(slots_out[bass.ds((u * 2 + b) * WIN, WIN), :], zw[:, b, :]).then_inc(s(f"z_stored{b}" + L), 16)
                windows(pool, store)
                pairs, seconds = load_pairs(pool), load_seconds(pool)
                pool.wait_ge(s("z_stored0" + L), pairs * 16)
                pool.wait_ge(s("z_stored1" + L), seconds * 16)
                nc.gpsimd.tensor_tensor(stored[:], table("ones")[0:1, 0:1], table("ones")[0:1, 0:1], ALU.mult).then_inc(s("all_stored"), 1)
                pool.wait_ge(s("all_stored"), layer + 1)
                for i in range(TILES):
                    pool.indirect_dma_start(out=z[:, i, :], out_offset=None, in_=slots_out[:, :],
                                            in_offset=bass.IndirectOffsetOnAxis(ap=slot_i[:, i:i + 1], axis=0)).then_inc(s(f"z_back{i}"), 16)

            def following(u, b):
                return (u, 1) if b == 0 else (u + 1, 0)

            def is_first(u):
                return isinstance(u, int) and u == 0

            def weights_sync(sp):
                def expert_of(u, b):
                    return sp.value_load(winexp_i[0:1, bass.ds(u * 2 + b, 1)], min_val=0, max_val=EXPERTS - 1)

                def load_rows(u, b):
                    if not is_first(u):
                        sp.wait_ge(s(f"xw_used{b}" + L), u)
                    sp.dma_start(xw[:, b, :], slots_in[bass.ds((u * 2 + b) * WIN, WIN), :]).then_inc(s(f"xw_in{b}" + L), 16)
                    if layer == 0:
                        e = expert_of(u, b)
                        if not is_first(u):
                            sp.wait_ge(s(f"xwT_ready{b}" + L), u)
                        sp.dma_start(par_s[:, b, 0:2 * DC], par_0[bass.ds(e, 1), :, 0:2 * DC].rearrange("e p n -> (e p) n")).then_inc(s(f"xw_in{b}" + L), 16)

                def load_w1(u, b, e):
                    if not is_first(u):
                        sp.wait_ge(s("hid_ps" + L), (u * 2 + b - 1) * FC)
                    sp.dma_start(w1_s[:, b, 0:DC * F1], w1[bass.ds(e, 1), :, :].rearrange("e p n -> (e p) n")).then_inc(s(f"w1_in{b}" + L), 16)

                def load_w2(u, b, e):
                    if not is_first(u):
                        sp.wait_ge(s(f"w2_used{b}" + L), u)
                    if layer == 0:
                        sp.dma_start(par_s[:, b, 2 * DC:], par_0[bass.ds(e, 1), :, 2 * DC:].rearrange("e p n -> (e p) n")).then_inc(s(f"b1_in{b}" + L), 16)
                    sp.dma_start(w2_s[:, b, :, :].rearrange("p f n -> p (f n)"), w2[bass.ds(e, 1), :, :].rearrange("e p n -> (e p) n")).then_inc(s(f"w2_in{b}" + L), 16)
                    if layer == 0:
                        if not is_first(u):
                            sp.wait_ge(s(f"z_ready{b}" + L), u)
                        sp.dma_start(b2_s[:, b, :], b2_0[bass.ds(e, 1), :].to_broadcast([P, D])).then_inc(s(f"b2_in{b}" + L), 16)

                def before():
                    e = expert_of(0, 0)
                    load_w1(0, 0, e)
                    load_w2(0, 0, e)
                    load_w1(0, 1, expert_of(0, 1))
                    sp.wait_ge(s("dispatched" + L), 16 * TILES)
                    load_rows(0, 0)

                def load(u, b):
                    load_rows(*following(u, b))
                    if is_first(u) and b == 0:
                        return
                    e = expert_of(u, b)
                    if not is_first(u):
                        load_w1(u, b, e)
                    load_w2(u, b, e)
                windows(sp, load, before)

            def turned_rows(b):
                return bank(7 * b)[:, 0:DC * P]

            ROWS_IN = 32 if layer == 0 else 16

            def expert_tensor(pe):
                def turn_rows(u, b):
                    pe.wait_ge(s(f"xw_in{b}" + L), u * ROWS_IN + ROWS_IN)
                    if not is_first(u):
                        pe.wait_ge(s(f"xwT_ready{b}" + L), u)
                    for c in range(DC):
                        last = nc.tensor.transpose(turned_rows(b)[:, c * P:(c + 1) * P], xw[:, b, c * P:(c + 1) * P], ident)
                    last.then_inc(s(f"xw_used{b}" + L), 1)

                def window(u, b):
                    w = u * 2 + b
                    pe.wait_ge(s(f"w1_in{b}" + L), u * 16 + 16)
                    pe.wait_ge(s(f"xwT_ready{b}" + L), u + 1)
                    w1v = w1_s[:, b, 0:DC * F1].rearrange("p (k f) -> p k f", f=F1)
                    for f in range(FC):
                        reused(pe, s("hid_ready" + L), w * FC + max(f - 3, 0))
                        for part in range(1 + layer):
                            for k in range(DC):
                                last = nc.tensor.matmul(bank(1 + f % 4)[:, part * WIN:(part + 1) * WIN],
                                                        w1v[:, k, part * FF + f * P:part * FF + (f + 1) * P], xwT[:, b, k, :],
                                                        start=(k == 0), stop=(k == DC - 1))
                        last.then_inc(s("hid_ps" + L), 1)
                    turn_rows(*following(u, b))
                    pe.wait_ge(s(f"w2_in{b}" + L), u * 16 + 16)
                    reused(pe, s(f"z_ready{b}" + L), u)
                    for f in range(FC):
                        pe.wait_ge(s("hid_ready" + L), w * FC + f + 1)
                        last = nc.tensor.matmul(bank(5 + b)[:, 0:D], hid[:, f, :], w2_s[:, b, f, :], start=(f == 0), stop=(f == FC - 1))
                    last.then_inc(s(f"w2_used{b}" + L), 1)
                windows(pe, window, lambda: turn_rows(0, 0))

            def expert_vector(dve, do):
                def rows_out(u, b):
                    dve.wait_ge(s(f"xw_used{b}" + L), u + 1)
                    if not is_first(u):
                        dve.wait_ge(s("hid_ps" + L), (u * 2 + b - 1) * FC)
                    turned = turned_rows(b).rearrange("p (c n) -> p c n", n=P)
                    if layer == 0:
                        dve.wait_ge(s(f"xw_in{b}" + L), u * ROWS_IN + ROWS_IN)
                        for c in range(DC):
                            last = nc.vector.tensor_scalar(xwT[:, b, c, :], turned[:, c, :], par_s[:, b, c:c + 1], par_s[:, b, DC + c:DC + c + 1],
                                                           ALU.mult, ALU.add)
                    else:
                        last = nc.vector.tensor_copy(xwT[:, b], turned)
                    last.then_inc(s(f"xwT_ready{b}" + L), 1)

                def window(u, b):
                    w = u * 2 + b
                    if layer == 1:
                        for f in range(FC):
                            dve.wait_ge(s("act_ready" + L), w * FC + f + 1)
                            nc.vector.tensor_tensor(hid[:, f, :], bank(1 + f % 4)[:, WIN:2 * WIN], act_a[:, f % 2, :],
                                                    ALU.mult).then_inc(s("hid_ready" + L), 1)
                    rows_out(*following(u, b))
                    dve.wait_ge(s(f"w2_used{b}" + L), u + 1)
                    reused(dve, s(f"z_stored{b}" + L), u * 16)
                    if layer == 0:
                        dve.wait_ge(s(f"b2_in{b}" + L), u * 16 + 16)
                        nc.vector.tensor_tensor(zw[:, b, :], bank(5 + b)[:, 0:D], b2_s[:, b, :], ALU.add).then_inc(s(f"z_ready{b}" + L), 1)
                    else:
                        nc.vector.tensor_copy(zw[:, b, :], bank(5 + b)[:, 0:D]).then_inc(s(f"z_ready{b}" + L), 1)
                windows(dve, window, lambda: rows_out(0, 0))

            def expert_scalar(act):
                def window(u, b):
                    w = u * 2 + b
                    if layer == 0:
                        act.wait_ge(s(f"b1_in{b}" + L), u * 16 + 16)
                    for f in range(FC):
                        act.wait_ge(s("hid_ps" + L), w * FC + f + 1)
                        src = bank(1 + f % 4)[:, 0:WIN]
                        if layer == 0:
                            if f == 0:
                                reused(act, s(f"w2_used{1 - b}" + L), u + b)
                            last = nc.scalar.activation(hid[:, f, :], src, ACT.Relu, bias=par_s[:, b, 2 * DC + f:2 * DC + f + 1])
                            last.then_inc(s("hid_ready" + L), 1)
                        else:
                            reused(act, s("hid_ready" + L), w * FC + max(f - 1, 0))
                            nc.scalar.activation(act_a[:, f % 2, :], src, ACT.Silu).then_inc(s("act_ready" + L), 1)
                windows(act, window)

            return logits_tensor, route_vector, route_scalar, dispatch_gpsimd, weights_sync, expert_tensor, expert_vector, expert_scalar

        moe0 = moe(0)
        moe1 = moe(1)

        def quant_weights_scalar(act):
            act.wait_ge(s("in_attn1"), 16)
            for g in range(4):
                last = nc.scalar.activation(z[:, g, :].rearrange("p (k n) -> p k n", k=DC)[:, :, 0:P], wa1_s[:, :, g, 0:P], ACT.Abs,
                                            accum_out=stat2[:, g, 0:1])
            return last

        def quant_weights_vector(dve, do):
            dve.wait_ge(s("in_attn1"), 16)
            ab = wscaleabs().rearrange("p (k g n) -> p k g n", k=DC, g=4)
            for g in range(4):
                do(nc.vector.tensor_reduce(wsum[:, g:g + 1], wa1_s[:, :, g, :], AX.XY, ALU.add, apply_absolute_value=True))
            nc.vector.tensor_copy(wscale[:], wsum[:]).then_inc(s("wsum_ready"), 1)
            dve.wait_ge(s("wsum_ps"), 1)
            do(nc.vector.tensor_scalar(wmean[:], bank(7)[:, 0:4], 1.0 / (D * D), 1e-5, ALU.mult, ALU.max))
            do(nc.vector.reciprocal(wscale[:], wmean[:]))
            do(nc.vector.tensor_tensor(qk_scale[:], wmean[:, 0:1], wmean[:, 1:2], ALU.mult))
            do(nc.vector.tensor_scalar(qk_scale[:], qk_scale[:], SCALE, None, ALU.mult))
            for g in range(4):
                dst = ab[:, :, g, :]
                do(nc.vector.tensor_scalar(dst, wa1_s[:, :, g, :], wscale[:, g:g + 1], HALF_EVEN, ALU.mult, ALU.add))
                do(nc.vector.tensor_scalar(dst, dst, HALF_EVEN, 1.0, ALU.subtract, ALU.min))
                last = nc.vector.tensor_scalar(wq1_s[:, :, g, :], dst, -1.0, None, ALU.max)
                if g < 3:
                    do(last)
            last.then_inc(s("wq1_ready"), 1)

        def wscaleabs():
            return wide[:, 0:DC * 4 * D]

        def quant_weights_tensor(pe):
            pe.wait_ge(s("wsum_ready"), 1)
            nc.tensor.matmul(bank(7)[:, 0:4], table("ones"), wscale[:], start=True, stop=True).then_inc(s("wsum_ps"), 1)

        def quant_vector(dve, do, src, tag, power):
            for i in range(TILES):
                do(nc.vector.bn_stats(stats[:, i, 0, :], src[:, i, :]))
            for i in range(TILES):
                do(nc.vector.bn_aggr(mv[:, i, :], stats[:, i, 0:1, :]))
            do(nc.vector.tensor_copy(stat2[:, :, 0:2], mv[:]))
            nc.vector.tensor_tensor(stat2[:, :, 2], mv[:, :, 0], mv[:, :, 0], ALU.mult).then_inc(s("stat" + tag), 1)
            dve.wait_ge(s("img_ps" + tag), 1)
            do(nc.vector.tensor_scalar(img[:, 0:3], bank(6)[0:IMAGES, 0:3], 1.0 / SEQ, None, ALU.mult))
            do(nc.vector.tensor_tensor(img[:, 3:4], img[:, 0:1], img[:, 0:1], ALU.mult))
            do(nc.vector.tensor_tensor(img[:, 4:5], img[:, 1:2], img[:, 2:3], ALU.add))
            do(nc.vector.tensor_tensor(img[:, 4:5], img[:, 4:5], img[:, 3:4], ALU.subtract))
            do(nc.vector.tensor_scalar(img[:, 4:5], img[:, 4:5], 0.0, None, ALU.max))
            nc.vector.tensor_copy(img[:, 1:2], img[:, 4:5]).then_inc(s("img" + tag), 1)
            dve.wait_ge(s("tok_ps" + tag), 1)
            do(nc.vector.tensor_copy(tokstat[:], bank(7)[:, 0:2 * TILES].rearrange("p (t a) -> p t a", a=2)))
            nc.vector.tensor_scalar(veps[:], tokstat[:, :, 1], EPS, None, ALU.add).then_inc(s("veps_ready"), 1)
            dve.wait_ge(s("rstd_ready"), power)
            for i in range(TILES):
                do(nc.vector.tensor_scalar(z[:, i, :], src[:, i, :], tokstat[:, i, 0:1], rstd[:, i:i + 1], ALU.subtract, ALU.mult))
            do(nc.vector.tensor_reduce(amax[:], z, AX.X, ALU.max, apply_absolute_value=True))
            do(nc.vector.tensor_scalar(amax[:], amax[:], 1e-5, None, ALU.max))
            do(nc.vector.tensor_scalar(inv_s[:], amax[:], 1.0 / 127.0, None, ALU.mult))
            do(nc.vector.reciprocal(act_s[:], amax[:]))
            do(nc.vector.tensor_scalar(act_s[:], act_s[:], 127.0, None, ALU.mult))
            for i in range(TILES):
                do(nc.vector.tensor_scalar(z[:, i, :], z[:, i, :], act_s[:, i:i + 1], HALF_EVEN, ALU.mult, ALU.add))
                do(nc.vector.tensor_scalar(z[:, i, :], z[:, i, :], HALF_EVEN, 127.0, ALU.subtract, ALU.min))
                last = nc.vector.tensor_scalar(xqb[:, i, :], z[:, i, :], -128.0, None, ALU.max)
                if i < TILES - 1:
                    do(last)
            last.then_inc(s("xq" + tag), 1)

        def quant_tensor(pe, tag):
            pe.wait_ge(s("stat" + tag), 1)
            for i in range(TILES):
                last = nc.tensor.matmul(bank(6)[0:IMAGES, 0:3], table("of_image")[:, i * IMAGES:(i + 1) * IMAGES], stat2[:, i, :],
                                        start=(i == 0), stop=(i == TILES - 1))
            last.then_inc(s("img_ps" + tag), 1)
            pe.wait_ge(s("img" + tag), 1)
            for i in range(TILES):
                last = nc.tensor.matmul(bank(7)[:, 2 * i:2 * i + 2], image_of[:, i * P:(i + 1) * P], img[:, 0:2],
                                        start=True, stop=True)
            last.then_inc(s("tok_ps" + tag), 1)
            pe.wait_ge(s("xq" + tag), 1)
            pe.wait_ge(s("identb_ready"), 1)
            for c in range(DC):
                for i in range(TILES):
                    last = nc.tensor.transpose(turned_bf16(c)[:, i * P:(i + 1) * P], xqb[:, i, c * P:(c + 1) * P], identb[:])
                last.then_inc(s("xqT_ps" + tag), 1)

        def turned_bf16(c):
            return psum[:, 4 + c, :].bitcast(BF16)[:, 0:ROWS]

        def quant_scalar(act, tag):
            for c in range(DC):
                act.wait_ge(s("xqT_ps" + tag), c + 1)
                nc.scalar.activation(xTb[:, c, :], turned_bf16(c), ACT.Copy).then_inc(s("xqT" + tag), 1)

        block = ctx.enter_context(nc.Block())

        @block.sync
        def _(sp):
            loads(sp)
            moe0[4](sp)
            moe1[4](sp)
            for i in range(TILES):
                n = min(P, TOKENS - i * P)
                sp.wait_ge(s("out_ready"), i + 1)
                sp.dma_start(out[i * P:i * P + n, :], h[0:n, i, :]).then_inc(s("out_stored"), 16)
            sp.wait_ge(s("out_stored"), 16 * TILES)

        @block.gpsimd
        def _(pool):
            powers = [NORMS]

            def power():
                pool.wait_ge(s("veps_ready"), powers[0] + 1)
                nc.gpsimd.tensor_tensor(rstd[:], veps[:], table("minus_half"), ALU.pow).then_inc(s("rstd_ready"), 1)
                powers[0] += 1

            embed_gpsimd(pool)
            pool.wait_ge(s("in_const"), 32)
            attn0[2](pool)
            power()
            power()
            moe0[3](pool)
            power()
            power()
            attn1[2](pool)
            power()
            power()
            moe1[3](pool)

        @block.scalar
        def _(act):
            do = Chain(act, "act_own")
            embed_scalar(act, do)
            turn_scalar(act, xT, "turn_a0")
            attn0[3](act)
            turn_scalar(act, xT, "turned_m0")
            moe0[2](act)
            moe0[7](act)
            quant_scalar(act, "_x1")
            attn1[3](act)
            quant_scalar(act, "_o1")
            turn_scalar(act, xT, "turned_m1")
            moe1[2](act)
            moe1[7](act)

        @block.tensor
        def _(pe):
            embed_tensor(pe)
            pe.wait_ge(s("turn_a0"), TILES)
            pe.wait_ge(s("in_attn0"), 64)
            attn0[0](pe)
            turn_tensor(pe, x, "x_moe0", "turned_m0")
            moe0[0](pe)
            quant_weights_tensor(pe)
            moe0[5](pe)
            quant_tensor(pe, "_x1")
            pe.wait_ge(s("spread"), 1)
            for i in range(TILES):
                last = nc.tensor.transpose(two_banks(0)[:, i * P:(i + 1) * P], spread[:, i, :], ident)
            last.then_inc(s("invT_ps"), 1)
            pe.wait_ge(s("invT_ready"), 1)
            pe.wait_ge(s("xqT_x1"), DC)
            attn1[0](pe)
            quant_tensor(pe, "_o1")
            pe.wait_ge(s("xqT_o1"), DC)
            for i in range(TILES):
                for c in range(DC):
                    last = nc.tensor.matmul(tile_bank(i), xTb[:, c, i * P:(i + 1) * P], wq1_s[:, c, 3, :], start=(c == 0), stop=(c == DC - 1))
                last.then_inc(s("y_attn1"), 1)
            turn_tensor(pe, x, "x_moe1", "turned_m1")
            moe1[0](pe)
            moe1[5](pe)

        @block.vector
        def _(dve):
            do = Chain(dve, "dve_own")
            embed_vector(dve, do)
            attn0[1](dve, do)
            def add_projection(i):
                dve.wait_ge(s("finished_a0"), i + 1)
                return nc.vector.tensor_tensor(h[:, i, :], tile_bank(i), h[:, i, :], ALU.add)
            norm_vector(dve, do, h, x, "x_moe0", NORMS + 1, add_projection)
            moe0[1](dve, do)
            quant_weights_vector(dve, do)
            moe0[6](dve, do)
            for i in range(TILES):
                last = do.post(nc.vector.tensor_tensor(h[:, i, :], h[:, i, :], x[:, i, :], ALU.add))
            do.until(last)

            def add_expert(back):
                def add(i):
                    dve.wait_ge(s(f"z_back{i}"), back)
                    return nc.vector.scalar_tensor_tensor(out=h[:, i, :], in0=z[:, i, :], scalar=gate[:, i:i + 1], in1=h[:, i, :],
                                                          op0=ALU.mult, op1=ALU.add)
                return add
            norm_vector(dve, do, h, x, "x_attn1", NORMS + 3, add_expert(16))
            dve.wait_ge(s("x_attn1"), TILES)
            quant_vector(dve, do, x, "_x1", NORMS + 4)
            do(nc.vector.tensor_copy(veps[:], inv_s[:]))
            nc.vector.tensor_copy(spread[:], inv_s[:].rearrange("p (t o) -> p t o", o=1).to_broadcast([P, TILES, P])).then_inc(s("spread"), 1)
            dve.wait_ge(s("invT_ps"), 1)
            nc.vector.tensor_copy(invT[:], two_banks(0)).then_inc(s("invT_ready"), 1)
            dve.wait_ge(s("invT_ready"), 1)
            attn1[1](dve, do)
            for i in range(TILES):
                dve.wait_ge(s("finished_a1"), i + 1)
                last = do.post(nc.vector.tensor_copy(xd[:, i, :], tile_bank(i)))
            do.until(last)
            quant_vector(dve, do, xd, "_o1", NORMS + 5)
            do(nc.vector.tensor_scalar(rsmall[:], inv_s[:], wmean[:, 3:4], None, ALU.mult))

            def add_projection1(i):
                dve.wait_ge(s("y_attn1"), i + 1)
                return nc.vector.scalar_tensor_tensor(out=h[:, i, :], in0=tile_bank(i), scalar=rsmall[:, i:i + 1], in1=h[:, i, :],
                                                      op0=ALU.mult, op1=ALU.add)
            norm_vector(dve, do, h, x, "x_moe1", NORMS + 6, add_projection1)
            moe1[1](dve, do)
            moe1[6](dve, do)
            for i in range(TILES):
                dve.wait_ge(s(f"z_back{i}"), 32)
                nc.vector.scalar_tensor_tensor(out=h[:, i, :], in0=z[:, i, :], scalar=gate[:, i:i + 1], in1=h[:, i, :],
                                               op0=ALU.mult, op1=ALU.add).then_inc(s("out_ready"), 1)


def kernel(**inputs):
    import concourse.bacc as bacc
    from concourse.bass_utils import run_bass_kernel_spmd

    a = {k: np.asarray(v) for k, v in inputs.items()}

    def rows(w):
        return w.reshape(w.shape[0] // P, P, *w.shape[1:]).swapaxes(0, 1)

    def col(v):
        return v.reshape(-1, P).T

    patches = a["x"].reshape(IMAGES, CHANNELS, GRID, PATCH, GRID, PATCH).transpose(0, 2, 4, 3, 5, 1).reshape(IMAGES, SEQ - 1, PD)
    xp = np.zeros((ROWS, PD), np.float32)
    xp[:TOKENS].reshape(IMAGES, SEQ, PD)[:, 1:] = patches
    partner = np.arange(D) ^ 1
    wq, wk, wv = a["L0_attn_Wq"], a["L0_attn_Wk"], a["L0_attn_Wv"]
    bq, bk, bv = a["L0_attn_bq"], a["L0_attn_bk"], a["L0_attn_bv"]
    e1 = a["L0_ffn_w1"].transpose(0, 2, 1).reshape(EXPERTS, DC, P, FF).transpose(0, 2, 1, 3)
    e2 = a["L0_ffn_w2"].transpose(0, 2, 1).reshape(EXPERTS, FC, P, D).transpose(0, 2, 1, 3)
    f1 = a["L1_ffn_w1"].reshape(EXPERTS, DC, P, 2 * FF).transpose(0, 2, 1, 3)
    f2 = a["L1_ffn_w2"].reshape(EXPERTS, FC, P, D).transpose(0, 2, 1, 3)
    by_expert = lambda v: v.reshape(EXPERTS, -1, P).transpose(0, 2, 1)
    arrays = {
        "xp": rows(xp),
        "cls_ln2b": np.stack([a["cls_tok"].reshape(D), a["L0_tok_ln2_b"]]),
        "Wp": rows(a["L0_tok_Wp"]),
        "ln1": np.stack([col(a["L0_tok_ln1_g"]), col(a["L0_tok_ln1_b"])], 1),
        "bp": a["L0_tok_bp"],
        "ln2_g": a["L0_tok_ln2_g"],
        "const": CONST,
        "const_rows": CONST_ROWS,
        "wa0": np.stack([rows(w.T) for w in (wq, wk, wq[partner], wk[partner], wv)], 2),
        "ba0": np.stack([col(b) for b in (bq, bk, bq[partner], bk[partner], bv)], 1),
        "wo0": rows(a["L0_attn_Wo"].T),
        "bo0": a["L0_attn_bo"],
        "cent": rows(a["L0_ffn_centroids"].T),
        "w1_0": e1.reshape(EXPERTS, P, DC * FF),
        "w2_0": e2.reshape(EXPERTS, P, FC * D),
        "par_0": np.concatenate([by_expert(a["L0_ffn_ln_g"]), by_expert(a["L0_ffn_ln_b"]), by_expert(a["L0_ffn_b1"])], 2),
        "b2_0": a["L0_ffn_b2"],
        "wa1": np.stack([rows(a[f"L1_attn_w_{n}"].T) for n in "qkvo"], 2),
        "router": rows(a["L1_ffn_router_w"]),
        "router_b": a["L1_ffn_router_b"],
        "w1_1": f1.reshape(EXPERTS, P, DC * 2 * FF),
        "w2_1": f2.reshape(EXPERTS, P, FC * D),
    }
    nc = bacc.Bacc("TRN2", target_bir_lowering=False, num_devices=1)
    args = {}
    for name, array in arrays.items():
        array = np.ascontiguousarray(array)
        arrays[name] = array
        args[name] = nc.dram_tensor(name, array.shape, mybir.dt.from_np(array.dtype), kind="ExternalInput").ap()
    out = nc.dram_tensor("out", (TOKENS, D), F32, kind="ExternalOutput").ap()
    vit_tower(nc, *args.values(), out)
    got = run_bass_kernel_spmd(nc, [arrays], core_ids=[0])
    return got.results[0]["out"].reshape(IMAGES, SEQ, D)
```

```python
from contextlib import ExitStack

import numpy as np

import concourse.bass as bass
from concourse import mybir

P = 128
IMAGES, CHANNELS, SIDE, PATCH = 16, 3, 96, 16
GRID = SIDE // PATCH
SEQ = GRID * GRID + 1
TOKENS = IMAGES * SEQ
TILES = -(-TOKENS // P)
ROWS = TILES * P
D = 256
DC = D // P
PD = PATCH * PATCH * CHANNELS
PC = PD // P
HEADS, HD = 16, 16
PAIRS = IMAGES // 2
PW = 2 * SEQ
HALF = TOKENS // 2
QPAD = 64
EXPERTS, FF = 8, 1024
FC = FF // P
WIN = P
WINDOWS = (TOKENS - EXPERTS) // WIN + EXPERTS
MIN_WINDOWS = -(-TOKENS // WIN)
DUMP = WINDOWS * WIN
SLOTS = DUMP + P
EPS = 1e-5
SCALE = HD ** -0.5
NEG = -1e30
WARM_MATMULS = 16
HALF_EVEN = 12582912.0

F32 = mybir.dt.float32
BF16 = mybir.dt.bfloat16
I32 = mybir.dt.int32
ALU = mybir.AluOpType
ACT = mybir.ActivationFunctionType
AX = mybir.AxisListType


def constant_columns():
    p = np.arange(P)[:, None]
    token = np.arange(ROWS).reshape(TILES, P).T
    inv_freq = 1.0 / 10000.0 ** (np.arange(0, HD, 2, dtype=np.float32) / HD)
    angle = np.outer(np.arange(SEQ, dtype=np.float32), inv_freq.astype(np.float32))
    freq = (np.arange(P) % HD) // 2
    sign = np.where(np.arange(P) % 2 == 0, -1.0, 1.0)[:, None]
    q = np.arange(P) % QPAD
    causal = np.where(np.arange(SEQ)[None, :] > q[:, None], NEG, 0.0)
    valid = (token < TOKENS)
    image = np.where(valid, token // SEQ, -1)
    is_patch = valid & (token % SEQ != 0)
    flat = np.arange(ROWS)
    tables = {
        "ident": np.eye(P),
        "minus_half": np.full((P, TILES), -0.5),
        "cos": np.cos(angle).T[freq],
        "sin": sign * np.sin(angle).T[freq],
        "causal": np.tile(causal, (1, 8)),
        "head4": ((p // HD) % 4 == np.arange(4)[None, :]),
        "head2": ((p // SEQ) == (np.arange(D)[None, :] // HD) % 2),
        "of_image": (image[:, :, None] == np.arange(IMAGES)).reshape(P, -1),
        "is_patch": is_patch,
        "valid": valid,
        "pad_slot": np.where(valid, 0, DUMP + token - TOKENS),
        "earlier": np.triu(np.ones((P, P)), 1),
        "ones": np.ones((P, P)),
        "first": np.broadcast_to(EXPERTS - np.arange(EXPERTS), (P, EXPERTS)),
        "full": np.broadcast_to(WIN * np.arange(TILES), (P, TILES)),
        "upto": np.broadcast_to(np.tril(np.ones((EXPERTS, EXPERTS))).reshape(-1), (P, EXPERTS * EXPERTS)),
        "slot": np.broadcast_to(np.arange(2 * WIN), (P, 2 * WIN)),
        "window": np.broadcast_to(np.arange(WINDOWS + 1), (P, WINDOWS + 1)),
        "tiles_before": np.broadcast_to(np.tril(np.ones((TILES, TILES)), -1).reshape(-1), (P, TILES * TILES)),
    }
    row_tables = {
        "image_of": (flat // SEQ)[None, :] == np.arange(IMAGES)[:, None],
        "patch_row": np.pad(np.stack([(flat % SEQ == 0), (flat % SEQ != 0)]), ((0, IMAGES - 2), (0, 0))),
    }
    where, at = {}, 0
    for name, table in tables.items():
        where[name] = (at, at + table.shape[1])
        at += table.shape[1]
    join = lambda ts: np.concatenate([np.asarray(t, np.float32) for t in ts.values()], 1)
    return join(tables), join(row_tables), where


CONST, CONST_ROWS, CONST_AT = constant_columns()
CONST_FIRST = P + TILES


def vit_tower(nc, xp, cls_ln2b, Wp, ln1, bp, ln2_g, const, const_rows, wa0, ba0, wo0, bo0, cent, w1_0, w2_0, par_0, b2_0,
              wa1, router, router_b, w1_1, w2_1, out):
    with ExitStack() as ctx:
        def sb(name, shape, dt=F32):
            return ctx.enter_context(nc.sbuf_tensor(name, shape, dt))

        def sem(name):
            return ctx.enter_context(nc.semaphore(name))

        slots_in = nc.dram_tensor("slots_in", [SLOTS, D], F32)
        slots_out = nc.dram_tensor("slots_out", [SLOTS, D], F32)

        cst = sb("cst", [P, CONST.shape[1]])

        def table(name, rows=P):
            a, b = CONST_AT[name]
            return cst[0:rows, a:b]

        cst_rows = sb("cst_rows", CONST_ROWS.shape)
        image_of, patch_row = cst_rows[:, 0:ROWS], cst_rows[0:2, ROWS:2 * ROWS]

        ident = table("ident")
        identb = sb("identb", [P, P], BF16)
        causal_b = sb("causal_b", [P, 8 * SEQ], BF16)
        patches = sb("patches", [P, TILES, PD])
        wide = sb("wide", [P, IMAGES * D])
        patchT = wide[:, 0:PC * ROWS].rearrange("p (c n) -> p c n", n=ROWS)
        vD = wide[0:PW].rearrange("p (i d) -> p i d", d=D)
        wp_s = sb("wp_s", [P, PC, D])
        ln1_s = sb("ln1_s", [P, 2, PC])
        bp_s = sb("bp_s", [P, D])
        ln2g_s = sb("ln2g_s", [P, D])
        cls_s = sb("cls_s", [2, D])
        wa0_s = sb("wa0_s", [P, DC, 3, D])
        ba0_s = sb("ba0_s", [P, 3, DC])
        wo0_s = sb("wo0_s", [P, DC, D])
        bo0_s = sb("bo0_s", [P, D])
        cent_s = sb("cent_s", [P, DC, EXPERTS])
        wa1_s = sb("wa1_s", [P, DC, 4, D])
        wq1_s = sb("wq1_s", [P, DC, 4, D], BF16)
        router_s = sb("router_s", [P, DC, EXPERTS])
        routerb_s = sb("routerb_s", [P, EXPERTS])

        h = sb("h", [P, TILES, D])
        x = sb("x", [P, TILES, D])
        xd_z = sb("xd_z", [P, 2, TILES, D])
        xd, z = xd_z[:, 0], xd_z[:, 1]
        chosen = z
        vT = xd_z[:].rearrange("p a t d -> p (a t d)")[:, 0:DC * IMAGES * 2 * SEQ].rearrange(
            "p (c i o k) -> p c i o k", c=DC, i=IMAGES, o=2)
        xT = sb("xT", [P, DC, ROWS])
        oT = sb("oT", [P, DC, ROWS])
        xqb = sb("xqb", [P, TILES, D], BF16)
        xTb = sb("xTb", [P, DC, ROWS], BF16)
        mv3 = sb("mv3", [P, 3, TILES, 2])
        veps3 = sb("veps3", [P, 3, TILES])
        rstd3 = sb("rstd3", [P, 3, TILES])
        stats = sb("stats", [P, TILES, 3, 6])
        mv = sb("mv", [P, TILES, 2])
        veps = sb("veps", [P, TILES])
        rstd = sb("rstd", [P, TILES])
        stat2 = sb("stat2", [P, TILES, 3])
        img = sb("img", [IMAGES, 8])
        tokstat = sb("tokstat", [P, TILES, 2])
        amax = sb("amax", [P, TILES])
        high = sb("high", [P, TILES])
        low = sb("low", [P, TILES])
        minus_half_even = sb("minus_half_even", [P, 1])
        inv_s = sb("inv_s", [P, TILES])
        act_s = sb("act_s", [P, TILES])
        spread = sb("spread", [P, TILES, P])
        invT = sb("invT", [P, ROWS])
        wsum = sb("wsum", [P, 4])
        wmean = sb("wmean", [P, 4])
        wscale = sb("wscale", [P, 4])
        qk_scale = sb("qk_scale", [P, 1])

        qr, kr = (patches[:].rearrange("p t d -> p (t d)")[:, i * DC * ROWS:(i + 1) * DC * ROWS].rearrange("p (c n) -> p c n", n=ROWS)
                  for i in range(2))
        qW = sb("qW", [P, 2, DC, 2, QPAD])
        kM = sb("kM", [P, 2, DC, 2, 4, SEQ])
        vM = sb("vM", [PW, 2, 2, D])
        sc = sb("sc", [P, 2, 2, 8 * SEQ])
        prob = sb("prob", [P, 2, HEADS, SEQ])
        smax = sb("smax", [P, 2, 2, 8])
        srec = sb("srec", [P, DC * PW])
        pT = sb("pT", [PW, 2, 8, P])

        lg = sb("lg", [P, TILES, EXPERTS])
        lmax = sb("lmax", [P, TILES])
        lexp = sb("lexp", [P, TILES, EXPERTS])
        gate = sb("gate", [P, TILES])
        r1 = sb("r1", [P, TILES, EXPERTS])
        rsmall = sb("rsmall", [P, TILES])
        hot = sb("hot", [P, TILES, EXPERTS])
        mine = sb("mine", [P, EXPERTS])
        rank = sb("rank", [P, TILES, EXPERTS])
        cmp = sb("cmp", [P, TILES * EXPERTS * TILES])
        nwin = sb("nwin", [P, EXPERTS])
        wend = sb("wend", [P, EXPERTS])
        wbeg = sb("wbeg", [P, EXPERTS])
        winexp = sb("winexp", [P, WINDOWS + 4])
        winexp_i = sb("winexp_i", [P, WINDOWS + 4], I32)
        slot_f = sb("slot_f", [P, TILES])
        slot_i = sb("slot_i", [P, TILES], I32)

        zero = sb("zero", [P, D])
        stored = sb("stored", [1, 1])
        w1_s = sb("w1_s", [P, 2, DC * 2 * FF])
        wpg_s = w1_s[:, 0, 0:PC * D].rearrange("p (c n) -> p c n", n=D)
        ln1b_s = w1_s[:, 1, 0:PC * P].rearrange("p (c n) -> p c n", n=P)
        w2_s = sb("w2_s", [P, 2, FC, D])
        par_s = sb("par_s", [P, 2, 2 * DC + FC])
        b2_s = sb("b2_s", [P, 2, D])
        xw = sb("xw", [P, 2, D])
        xwT = sb("xwT", [P, 2, DC, WIN])
        hid = patches[:].rearrange("p t d -> p (t d)")[:, 2 * DC * ROWS:2 * DC * ROWS + FC * WIN].rearrange("p (f n) -> p f n", n=WIN)
        act_a = sb("act_a", [P, 2, WIN])
        zw = sb("zw", [P, 2, D])

        psum = ctx.enter_context(nc.psum_tensor("psum", [P, 8, 512], F32))

        block = None
        S = {}

        def s(name):
            if name not in S:
                S[name] = sem(name)
            return S[name]

        class Chain:

            def __init__(self, eng, name):
                self.eng, self.sem, self.n = eng, s(name), 0

            def __call__(self, ins):
                ins.then_inc(self.sem, 1)
                self.n += 1
                self.eng.wait_ge(self.sem, self.n)

            def post(self, ins):
                ins.then_inc(self.sem, 1)
                self.n += 1
                return self.n

            def until(self, ticket):
                self.eng.wait_ge(self.sem, ticket)

        for name in ("dve_own", "act_own", "pool_own"):
            s(name)

        def loads(sp):
            sp.dma_start(patches[:, 0, :], xp[:, 0, :]).then_inc(s("in_patch0"), 16)
            sp.dma_start(cst[:, 0:CONST_FIRST], const[:, 0:CONST_FIRST]).then_inc(s("in_first"), 16)
            sp.dma_start(patches[:, 1, :], xp[:, 1, :]).then_inc(s("in_patch1"), 16)
            sp.dma_start(ln1_s[:], ln1[:]).then_inc(s("in_embed"), 16)
            sp.dma_start(wp_s[:], Wp[:]).then_inc(s("in_embed"), 16)
            for i in range(2, TILES):
                sp.dma_start(patches[:, i, :], xp[:, i, :]).then_inc(s(f"in_patch{i}"), 16)
            for dst, src in ((bp_s, bp), (ln2g_s, ln2_g)):
                sp.dma_start(dst[:], src.rearrange("(a d) -> a d", a=1).to_broadcast([P, D])).then_inc(s("in_rows"), 16)
            sp.dma_start(cls_s[:], cls_ln2b[:]).then_inc(s("in_rows"), 16)
            sp.dma_start(cst[:, CONST_FIRST:], const[:, CONST_FIRST:]).then_inc(s("in_const"), 16)
            sp.dma_start(cst_rows[:], const_rows[:]).then_inc(s("in_const"), 16)
            sp.dma_start(wa0_s[:], wa0[:]).then_inc(s("in_attn0"), 16)
            sp.dma_start(ba0_s[:], ba0[:]).then_inc(s("in_attn0"), 16)
            sp.dma_start(wo0_s[:], wo0[:]).then_inc(s("in_attn0"), 16)
            sp.dma_start(bo0_s[:], bo0.rearrange("(a d) -> a d", a=1).to_broadcast([P, D])).then_inc(s("in_attn0"), 16)
            sp.dma_start(cent_s[:], cent[:]).then_inc(s("in_moe0"), 16)
            sp.dma_start(wa1_s[:], wa1[:]).then_inc(s("in_attn1"), 16)
            sp.dma_start(router_s[:], router[:]).then_inc(s("in_moe1"), 16)
            sp.dma_start(routerb_s[:], router_b.rearrange("(a d) -> a d", a=1).to_broadcast([P, EXPERTS])).then_inc(s("in_moe1"), 16)
            sp.wait_ge(s("zeros"), 1)
            for slots in (slots_in, slots_out):
                sp.dma_start(slots[:, :].rearrange("(w p) d -> p w d", p=P),
                             zero[:].rearrange("p (o d) -> p o d", o=1).to_broadcast([P, SLOTS // P, D])).then_inc(s("slots_zeroed"), 16)

        ZEROED = 32

        def norm_vector(dve, do, src, dst, eps_done, prepare=None):
            made, counted = {}, {}
            for i in range(TILES + 2):
                if i < TILES and prepare is not None:
                    made[i] = do.post(prepare(i))
                if 1 <= i <= TILES:
                    if prepare is not None:
                        do.until(made[i - 1])
                    counted[i - 1] = do.post(nc.vector.bn_stats(stats[:, i - 1, 0, :], src[:, i - 1, :]))
                if i >= 2:
                    do.until(counted[i - 2])
                    last = do.post(nc.vector.bn_aggr(mv[:, i - 2, :], stats[:, i - 2, 0:1, :]))
            do.until(last)
            nc.vector.tensor_scalar(veps[:], mv[:, :, 1], EPS, None, ALU.add).then_inc(s("veps_ready"), 1)
            dve.wait_ge(s("rstd_ready"), eps_done)
            for i in range(TILES):
                nc.vector.tensor_scalar(dst[:, i, :], src[:, i, :], mv[:, i, 0:1], rstd[:, i:i + 1],
                                        ALU.subtract, ALU.mult).then_inc(s("x_normed"), 1)

        EMBED_STAGES = ([("patch", 0), ("patch", 1), ("patch_norm", 0), ("patch", 2), ("patch_norm", 1), ("patch", 3),
                         ("patch_norm", 2), ("patch", 4), ("patch_norm", 3), ("patch_norm", 4)]
                        + [("y", 0), ("h", 0), ("y", 1), ("x", 0), ("h", 1), ("y", 2), ("x", 1), ("h", 2), ("y", 3), ("x", 2),
                           ("h", 3), ("y", 4), ("x", 3), ("h", 4), ("x", 4)])
        POWERS_OF = {"patch": 0, "y": 1, "h": 2}
        NORMS = 3 * TILES
        EMBED_POWERS = [stage for stage in EMBED_STAGES if stage[0] in POWERS_OF]

        def embed_vector(dve, do):
            nc.vector.memset(zero[:], 0.0).then_inc(s("zeros"), 1)
            do(nc.vector.memset(oT[:], 0.0))
            do(nc.vector.memset(minus_half_even[:], -HALF_EVEN))
            do(nc.vector.memset(qW[:], 0.0))

            def mean_of(kind, i):
                return mv3[:, POWERS_OF[kind], i, 0:1]

            def rstd_of(kind, i):
                return rstd3[:, POWERS_OF[kind], i:i + 1]

            def statistics(kind, i, src, groups=1):
                width = src.shape[-1] // groups
                for g in range(groups):
                    counted = do.post(nc.vector.bn_stats(stats[:, i, g, :], src[:, g * width:(g + 1) * width]))
                do.until(counted)
                do(nc.vector.bn_aggr(mv3[:, POWERS_OF[kind], i, :], stats[:, i, 0:groups, :]))
                nc.vector.tensor_scalar(veps3[:, POWERS_OF[kind], i:i + 1], mv3[:, POWERS_OF[kind], i, 1:2], EPS, None,
                                        ALU.add).then_inc(s("veps_ready"), 1)

            def power_done(kind, i):
                dve.wait_ge(s("rstd_ready"), EMBED_POWERS.index((kind, i)) + 1)

            for stage, i in EMBED_STAGES:
                if stage == "patch":
                    dve.wait_ge(s(f"in_patch{i}"), 16)
                    statistics("patch", i, patches[:, i, :], groups=3)
                elif stage == "patch_norm":
                    power_done("patch", i)
                    nc.vector.tensor_scalar(patches[:, i, :], patches[:, i, :], mean_of("patch", i), rstd_of("patch", i),
                                            ALU.subtract, ALU.mult).then_inc(s("patch_normed"), 1)
                elif stage == "y":
                    if i == 0:
                        dve.wait_ge(s("in_rows"), 48)
                        dve.wait_ge(s("bias_ps"), 1)
                        nc.vector.tensor_tensor(bp_s[:], psum[:, 7, 0:D], bp_s[:], ALU.add).then_inc(s("bias_row"), 1)
                        dve.wait_ge(s("bias_row"), 1)
                    dve.wait_ge(s("y_ps"), i + 1)
                    nc.vector.tensor_tensor(x[:, i, :], psum[:, 4 + i % 2, 0:D], bp_s[:], ALU.add).then_inc(s("y_read"), 1)
                    dve.wait_ge(s("y_read"), i + 1)
                    statistics("y", i, x[:, i, :])
                elif stage == "h":
                    if i == 0:
                        dve.wait_ge(s("in_const"), 32)
                    power_done("y", i)
                    do(nc.vector.tensor_tensor(rstd_of("y", i), rstd_of("y", i), table("is_patch")[:, i:i + 1], ALU.mult))
                    do(nc.vector.scalar_tensor_tensor(out=xd[:, i, :], in0=x[:, i, :], scalar=mean_of("y", i), in1=ln2g_s[:],
                                                      op0=ALU.subtract, op1=ALU.mult))
                    dve.wait_ge(s("cls_ps"), i + 1)
                    nc.vector.scalar_tensor_tensor(out=h[:, i, :], in0=xd[:, i, :], scalar=rstd_of("y", i), in1=psum[:, 6 + i % 2, 0:D],
                                                   op0=ALU.mult, op1=ALU.add).then_inc(s("h_made"), 1)
                    dve.wait_ge(s("h_made"), i + 1)
                    statistics("h", i, h[:, i, :])
                else:
                    power_done("h", i)
                    nc.vector.tensor_scalar(x[:, i, :], h[:, i, :], mean_of("h", i), rstd_of("h", i),
                                            ALU.subtract, ALU.mult).then_inc(s("x_normed"), 1)
            dve.wait_ge(s("in_attn0"), 64)
            dve.wait_ge(s("x_normed"), TILES)
            for i in range(TILES):
                last = do.post(nc.vector.tensor_tensor(h[:, i, :], h[:, i, :], bo0_s[:], ALU.add))
            do.until(last)

        def embed_gpsimd(pool):
            pool.wait_ge(s("in_first"), 16)
            for n, (kind, i) in enumerate(EMBED_POWERS):
                k = POWERS_OF[kind]
                pool.wait_ge(s("veps_ready"), n + 1)
                nc.gpsimd.tensor_tensor(rstd3[:, k, i:i + 1], veps3[:, k, i:i + 1], table("minus_half")[:, 0:1],
                                        ALU.pow).then_inc(s("rstd_ready"), 1)

        def two_banks(c):
            b = 2 * (c % 2)
            return psum[:, b:b + 2, :].rearrange("p b n -> p (b n)")[:, 0:ROWS]

        def patch_banks(i):
            b = 2 * (i % 2)
            return psum[:, b:b + 2, :].rearrange("p b n -> p (b n)")[:, 0:PD]

        def tile_bank(i):
            return psum[:, i, 0:D]

        def embed_scalar(act, do):
            act.wait_ge(s("in_embed"), 32)
            for c in range(PC):
                nc.scalar.activation(wpg_s[:, c, :], wp_s[:, c, :], ACT.Copy, scale=ln1_s[:, 0, c:c + 1]).then_inc(s("wpg_ready"), 1)
            act.wait_ge(s("in_first"), 16)
            nc.scalar.activation(identb[:], ident, ACT.Copy)
            for i in range(TILES):
                if i == 1:
                    for c in range(PC):
                        nc.scalar.activation(ln1b_s[:, c, :], ident, ACT.Identity, scale=0.0,
                                             bias=ln1_s[:, 1, c:c + 1]).then_inc(s("ln1b_ready"), 1)
                act.wait_ge(s("patchT_ps"), i + 1)
                nc.scalar.activation(patchT[:, :, i * P:(i + 1) * P], patch_banks(i).rearrange("p (c n) -> p c n", n=P),
                                     ACT.Copy).then_inc(s("patchT"), 1)
            act.wait_ge(s("in_const"), 32)
            nc.scalar.activation(causal_b[:], table("causal"), ACT.Copy).then_inc(s("identb_ready"), 1)

        def embed_tensor(pe):
            def turn(i):
                pe.wait_ge(s("patch_normed"), i + 1)
                if i >= 2:
                    pe.wait_ge(s("patchT"), i - 1)
                for c in range(PC):
                    last = nc.tensor.transpose(patch_banks(i)[:, c * P:(c + 1) * P], patches[:, i, c * P:(c + 1) * P], ident)
                last.then_inc(s("patchT_ps"), 1)

            def embed(i):
                pe.wait_ge(s("patchT"), i + 1)
                if i == 0:
                    pe.wait_ge(s("wpg_ready"), PC)
                if i >= 2:
                    pe.wait_ge(s("y_read"), i - 1)
                for c in range(PC):
                    last = nc.tensor.matmul(psum[:, 4 + i % 2, 0:D], patchT[:, c, i * P:(i + 1) * P], wpg_s[:, c, :],
                                            start=(c == 0), stop=(c == PC - 1))
                last.then_inc(s("y_ps"), 1)

            def row_constants(i):
                if i >= 2:
                    pe.wait_ge(s("h_made"), i - 1)
                nc.tensor.matmul(psum[:, 6 + i % 2, 0:D], patch_row[:, i * P:(i + 1) * P], cls_s[:],
                                 start=True, stop=True).then_inc(s("cls_ps"), 1)
            pe.wait_ge(s("zeros"), 1)
            for _ in range(WARM_MATMULS // 2):
                nc.tensor.matmul(psum[:, 7, 0:D], zero[:, 0:P], zero[:], start=True, stop=True)
            pe.wait_ge(s("in_first"), 16)
            turn(0)
            turn(1)
            pe.wait_ge(s("in_embed"), 32)
            pe.wait_ge(s("ln1b_ready"), PC)
            for c in range(PC):
                last = nc.tensor.matmul(psum[:, 7, 0:D], ln1b_s[:, c, :], wp_s[:, c, :], start=(c == 0), stop=(c == PC - 1))
            last.then_inc(s("bias_ps"), 1)
            embed(0)
            turn(2)
            pe.wait_ge(s("in_const"), 32)
            pe.wait_ge(s("in_rows"), 48)
            row_constants(0)
            pe.wait_ge(s("bias_row"), 1)
            row_constants(1)
            for i in range(1, TILES):
                embed(i)
                if i + 2 < TILES:
                    turn(i + 2)
                if i >= 2:
                    row_constants(i)
            turn_tensor(pe, x, 0, 0)

        def turn_tensor(pe, src, normed, turned):
            for i in range(TILES):
                pe.wait_ge(s("x_normed"), normed * TILES + i + 1)
                for c in range(DC):
                    last = nc.tensor.transpose(psum[:, i, c * P:(c + 1) * P], src[:, i, c * P:(c + 1) * P], ident)
                last.then_inc(s("turned_ps"), 1)

        def turn_scalar(act, dst, turned):
            for i in range(TILES):
                act.wait_ge(s("turned_ps"), turned * TILES + i + 1)
                nc.scalar.activation(dst[:, :, i * P:(i + 1) * P], psum[:, i, 0:DC * P].rearrange("p (c n) -> p c n", n=P),
                                     ACT.Copy).then_inc(s("turned"), 1)

        swapped = patches[:].rearrange("p t d -> p (t d)")[:, 2 * DC * ROWS:2 * DC * ROWS + 4 * HALF].rearrange("p (s n) -> p s n", n=HALF)

        def bank(b, parts=P):
            return psum[0:parts, b, :]

        def reused(engine, semaphore, count):
            if not (isinstance(count, int) and count <= 0):
                engine.wait_ge(semaphore, count)

        def keep_warm(pe, b, count):
            for _ in range(count):
                nc.tensor.matmul(bank(b)[:, 0:8 * SEQ], identb[:], causal_b[:], start=True, stop=True)

        def attention(layer):
            done = layer * PAIRS
            read = layer * (PAIRS + 2) + 2
            L = f"_a{layer}"
            src = xT if layer == 0 else xTb
            weights = wa0_s if layer == 0 else wq1_s
            Q, K, V = 0, 1, 2
            halves = range(2)
            values = [("v", V, c, half) for half in halves for c in range(DC)]

            def queries_keys(half):
                return [("qk", g, c, half) for c in range(DC) for g in (Q, K)]
            by_key = [("t", p) for p in range(PAIRS)]
            units = values + queries_keys(0) + by_key + queries_keys(1)

            def read_count(upto, kind):
                return sum(unit[0] == kind for unit in units[:upto + 1])

            def unit_psum(n, parts=P):
                return psum[0:parts, n % 8, :]

            def project_tensor(pe):
                for n, unit in enumerate(units):
                    if n >= 8:
                        kind = units[n - 8][0]
                        pe.wait_ge(s(f"{kind}_read" + L), read_count(n - 8, kind))
                    if unit[0] == "t":
                        p = unit[1]
                        pe.wait_ge(s("v_read" + L), DC * (p // (PAIRS // 2) + 1))
                        for j in range(2):
                            for c in range(DC):
                                last = nc.tensor.transpose(
                                    unit_psum(n, PW)[:, j * D + c * P:j * D + (c + 1) * P],
                                    vT[:, c, 2 * p + j, :, :].rearrange("p o k -> p (o k)"), ident)
                    else:
                        _, g, c, half = unit
                        for k in range(DC):
                            last = nc.tensor.matmul(unit_psum(n)[:, 0:HALF], weights[:, k, g, c * P:(c + 1) * P],
                                                    src[:, k, half * HALF:(half + 1) * HALF], start=(k == 0), stop=(k == DC - 1))
                    last.then_inc(s("unit" + L), 1)

            def values_twice(c, half):
                return vT[:, c, half * IMAGES // 2:(half + 1) * IMAGES // 2, :, :]

            def twice(tokens):
                return tokens.rearrange("p (i o k) -> p i o k", o=1, k=SEQ).to_broadcast([P, IMAGES // 2, 2, SEQ])

            turns = [unit for unit in units if unit[0] == "qk"]

            def rotated_part(n):
                _, g, c, half = turns[n]
                return (qr if g == Q else kr)[:, c, half * HALF:(half + 1) * HALF]

            def swap_sync(sp):
                for n in range(len(turns)):
                    sp.wait_ge(s("qk_read" + L), n + 1)
                    if n >= 4:
                        sp.wait_ge(s("rotated"), n - 3)
                    for odd in range(2):
                        sp.dma_start(swapped[odd:P:2, n % 4, :], rotated_part(n)[1 - odd:P:2, :]).then_inc(s(f"swapped{n % 4}"), 16)

            def rotate_vector(dve, half):
                images = lambda a: a.rearrange("p (i k) -> p i k", k=SEQ)
                over_images = lambda name: table(name).rearrange("p (o k) -> p o k", o=1).to_broadcast([P, IMAGES // 2, SEQ])
                for n in range(4 * half, 4 * half + 4):
                    dve.wait_ge(s(f"swapped{n % 4}"), 32 * (n // 4 + 1))
                    nc.vector.tensor_tensor(images(rotated_part(n)), images(rotated_part(n)), over_images("cos"), ALU.mult)
                    nc.vector.tensor_tensor(images(swapped[:, n % 4, :]), images(swapped[:, n % 4, :]), over_images("sin"),
                                            ALU.mult).then_inc(s("products"), 1)

            def project_vector(dve):
                for n, unit in enumerate(units):
                    if unit[0] == "v":
                        _, g, c, half = unit
                        dve.wait_ge(s("unit" + L), n + 1)
                        nc.vector.tensor_tensor(values_twice(c, half), twice(unit_psum(n)[:, 0:HALF]),
                                                twice(invT[:, half * HALF:(half + 1) * HALF]), ALU.mult).then_inc(s("v_read" + L), 1)
                    if unit[0] == "qk":
                        _, g, c, half = unit
                        dve.wait_ge(s("unit" + L), n + 1)
                        nc.vector.tensor_tensor(rotated_part(turns.index(unit)), unit_psum(n)[:, 0:HALF],
                                                invT[:, half * HALF:(half + 1) * HALF], ALU.mult).then_inc(s("qk_read" + L), 1)

            def add_gpsimd(pool, half):
                for n in range(4 * half, 4 * half + 4):
                    pool.wait_ge(s("products"), n + 1)
                    nc.gpsimd.tensor_tensor(rotated_part(n), rotated_part(n), swapped[:, n % 4, :], ALU.add).then_inc(s("rotated"), 1)

            def first_spreads(pool):
                pool.wait_ge(s("rotated") if layer == 0 else s("qk_read" + L), len(turns) // 2)
                spread_gpsimd(pool, 0, 0)
                spread_gpsimd(pool, 1, 1)

            def project_scalar(act):
                for n, unit in enumerate(units):
                    if unit[0] == "v" and layer == 0:
                        _, g, c, half = unit
                        act.wait_ge(s("unit" + L), n + 1)
                        nc.scalar.activation(values_twice(c, half), twice(unit_psum(n)[:, 0:HALF]), ACT.Identity,
                                             bias=ba0_s[:, V, c:c + 1]).then_inc(s("v_read" + L), 1)
                    if unit[0] == "qk" and layer == 0:
                        _, g, c, half = unit
                        act.wait_ge(s("unit" + L), n + 1)
                        nc.scalar.activation(rotated_part(turns.index(unit)), unit_psum(n)[:, 0:HALF], ACT.Identity,
                                             bias=ba0_s[:, g, c:c + 1]).then_inc(s("qk_read" + L), 1)
                    if unit[0] == "t":
                        p = unit[1]
                        act.wait_ge(s("unit" + L), n + 1)
                        nc.scalar.activation(vD[:, 2 * p:2 * p + 2, :], unit_psum(n, PW).rearrange("p (j d) -> p j d", d=D),
                                             ACT.Copy).then_inc(s("t_read" + L), 1)

            def scores_psum(buf):
                return psum[:, 2 * buf:2 * buf + 2, 0:8 * SEQ]

            def scores_tensor(pe, p, buf):
                pe.wait_ge(s("kM_ready"), done + p + 1)
                if not early(p):
                    pe.wait_ge(s("sc_read"), done + p - 1)
                if layer == 1:
                    keep_warm(pe, 2 * buf, 4)
                for c in range(DC):
                    columns = slice(c * 4 * SEQ, (c + 1) * 4 * SEQ)
                    for j in range(2):
                        rows = slice(64 * j, 64 * j + QPAD)
                        for r in range(2):
                            if layer == 0:
                                nc.tensor.matmul(bank(2 * buf + r)[rows, columns], identb[:, rows], causal_b[:, columns],
                                                 start=True, stop=False)
                            last = nc.tensor.matmul(bank(2 * buf + r)[rows, columns], qW[64 * r:64 * r + 64, buf, c, j, :],
                                                    kM[64 * r:64 * r + 64, buf, c, j, :, :].rearrange("p a k -> p (a k)"),
                                                    start=(layer == 1), stop=True)
                last.then_inc(s("sc_ps"), 1)

            def early(p):
                return isinstance(p, int) and p < 2

            def turn_probs_tensor(pe, p, buf):
                pe.wait_ge(s("exp"), done + p + 1)
                if not (isinstance(p, int) and p == 0):
                    pe.wait_ge(s("pT_ready"), done + p)
                for g in range(8):
                    last = nc.tensor.transpose(bank(4 + g // 4, PW)[:, (g % 4) * P:(g % 4 + 1) * P],
                                               prob[:, buf, 2 * g:2 * g + 2, :].rearrange("p a k -> p (a k)"), ident)
                last.then_inc(s("pT_ps"), 1)

            def output_tensor(pe, p, buf):
                pe.wait_ge(s("pT_ready"), done + p + 1)
                pe.wait_ge(s("vM_ready"), done + p + 1)
                dst = bank(6 + buf)
                for g in range(8):
                    r, c, hp = g // 4, (g // 2) % 2, g % 2
                    row = 64 * r + 32 * hp
                    for j in range(2):
                        nc.tensor.matmul(dst[row:row + 32, c * PW + j * SEQ:c * PW + (j + 1) * SEQ],
                                         vM[:, buf, j, c * P + row:c * P + row + 32],
                                         pT[:, buf, g, 64 * j:64 * j + SEQ], start=True, stop=True, tile_position=(0, row))
                    last = nc.tensor.matmul(dst[row:row + 32, (DC + c) * PW:(DC + c + 1) * PW], table("head2", PW)[:, 0:2 * HD],
                                            pT[:, buf, g, :].rearrange("p (j q) -> p j q", j=2)[:, :, 0:SEQ],
                                            start=True, stop=True, tile_position=(0, row))
                last.then_inc(s("o_ps"), 1)

            def tensor(pe):
                pe.wait_ge(s("identb_ready"), 1)
                project_tensor(pe)
                for kind in ("qk", "t", "v"):
                    pe.wait_ge(s(f"{kind}_read" + L), read_count(len(units), kind))
                keep_warm(pe, 6, 8)
                scores_tensor(pe, 0, 0)
                scores_tensor(pe, 1, 1)
                keep_warm(pe, 6, 10)
                turn_probs_tensor(pe, 0, 0)
                with pe.Fori(1, PAIRS // 2) as u:
                    for b in range(2):
                        p = u * 2 + b
                        scores_tensor(pe, p, b)
                        turn_probs_tensor(pe, p - 1, 1 - b)
                        output_tensor(pe, p - 2, b)

                def finish(i):
                    pe.wait_ge(s("o_read"), read + min(PAIRS, -(-(i + 1) * P // PW)))
                    if i == TILES - 1:
                        pe.wait_ge(s("pT_ready"), done + PAIRS)
                    for c in range(DC):
                        if layer == 0:
                            last = nc.tensor.matmul(tile_bank(i), oT[:, c, i * P:(i + 1) * P], wo0_s[:, c, :], start=(c == 0), stop=(c == DC - 1))
                        else:
                            last = nc.tensor.transpose(tile_bank(i)[:, c * P:(c + 1) * P], oT[:, c, i * P:(i + 1) * P], ident)
                    last.then_inc(s("finished" + L), 1)
                pe.wait_ge(s("sc_read"), done + PAIRS - 1)
                finish(0)
                finish(1)
                turn_probs_tensor(pe, PAIRS - 1, 1)
                keep_warm(pe, 3, 6)
                output_tensor(pe, PAIRS - 2, 0)
                finish(2)
                keep_warm(pe, 3, 6)
                output_tensor(pe, PAIRS - 1, 1)
                keep_warm(pe, 5, 12)
                finish(3)
                finish(4)

            def softmax_vector(dve, p, buf):
                heads = lambda a: a.rearrange("p r (n k) -> p r n k", k=SEQ)
                dve.wait_ge(s("sc_ps"), done + p + 1)
                nc.vector.reduce_max(smax[:, buf], heads(scores_psum(buf)), AX.X).then_inc(s("smax"), 1)
                dve.wait_ge(s("smax"), done + p + 1)
                if not early(p):
                    dve.wait_ge(s("exp"), done + p - 1)
                nc.vector.tensor_tensor(heads(sc[:, buf]), heads(scores_psum(buf)),
                                        smax[:, buf].rearrange("p r (n o) -> p r n o", o=1).to_broadcast([P, 2, 8, SEQ]),
                                        ALU.subtract).then_inc(s("sc_read"), 1)

            def output_vector(dve, p, buf):
                dve.wait_ge(s("o_ps"), done + p + 1)
                nc.vector.reciprocal(srec[:], bank(6 + buf)[:, DC * PW:2 * DC * PW]).then_inc(s("srec"), 1)
                dve.wait_ge(s("srec"), done + p + 1)
                dst = oT[:, :, bass.ds(p * PW, PW)]
                raw = bank(6 + buf)[:, 0:DC * PW].rearrange("p (c n) -> p c n", n=PW)
                rec = srec[:].rearrange("p (c n) -> p c n", n=PW)
                if layer == 0:
                    nc.vector.tensor_tensor(dst, raw, rec, ALU.mult).then_inc(s("o_read"), 1)
                else:
                    nc.vector.scalar_tensor_tensor(out=dst, in0=raw, scalar=wmean[:, 2:3], in1=rec, op0=ALU.mult,
                                                   op1=ALU.mult).then_inc(s("o_read"), 1)
                dve.wait_ge(s("o_read"), read + p + 1)

            def vector(dve, do):
                if layer == 0:
                    rotate_vector(dve, 0)
                else:
                    project_vector(dve)
                for p in range(2):
                    softmax_vector(dve, p, p)
                    nc.vector.memset(srec[:, 0:1], 0.0).then_inc(s("o_read"), 1)
                if layer == 0:
                    rotate_vector(dve, 1)
                dve.wait_ge(s("o_read"), read)
                with dve.Fori(1, PAIRS // 2) as u:
                    for b in range(2):
                        p = u * 2 + b
                        softmax_vector(dve, p, b)
                        output_vector(dve, p - 2, b)
                output_vector(dve, PAIRS - 2, 0)
                output_vector(dve, PAIRS - 1, 1)

            def spread_gpsimd(pool, p, buf):
                if not early(p):
                    pool.wait_ge(s("sc_ps"), done + p - 1)
                pair = lambda a: a[:, :, bass.ds(p * PW, PW)].rearrange("p c (j k) -> p c j k", k=SEQ)
                nc.gpsimd.tensor_copy(qW[:, buf, :, :, 0:SEQ], pair(qr))
                for c in range(DC):
                    last = nc.gpsimd.tensor_tensor(
                        kM[:, buf, c, :, :, :],
                        kr[:, c, bass.ds(p * PW, PW)].rearrange("p (j o k) -> p j o k", o=1, k=SEQ).to_broadcast([P, 2, 4, SEQ]),
                        table("head4").rearrange("p (o a u) -> p o a u", o=1, u=1).to_broadcast([P, 2, 4, SEQ]), ALU.mult)
                last.then_inc(s("kM_ready"), 1)

            def gpsimd(pool):
                if layer == 0:
                    add_gpsimd(pool, 0)
                first_spreads(pool)
                spread_gpsimd(pool, 2, 0)
                spread_gpsimd(pool, 3, 1)
                if layer == 0:
                    add_gpsimd(pool, 1)
                pool.wait_ge(s("rotated") if layer == 0 else s("qk_read" + L), len(turns))
                with pool.Fori(2, PAIRS // 2) as u:
                    for b in range(2):
                        spread_gpsimd(pool, u * 2 + b, b)

            def mask_values_scalar(act, p, buf):
                act.wait_ge(s("o_read"), read + p - 1)
                of_heads = lambda a, odd: a.rearrange("p j (n a d) -> p (j n) a d", a=2, d=HD)[:, :, odd, :]
                for odd in range(2):
                    last = nc.scalar.activation(of_heads(vM[:, buf], odd), of_heads(vD[:, bass.ds(p * 2, 2), :], odd), ACT.Copy,
                                                scale=table("head2", PW)[:, odd * HD:odd * HD + 1])
                last.then_inc(s("vM_ready"), 1)

            def scalar(act):
                def step(p, buf):
                    act.wait_ge(s("sc_read"), done + p + 1)
                    if not early(p):
                        act.wait_ge(s("pT_ps"), done + p - 1)
                    nc.scalar.activation(prob[:, buf].rearrange("p n k -> p (n k)"), sc[:, buf].rearrange("p r n -> p (r n)"), ACT.Exp,
                                         scale=SCALE if layer == 0 else qk_scale[:, 0:1]).then_inc(s("exp"), 1)
                    if not (isinstance(p, int) and p == 0):
                        mask_values_scalar(act, p - 1, 1 - buf)
                    act.wait_ge(s("pT_ps"), done + p + 1)
                    if not early(p):
                        act.wait_ge(s("o_ps"), done + p - 1)
                    nc.scalar.activation(pT[:, buf], psum[0:PW, 4:6, :].rearrange("p b (g n) -> p (b g) n", n=P),
                                         ACT.Copy).then_inc(s("pT_ready"), 1)
                project_scalar(act)
                act.wait_ge(s("t_read" + L), PAIRS)
                step(0, 0)
                step(1, 1)
                with act.Fori(1, PAIRS // 2) as u:
                    for b in range(2):
                        step(u * 2 + b, b)
                mask_values_scalar(act, PAIRS - 1, 1)

            return tensor, vector, gpsimd, scalar, swap_sync

        attn0 = attention(0)
        attn1 = attention(1)

        def moe(layer):
            L = f"_m{layer}"
            F1 = FF * (1 + layer)
            w1, w2 = (w1_0, w2_0) if layer == 0 else (w1_1, w2_1)
            logit_w = cent_s if layer == 0 else router_s

            def load_count(engine):
                return engine.value_load(winexp_i[0:1, WINDOWS + 1:WINDOWS + 2], min_val=MIN_WINDOWS, max_val=WINDOWS)

            def load_pairs(engine):
                return engine.value_load(winexp_i[0:1, WINDOWS + 2:WINDOWS + 3], min_val=-(-MIN_WINDOWS // 2), max_val=WINDOWS // 2)

            def load_seconds(engine):
                return engine.value_load(winexp_i[0:1, WINDOWS + 3:WINDOWS + 4], min_val=MIN_WINDOWS // 2, max_val=WINDOWS // 2)

            def windows(engine, body, before=None):
                engine.wait_ge(s("table" + L), 1)
                count = load_count(engine)
                pairs = load_pairs(engine)
                if before is not None:
                    before()
                body(0, 0)
                body(0, 1)
                with engine.Fori(1, pairs) as u:
                    body(u, 0)
                    with engine.If(u * 2 + 1 < count):
                        body(u, 1)
                return count

            def logits_tensor(pe):
                pe.wait_ge(s("in_moe0" if layer == 0 else "in_moe1"), 16 if layer == 0 else 32)
                for i in range(TILES):
                    pe.wait_ge(s("turned"), (1 + layer) * TILES + i + 1)
                    for c in range(DC):
                        last = nc.tensor.matmul(bank(7)[:, i * EXPERTS:(i + 1) * EXPERTS], xT[:, c, i * P:(i + 1) * P],
                                                logit_w[:, c, :], start=(c == 0), stop=(c == DC - 1))
                last.then_inc(s("logits" + L), 1)
                pe.wait_ge(s("hot" + L), 1)
                nc.tensor.matmul(bank(5)[:, 0:EXPERTS], table("earlier"), mine[:], start=True, stop=True)
                nc.tensor.matmul(bank(6)[:, 0:EXPERTS], table("ones"), mine[:], start=True, stop=True).then_inc(s("ranks" + L), 1)
                keep_warm(pe, 4, 3 * WARM_MATMULS // 2)

            def route_vector(dve, do):
                T8 = [P, TILES, EXPERTS]
                per_expert = lambda a: a.rearrange("p (o e) -> p o e", o=1).to_broadcast(T8)
                per_row = lambda a: a.rearrange("p (t o) -> p t o", o=1).to_broadcast(T8)
                dve.wait_ge(s("logits" + L), 1)
                logits = bank(7)[:, 0:TILES * EXPERTS].rearrange("p (t e) -> p t e", e=EXPERTS)
                if layer == 0:
                    do(nc.vector.reduce_max(lmax[:], logits, AX.X))
                    ranked, top = logits, lmax
                    nc.vector.tensor_copy(gate[:], lmax[:]).then_inc(s("gate_in" + L), 1)
                else:
                    do(nc.vector.tensor_tensor(lg[:], logits, per_expert(routerb_s[:]), ALU.add))
                    do(nc.vector.reduce_max(lmax[:], lg[:], AX.X))
                    nc.vector.tensor_tensor(lexp[:], lg[:], per_row(lmax[:]), ALU.subtract).then_inc(s("gate_in" + L), 1)
                    dve.wait_ge(s("gate_exp" + L), 1)
                    do(nc.vector.reduce_max(lmax[:], lexp[:], AX.X))
                    ranked, top = lexp[:], lmax
                do(nc.vector.tensor_tensor(r1[:], ranked, per_row(top[:]), ALU.is_equal))
                do(nc.vector.tensor_tensor(r1[:], r1[:], per_expert(table("first")), ALU.mult))
                do(nc.vector.reduce_max(rsmall[:], r1[:], AX.X))
                do(nc.vector.tensor_tensor(hot[:], r1[:], per_row(rsmall[:]), ALU.is_equal))
                do(nc.vector.tensor_tensor(hot[:], hot[:], per_row(table("valid")), ALU.mult))
                nc.vector.reduce_sum(mine[:], hot[:].rearrange("p t e -> p e t"), AX.X).then_inc(s("hot" + L), 1)
                ct = cmp[:].rearrange("p (t e u) -> p t e u", e=EXPERTS, u=TILES)
                for i in range(TILES):
                    last = do.post(nc.vector.tensor_tensor(
                        ct[:, i], hot[:].rearrange("p u e -> p e u"),
                        table("tiles_before")[:, i * TILES:(i + 1) * TILES].rearrange("p (o u) -> p o u", o=1).to_broadcast([P, EXPERTS, TILES]),
                        ALU.mult))
                do.until(last)
                last = do.post(nc.vector.reduce_sum(rank[:], ct, AX.X))
                if layer == 0:
                    do(nc.vector.tensor_tensor(tokstat[:, :, 0], rstd[:], rstd[:], ALU.mult))
                    do(nc.vector.tensor_tensor(tokstat[:, :, 1], tokstat[:, :, 0], mv[:, :, 1], ALU.mult))
                    nc.vector.tensor_scalar(veps[:], tokstat[:, :, 1], EPS, None, ALU.add).then_inc(s("veps_ready"), 1)
                dve.wait_ge(s("ranks" + L), 1)
                do.until(last)
                c5 = cmp[:, 0:EXPERTS * TILES].rearrange("p (e t) -> p e t", t=TILES)
                do(nc.vector.tensor_tensor(c5, bank(6)[:, 0:EXPERTS].rearrange("p (e o) -> p e o", o=1).to_broadcast([P, EXPERTS, TILES]),
                                           table("full").rearrange("p (o t) -> p o t", o=1).to_broadcast([P, EXPERTS, TILES]), ALU.is_gt))
                ranked_in = do.post(nc.vector.tensor_tensor(rank[:], rank[:], per_expert(bank(5)[:, 0:EXPERTS]), ALU.add))
                do(nc.vector.reduce_sum(nwin[:], c5, AX.X))
                c8 = cmp[:, EXPERTS * TILES:EXPERTS * (TILES + EXPERTS)].rearrange("p (e f) -> p e f", f=EXPERTS)
                do(nc.vector.tensor_tensor(c8, table("upto").rearrange("p (e f) -> p e f", f=EXPERTS),
                                           nwin[:].rearrange("p (o f) -> p o f", o=1).to_broadcast([P, EXPERTS, EXPERTS]), ALU.mult))
                do(nc.vector.reduce_sum(wend[:], c8, AX.X))
                do(nc.vector.tensor_tensor(wbeg[:], wend[:], nwin[:], ALU.subtract))
                do.until(ranked_in)
                do(nc.vector.scalar_tensor_tensor(out=rank[:], in0=per_expert(wbeg[:]), scalar=float(WIN), in1=rank[:],
                                                  op0=ALU.mult, op1=ALU.add))
                do(nc.vector.tensor_tensor(rank[:], rank[:], hot[:], ALU.mult))
                do(nc.vector.reduce_sum(slot_f[:], rank[:], AX.X))
                do(nc.vector.tensor_tensor(slot_f[:], slot_f[:], table("pad_slot"), ALU.add))
                nc.vector.tensor_copy(slot_i[:], slot_f[:]).then_inc(s("slots" + L), 1)
                cw = cmp[:, 0:(WINDOWS + 1) * EXPERTS].rearrange("p (w e) -> p w e", e=EXPERTS)
                do(nc.vector.tensor_tensor(cw, wend[:].rearrange("p (o e) -> p o e", o=1).to_broadcast([P, WINDOWS + 1, EXPERTS]),
                                           table("window").rearrange("p (w o) -> p w o", o=1).to_broadcast([P, WINDOWS + 1, EXPERTS]), ALU.is_le))
                do(nc.vector.reduce_sum(winexp[:, 0:WINDOWS + 1], cw, AX.X))
                do.post(nc.vector.tensor_scalar(winexp_i[:, 0:WINDOWS + 1], winexp[:, 0:WINDOWS + 1], float(EXPERTS - 1), None, ALU.min))
                count = wend[:, EXPERTS - 1:EXPERTS]
                do.post(nc.vector.tensor_copy(winexp_i[:, WINDOWS + 1:WINDOWS + 2], count))
                do(nc.vector.tensor_scalar(cmp[:, 0:1], count, 0.5, 0.25, ALU.mult, ALU.add))
                do(nc.vector.tensor_scalar(winexp[:, WINDOWS + 2:WINDOWS + 3], cmp[:, 0:1], HALF_EVEN, HALF_EVEN, ALU.add, ALU.subtract))
                do.post(nc.vector.tensor_copy(winexp_i[:, WINDOWS + 2:WINDOWS + 3], winexp[:, WINDOWS + 2:WINDOWS + 3]))
                nc.vector.tensor_tensor(winexp_i[:, WINDOWS + 3:WINDOWS + 4], count,
                                        winexp[:, WINDOWS + 2:WINDOWS + 3], ALU.subtract).then_inc(s("table" + L), 1)
                for i in range(TILES):
                    nc.vector.tensor_scalar(chosen[:, i, :], table("slot"), slot_f[:, i:i + 1], None,
                                            ALU.is_equal).then_inc(s("chosen" + L), 1)
                if layer == 0:
                    dve.wait_ge(s("gate_exp" + L), 1)
                    do(nc.vector.tensor_scalar(gate[:], gate[:], 1.0, None, ALU.add))
                else:
                    do(nc.vector.reduce_sum(gate[:], lexp[:], AX.X))
                do(nc.vector.reciprocal(gate[:], gate[:]))
                if layer == 0:
                    weight_scales_vector(dve, do)

            def route_scalar(act):
                act.wait_ge(s("gate_in" + L), 1)
                if layer == 0:
                    nc.scalar.activation(gate[:], gate[:], ACT.Exp, scale=-1.0).then_inc(s("gate_exp" + L), 1)
                    act.wait_ge(s("rstd_ready"), NORMS + 2)
                    for i in range(TILES):
                        nc.scalar.activation(xd[:, i, :], x[:, i, :], ACT.Copy, scale=rstd[:, i:i + 1]).then_inc(s("inner_normed"), 1)
                else:
                    nc.scalar.activation(lexp[:], lexp[:], ACT.Exp).then_inc(s("gate_exp" + L), 1)

            def dispatch_gpsimd(pool):
                rows = xd if layer == 0 else x
                pool.wait_ge(s("slots_zeroed"), ZEROED)
                pool.wait_ge(s("slots" + L), 1)
                if layer == 0:
                    pool.wait_ge(s("inner_normed"), TILES)
                for i in range(TILES):
                    pool.indirect_dma_start(out=slots_in[:, :], out_offset=bass.IndirectOffsetOnAxis(ap=slot_i[:, i:i + 1], axis=0),
                                            in_=rows[:, i, :], in_offset=None).then_inc(s("dispatched" + L), 16)

                def store(u, b):
                    pool.wait_ge(s(f"z_ready{b}" + L), u + 1)
                    pool.dma_start(slots_out[bass.ds((u * 2 + b) * WIN, WIN), :], zw[:, b, :]).then_inc(s(f"z_stored{b}" + L), 16)
                windows(pool, store)
                pairs, seconds = load_pairs(pool), load_seconds(pool)
                pool.wait_ge(s("z_stored0" + L), pairs * 16)
                pool.wait_ge(s("z_stored1" + L), seconds * 16)
                nc.gpsimd.tensor_tensor(stored[:], table("ones")[0:1, 0:1], table("ones")[0:1, 0:1], ALU.mult).then_inc(s("all_stored"), 1)
                pool.wait_ge(s("all_stored"), layer + 1)
                for i in range(TILES):
                    pool.indirect_dma_start(out=z[:, i, :], out_offset=None, in_=slots_out[:, :],
                                            in_offset=bass.IndirectOffsetOnAxis(ap=slot_i[:, i:i + 1], axis=0)).then_inc(s(f"z_back{i}"), 16)

            def following(u, b):
                return (u, 1) if b == 0 else (u + 1, 0)

            def is_first(u):
                return isinstance(u, int) and u == 0

            def weights_sync(sp):
                def expert_of(u, b):
                    return sp.value_load(winexp_i[0:1, bass.ds(u * 2 + b, 1)], min_val=0, max_val=EXPERTS - 1)

                def load_rows(u, b):
                    if not is_first(u):
                        sp.wait_ge(s(f"xw_used{b}" + L), u)
                        sp.dma_start(xw[:, b, :], slots_in[bass.ds((u * 2 + b) * WIN, WIN), :]).then_inc(s(f"xw_in{b}" + L), 16)
                    if layer == 0:
                        e = expert_of(u, b)
                        if not is_first(u):
                            sp.wait_ge(s(f"xwT_ready{b}" + L), u)
                        sp.dma_start(par_s[:, b, 0:2 * DC], par_0[bass.ds(e, 1), :, 0:2 * DC].rearrange("e p n -> (e p) n")).then_inc(s(f"gain_in{b}" + L), 16)

                def load_w1(u, b, e):
                    if not is_first(u):
                        sp.wait_ge(s("hid_ps" + L), (u * 2 + b - 1) * FC)
                    sp.dma_start(w1_s[:, b, 0:DC * F1], w1[bass.ds(e, 1), :, :].rearrange("e p n -> (e p) n")).then_inc(s(f"w1_in{b}" + L), 16)

                def load_w2(u, b, e):
                    if not is_first(u):
                        sp.wait_ge(s(f"w2_used{b}" + L), u)
                    if layer == 0:
                        sp.dma_start(par_s[:, b, 2 * DC:], par_0[bass.ds(e, 1), :, 2 * DC:].rearrange("e p n -> (e p) n")).then_inc(s(f"b1_in{b}" + L), 16)
                    sp.dma_start(w2_s[:, b, :, :].rearrange("p f n -> p (f n)"), w2[bass.ds(e, 1), :, :].rearrange("e p n -> (e p) n")).then_inc(s(f"w2_in{b}" + L), 16)
                    if layer == 0:
                        if not is_first(u):
                            sp.wait_ge(s(f"z_ready{b}" + L), u)
                        sp.dma_start(b2_s[:, b, :], b2_0[bass.ds(e, 1), :].to_broadcast([P, D])).then_inc(s(f"b2_in{b}" + L), 16)

                def load(u, b):
                    if is_first(u):
                        load_rows(u, b)
                    else:
                        load_rows(*following(u, b))
                    e = expert_of(u, b)
                    load_w1(u, b, e)
                    load_w2(u, b, e)
                    if is_first(u) and b == 1:
                        sp.wait_ge(s("dispatched" + L), 16 * TILES)
                        load_rows(1, 0)
                windows(sp, load)

            def turned_rows(b):
                return bank(7 * b)[:, 0:DC * P]

            def expert_tensor(pe):
                def select_rows(b):
                    rows = xd if layer == 0 else x
                    for c in range(DC):
                        for i in range(TILES):
                            last = nc.tensor.matmul(turned_rows(b)[:, c * P:(c + 1) * P], rows[:, i, c * P:(c + 1) * P],
                                                    chosen[:, i, b * WIN:(b + 1) * WIN], start=(i == 0), stop=(i == TILES - 1))
                    last.then_inc(s(f"xw_used{b}" + L), 1)

                def turn_rows(u, b):
                    if is_first(u):
                        return
                    pe.wait_ge(s(f"xw_in{b}" + L), u * 16)
                    pe.wait_ge(s(f"xwT_ready{b}" + L), u)
                    for c in range(DC):
                        last = nc.tensor.transpose(turned_rows(b)[:, c * P:(c + 1) * P], xw[:, b, c * P:(c + 1) * P], ident)
                    last.then_inc(s(f"xw_used{b}" + L), 1)

                def window(u, b):
                    w = u * 2 + b
                    pe.wait_ge(s(f"w1_in{b}" + L), u * 16 + 16)
                    pe.wait_ge(s(f"xwT_ready{b}" + L), u + 1)
                    w1v = w1_s[:, b, 0:DC * F1].rearrange("p (k f) -> p k f", f=F1)
                    for f in range(FC):
                        reused(pe, s("hid_ready" + L), w * FC + max(f - 3, 0))
                        for part in range(1 + layer):
                            for k in range(DC):
                                last = nc.tensor.matmul(bank(1 + f % 4)[:, part * WIN:(part + 1) * WIN],
                                                        w1v[:, k, part * FF + f * P:part * FF + (f + 1) * P], xwT[:, b, k, :],
                                                        start=(k == 0), stop=(k == DC - 1))
                        last.then_inc(s("hid_ps" + L), 1)
                    turn_rows(*following(u, b))
                    pe.wait_ge(s(f"w2_in{b}" + L), u * 16 + 16)
                    reused(pe, s(f"z_ready{b}" + L), u)
                    for f in range(FC):
                        pe.wait_ge(s("hid_ready" + L), w * FC + f + 1)
                        last = nc.tensor.matmul(bank(5 + b)[:, 0:D], hid[:, f, :], w2_s[:, b, f, :], start=(f == 0), stop=(f == FC - 1))
                    last.then_inc(s(f"w2_used{b}" + L), 1)

                def before():
                    pe.wait_ge(s("chosen" + L), TILES)
                    if layer == 0:
                        pe.wait_ge(s("inner_normed"), TILES)
                    select_rows(0)
                    select_rows(1)
                    keep_warm(pe, 4, WARM_MATMULS // 2)
                windows(pe, window, before)

            def expert_vector(dve, do):
                def rows_out(u, b):
                    dve.wait_ge(s(f"xw_used{b}" + L), u + 1)
                    if not is_first(u):
                        dve.wait_ge(s("hid_ps" + L), (u * 2 + b - 1) * FC)
                    turned = turned_rows(b).rearrange("p (c n) -> p c n", n=P)
                    if layer == 0:
                        dve.wait_ge(s(f"gain_in{b}" + L), u * 16 + 16)
                        for c in range(DC):
                            last = nc.vector.tensor_scalar(xwT[:, b, c, :], turned[:, c, :], par_s[:, b, c:c + 1], par_s[:, b, DC + c:DC + c + 1],
                                                           ALU.mult, ALU.add)
                    else:
                        last = nc.vector.tensor_copy(xwT[:, b], turned)
                    last.then_inc(s(f"xwT_ready{b}" + L), 1)

                def window(u, b):
                    w = u * 2 + b
                    if layer == 1:
                        for f in range(FC):
                            dve.wait_ge(s("act_ready" + L), w * FC + f + 1)
                            nc.vector.tensor_tensor(hid[:, f, :], bank(1 + f % 4)[:, WIN:2 * WIN], act_a[:, f % 2, :],
                                                    ALU.mult).then_inc(s("hid_ready" + L), 1)
                    rows_out(*following(u, b))
                    if layer == 0 and is_first(u) and b == 0:
                        quant_weights_vector(dve, do)
                    dve.wait_ge(s(f"w2_used{b}" + L), u + 1)
                    reused(dve, s(f"z_stored{b}" + L), u * 16)
                    if layer == 0:
                        dve.wait_ge(s(f"b2_in{b}" + L), u * 16 + 16)
                        nc.vector.tensor_tensor(zw[:, b, :], bank(5 + b)[:, 0:D], b2_s[:, b, :], ALU.add).then_inc(s(f"z_ready{b}" + L), 1)
                    else:
                        nc.vector.tensor_copy(zw[:, b, :], bank(5 + b)[:, 0:D]).then_inc(s(f"z_ready{b}" + L), 1)
                windows(dve, window, lambda: rows_out(0, 0))

            def expert_scalar(act):
                def window(u, b):
                    w = u * 2 + b
                    if layer == 0:
                        act.wait_ge(s(f"b1_in{b}" + L), u * 16 + 16)
                    for f in range(FC):
                        act.wait_ge(s("hid_ps" + L), w * FC + f + 1)
                        src = bank(1 + f % 4)[:, 0:WIN]
                        if layer == 0:
                            if f == 0:
                                reused(act, s(f"w2_used{1 - b}" + L), u + b)
                            last = nc.scalar.activation(hid[:, f, :], src, ACT.Relu, bias=par_s[:, b, 2 * DC + f:2 * DC + f + 1])
                            last.then_inc(s("hid_ready" + L), 1)
                        else:
                            reused(act, s("hid_ready" + L), w * FC + max(f - 1, 0))
                            nc.scalar.activation(act_a[:, f % 2, :], src, ACT.Silu).then_inc(s("act_ready" + L), 1)
                windows(act, window)

            return logits_tensor, route_vector, route_scalar, dispatch_gpsimd, weights_sync, expert_tensor, expert_vector, expert_scalar

        moe0 = moe(0)
        moe1 = moe(1)

        def quant_weights_scalar(act):
            act.wait_ge(s("in_attn1"), 16)
            act.wait_ge(s("pT_ps"), PAIRS)
            for g in range(4):
                if g > 0:
                    act.wait_ge(s("wsum_ready"), g)
                nc.scalar.activation(prob[:].rearrange("p b n k -> p (b n k)")[:, 0:DC * D].rearrange("p (k n) -> p k n", k=DC),
                                     wa1_s[:, :, g, :], ACT.Abs, accum_out=wsum[:, g:g + 1]).then_inc(s("wsum_ready"), 1)

        def weight_scales_vector(dve, do):
            dve.wait_ge(s("wsum_ps"), 1)
            do(nc.vector.tensor_scalar(wmean[:], bank(5)[:, 8:12], 1.0 / (D * D), 1e-5, ALU.mult, ALU.max))
            do(nc.vector.reciprocal(wscale[:], wmean[:]))
            do(nc.vector.tensor_tensor(qk_scale[:], wmean[:, 0:1], wmean[:, 1:2], ALU.mult))
            do(nc.vector.tensor_scalar(qk_scale[:], qk_scale[:], SCALE, None, ALU.mult))

        def quant_weights_vector(dve, do):
            ab = wscaleabs().rearrange("p (k g n) -> p k g n", k=DC, g=4)
            for g in range(4):
                step = do.post(nc.vector.tensor_scalar(ab[:, :, g, :], wa1_s[:, :, g, :], wscale[:, g:g + 1], HALF_EVEN, ALU.mult, ALU.add))
            do.until(step)
            for g in range(4):
                step = do.post(nc.vector.tensor_scalar(ab[:, :, g, :], ab[:, :, g, :], HALF_EVEN, 1.0, ALU.subtract, ALU.min))
            do.until(step)
            for g in range(4):
                nc.vector.tensor_scalar(wq1_s[:, :, g, :], ab[:, :, g, :], -1.0, None, ALU.max).then_inc(s("wq1_ready"), 1)

        def wscaleabs():
            return wide[:, 0:DC * 4 * D]

        def quant_weights_tensor(pe):
            pe.wait_ge(s("wsum_ready"), 4)
            nc.tensor.matmul(bank(5)[:, 8:12], table("ones"), wsum[:], start=True, stop=True).then_inc(s("wsum_ps"), 1)

        def quant_vector(dve, do, tile, tag, power, whole=None):
            if whole is not None:
                do(nc.vector.tensor_tensor(tokstat[:, :, 0], rstd[:], rstd[:], ALU.mult))
                nc.vector.tensor_tensor(stat2[:, :, 1], tokstat[:, :, 0], mv[:, :, 1], ALU.mult).then_inc(s("stat" + tag), 1)
                do.post(nc.vector.tensor_reduce(high[:], whole, AX.X, ALU.max))
                dve.wait_ge(s("img_ps" + tag), 1)
                nc.vector.tensor_scalar(img[:, 1:2], bank(7)[0:IMAGES, 1:2], 1.0 / SEQ, None, ALU.mult).then_inc(s("img" + tag), 1)
                extremes = do.post(nc.vector.tensor_reduce(low[:], whole, AX.X, ALU.min))
            else:
                for i in range(TILES):
                    dve.wait_ge(s("finished_a1"), i + 1)
                    counted = do.post(nc.vector.bn_stats(stats[:, i, 0, :], tile(i)))
                for i in range(TILES):
                    do.until(counted - TILES + 1 + i)
                    last = do.post(nc.vector.bn_aggr(mv[:, i, :], stats[:, i, 0:1, :]))
                do.until(last)
                do(nc.vector.tensor_tensor(stat2[:, :, 1], mv[:, :, 0], mv[:, :, 0], ALU.mult))
                do.post(nc.vector.tensor_tensor(stat2[:, :, 1], stat2[:, :, 1], mv[:, :, 1], ALU.add))
                nc.vector.tensor_copy(stat2[:, :, 0], mv[:, :, 0]).then_inc(s("stat" + tag), 1)
                for i in range(TILES):
                    do.post(nc.vector.tensor_reduce(high[:, i:i + 1], tile(i), AX.X, ALU.max))
                dve.wait_ge(s("img_ps" + tag), 1)
                do(nc.vector.tensor_scalar(img[:, 0:2], bank(7)[0:IMAGES, 0:2], 1.0 / SEQ, None, ALU.mult))
                do(nc.vector.tensor_tensor(img[:, 3:4], img[:, 0:1], img[:, 0:1], ALU.mult))
                nc.vector.tensor_tensor(img[:, 1:2], img[:, 1:2], img[:, 3:4], ALU.subtract).then_inc(s("img" + tag), 1)
                for i in range(TILES):
                    extremes = do.post(nc.vector.tensor_reduce(low[:, i:i + 1], tile(i), AX.X, ALU.min))
            dve.wait_ge(s("tok_ps" + tag), 1)
            of_token = bank(7)[:, 8:8 + 2 * TILES].rearrange("p (t a) -> p t a", a=2)
            nc.vector.tensor_scalar(veps[:], of_token[:, :, 1], 0.0, EPS, ALU.max, ALU.add).then_inc(s("veps_ready"), 1)
            do.until(extremes)
            if whole is None:
                do(nc.vector.tensor_copy(tokstat[:, :, 0], of_token[:, :, 0]))
                do.post(nc.vector.tensor_tensor(high[:], high[:], tokstat[:, :, 0], ALU.subtract))
                do(nc.vector.tensor_tensor(low[:], tokstat[:, :, 0], low[:], ALU.subtract))
            else:
                do(nc.vector.tensor_scalar(low[:], low[:], -1.0, None, ALU.mult))
            do(nc.vector.tensor_tensor(high[:], high[:], low[:], ALU.max))
            dve.wait_ge(s("rstd_ready"), power)
            do(nc.vector.tensor_tensor(amax[:], high[:], rstd[:], ALU.mult))
            do(nc.vector.tensor_scalar(amax[:], amax[:], 1e-5, None, ALU.max))
            inverted = do.post(nc.vector.reciprocal(act_s[:], amax[:]))
            nc.vector.tensor_scalar(inv_s[:], amax[:], 1.0 / 127.0, None, ALU.mult).then_inc(s("inverse" + tag), 1)
            do.until(inverted)
            scaled = do.post(nc.vector.tensor_scalar(act_s[:], act_s[:], 127.0, None, ALU.mult))
            for i in range(TILES):
                if whole is None:
                    normed = do.post(nc.vector.tensor_scalar(z[:, i, :], tile(i), tokstat[:, i, 0:1], rstd[:, i:i + 1], ALU.subtract, ALU.mult))
                else:
                    normed = do.post(nc.vector.tensor_scalar(z[:, i, :], tile(i), rstd[:, i:i + 1], None, ALU.mult))
            do.until(scaled)
            first = normed - TILES + 1
            for i in range(TILES + 1):
                if i < TILES:
                    do.until(first + i)
                    rounded = do.post(nc.vector.tensor_scalar(z[:, i, :], z[:, i, :], act_s[:, i:i + 1], HALF_EVEN, ALU.mult, ALU.add))
                if i > 0:
                    do.until(rounded - 1 if i < TILES else rounded)
                    nc.vector.tensor_scalar(z[:, i - 1, :], z[:, i - 1, :], HALF_EVEN + 127.0, HALF_EVEN - 128.0,
                                            ALU.min, ALU.max).then_inc(s("rounded" + tag), 1)

        def quant_tensor(pe, tag):
            first = 1 if tag == "_x1" else 0
            if tag == "_x1":
                pe.wait_ge(s("z_back3"), 16)
            keep_warm(pe, 6, 3 * WARM_MATMULS // 2 if tag == "_x1" else WARM_MATMULS)
            pe.wait_ge(s("stat" + tag), 1)
            for i in range(TILES):
                last = nc.tensor.matmul(bank(7)[0:IMAGES, first:2], table("of_image")[:, i * IMAGES:(i + 1) * IMAGES], stat2[:, i, first:2],
                                        start=(i == 0), stop=(i == TILES - 1))
            last.then_inc(s("img_ps" + tag), 1)
            keep_warm(pe, 6, 4)
            pe.wait_ge(s("img" + tag), 1)
            for i in range(TILES):
                last = nc.tensor.matmul(bank(7)[:, 8 + 2 * i + first:8 + 2 * i + 2], image_of[:, i * P:(i + 1) * P], img[:, first:2],
                                        start=True, stop=True)
            last.then_inc(s("tok_ps" + tag), 1)
            keep_warm(pe, 6, WARM_MATMULS)
            if tag == "_x1":
                pe.wait_ge(s("spread"), 1)
                for i in range(TILES):
                    last = nc.tensor.transpose(two_banks(0)[:, i * P:(i + 1) * P], spread[:, i, :], ident)
                last.then_inc(s("invT_ps"), 1)
            for i in range(TILES):
                pe.wait_ge(s("xq" + tag), i + 1)
                if i >= 2:
                    pe.wait_ge(s("xqT" + tag), i - 1)
                for c in range(DC):
                    last = nc.tensor.transpose(turned_bf16(i)[:, c * P:(c + 1) * P], xqb[:, i, c * P:(c + 1) * P], identb[:])
                last.then_inc(s("xqT_ps" + tag), 1)
                if tag == "_x1":
                    keep_warm(pe, 4, 2)

        def turned_bf16(i):
            return psum[:, 5 + i % 2, :].bitcast(BF16)[:, 0:DC * P]

        def quant_scalar(act, tag):
            def whole_numbers(i):
                act.wait_ge(s("rounded" + tag), i + 1)
                nc.scalar.activation(xqb[:, i, :], z[:, i, :], ACT.Identity, bias=minus_half_even[:]).then_inc(s("xq" + tag), 1)

            def channel_major(i):
                act.wait_ge(s("xqT_ps" + tag), i + 1)
                nc.scalar.activation(xTb[:, :, i * P:(i + 1) * P], turned_bf16(i).rearrange("p (c n) -> p c n", n=P),
                                     ACT.Copy).then_inc(s("xqT" + tag), 1)
            if tag == "_x1":
                act.wait_ge(s("inverse_x1"), 1)
                nc.scalar.activation(spread[:], inv_s[:].rearrange("p (t o) -> p t o", o=1).to_broadcast([P, TILES, P]),
                                     ACT.Copy).then_inc(s("spread"), 1)
            whole_numbers(0)
            if tag == "_x1":
                act.wait_ge(s("invT_ps"), 1)
                nc.scalar.activation(invT[:], two_banks(0), ACT.Copy).then_inc(s("invT_ready"), 1)
            for i in range(1, TILES):
                whole_numbers(i)
                channel_major(i - 1)
            channel_major(TILES - 1)

        block = ctx.enter_context(nc.Block())

        @block.sync
        def _(sp):
            loads(sp)
            attn0[4](sp)
            moe0[4](sp)
            moe1[4](sp)
            for i in range(TILES):
                n = min(P, TOKENS - i * P)
                sp.wait_ge(s("out_ready"), i + 1)
                sp.dma_start(out[i * P:i * P + n, :], h[0:n, i, :]).then_inc(s("out_stored"), 16)
            sp.wait_ge(s("out_stored"), 16 * TILES)

        @block.gpsimd
        def _(pool):
            powers = [NORMS]

            def power():
                pool.wait_ge(s("veps_ready"), powers[0] + 1)
                nc.gpsimd.tensor_tensor(rstd[:], veps[:], table("minus_half"), ALU.pow).then_inc(s("rstd_ready"), 1)
                powers[0] += 1

            embed_gpsimd(pool)
            pool.wait_ge(s("in_const"), 32)
            attn0[2](pool)
            power()
            power()
            moe0[3](pool)
            power()
            power()
            attn1[2](pool)
            power()
            power()
            moe1[3](pool)

        @block.scalar
        def _(act):
            do = Chain(act, "act_own")
            embed_scalar(act, do)
            turn_scalar(act, xT, 0)
            attn0[3](act)
            quant_weights_scalar(act)
            turn_scalar(act, xT, 1)
            moe0[2](act)
            moe0[7](act)
            quant_scalar(act, "_x1")
            attn1[3](act)
            quant_scalar(act, "_o1")
            turn_scalar(act, xT, 2)
            moe1[2](act)
            moe1[7](act)

        @block.tensor
        def _(pe):
            embed_tensor(pe)
            pe.wait_ge(s("turned"), TILES)
            pe.wait_ge(s("in_attn0"), 64)
            attn0[0](pe)
            quant_weights_tensor(pe)
            keep_warm(pe, 6, WARM_MATMULS)
            turn_tensor(pe, x, 1, 1)
            moe0[0](pe)
            moe0[5](pe)
            quant_tensor(pe, "_x1")
            pe.wait_ge(s("invT_ready"), 1)
            pe.wait_ge(s("wq1_ready"), 4)
            pe.wait_ge(s("xqT_x1"), TILES)
            attn1[0](pe)
            quant_tensor(pe, "_o1")
            for i in range(TILES):
                pe.wait_ge(s("xqT_o1"), i + 1)
                for c in range(DC):
                    last = nc.tensor.matmul(tile_bank(i), xTb[:, c, i * P:(i + 1) * P], wq1_s[:, c, 3, :], start=(c == 0), stop=(c == DC - 1))
                last.then_inc(s("y_attn1"), 1)
            keep_warm(pe, 6, WARM_MATMULS)
            turn_tensor(pe, x, 3, 2)
            moe1[0](pe)
            moe1[5](pe)

        @block.vector
        def _(dve):
            do = Chain(dve, "dve_own")
            embed_vector(dve, do)
            attn0[1](dve, do)
            def add_projection(i):
                dve.wait_ge(s("finished_a0"), i + 1)
                return nc.vector.tensor_tensor(h[:, i, :], tile_bank(i), h[:, i, :], ALU.add)
            norm_vector(dve, do, h, x, NORMS + 1, add_projection)
            moe0[1](dve, do)
            moe0[6](dve, do)
            for i in range(TILES):
                last = do.post(nc.vector.tensor_tensor(h[:, i, :], h[:, i, :], x[:, i, :], ALU.add))
            do.until(last)

            def add_expert(back):
                def add(i):
                    dve.wait_ge(s(f"z_back{i}"), back)
                    return nc.vector.scalar_tensor_tensor(out=h[:, i, :], in0=z[:, i, :], scalar=gate[:, i:i + 1], in1=h[:, i, :],
                                                          op0=ALU.mult, op1=ALU.add)
                return add
            norm_vector(dve, do, h, x, NORMS + 3, add_expert(16))
            dve.wait_ge(s("x_normed"), 3 * TILES)
            quant_vector(dve, do, lambda i: x[:, i, :], "_x1", NORMS + 4, whole=x[:])
            dve.wait_ge(s("invT_ready"), 1)
            attn1[1](dve, do)
            quant_vector(dve, do, tile_bank, "_o1", NORMS + 5)
            do(nc.vector.tensor_scalar(rsmall[:], inv_s[:], wmean[:, 3:4], None, ALU.mult))

            def add_projection1(i):
                dve.wait_ge(s("y_attn1"), i + 1)
                return nc.vector.scalar_tensor_tensor(out=h[:, i, :], in0=tile_bank(i), scalar=rsmall[:, i:i + 1], in1=h[:, i, :],
                                                      op0=ALU.mult, op1=ALU.add)
            norm_vector(dve, do, h, x, NORMS + 6, add_projection1)
            moe1[1](dve, do)
            moe1[6](dve, do)
            for i in range(TILES):
                dve.wait_ge(s(f"z_back{i}"), 32)
                nc.vector.scalar_tensor_tensor(out=h[:, i, :], in0=z[:, i, :], scalar=gate[:, i:i + 1], in1=h[:, i, :],
                                               op0=ALU.mult, op1=ALU.add).then_inc(s("out_ready"), 1)


def kernel(**inputs):
    import concourse.bacc as bacc
    from concourse.bass_utils import run_bass_kernel_spmd

    a = {k: np.asarray(v) for k, v in inputs.items()}

    def rows(w):
        return w.reshape(w.shape[0] // P, P, *w.shape[1:]).swapaxes(0, 1)

    def col(v):
        return v.reshape(-1, P).T

    patches = a["x"].reshape(IMAGES, CHANNELS, GRID, PATCH, GRID, PATCH).transpose(0, 2, 4, 3, 5, 1).reshape(IMAGES, SEQ - 1, PD)
    xp = np.zeros((ROWS, PD), np.float32)
    xp[:TOKENS].reshape(IMAGES, SEQ, PD)[:, 1:] = patches
    wq, wk, wv = a["L0_attn_Wq"], a["L0_attn_Wk"], a["L0_attn_Wv"]
    bq, bk, bv = a["L0_attn_bq"], a["L0_attn_bk"], a["L0_attn_bv"]
    e1 = a["L0_ffn_w1"].transpose(0, 2, 1).reshape(EXPERTS, DC, P, FF).transpose(0, 2, 1, 3)
    e2 = a["L0_ffn_w2"].transpose(0, 2, 1).reshape(EXPERTS, FC, P, D).transpose(0, 2, 1, 3)
    f1 = a["L1_ffn_w1"].reshape(EXPERTS, DC, P, 2 * FF).transpose(0, 2, 1, 3)
    f2 = a["L1_ffn_w2"].reshape(EXPERTS, FC, P, D).transpose(0, 2, 1, 3)
    by_expert = lambda v: v.reshape(EXPERTS, -1, P).transpose(0, 2, 1)
    arrays = {
        "xp": rows(xp),
        "cls_ln2b": np.stack([a["cls_tok"].reshape(D), a["L0_tok_ln2_b"]]),
        "Wp": rows(a["L0_tok_Wp"]),
        "ln1": np.stack([col(a["L0_tok_ln1_g"]), col(a["L0_tok_ln1_b"])], 1),
        "bp": a["L0_tok_bp"],
        "ln2_g": a["L0_tok_ln2_g"],
        "const": CONST,
        "const_rows": CONST_ROWS,
        "wa0": np.stack([rows(w.T) for w in (wq, wk, wv)], 2),
        "ba0": np.stack([col(b) for b in (bq, bk, bv)], 1),
        "wo0": rows(a["L0_attn_Wo"].T),
        "bo0": a["L0_attn_bo"],
        "cent": rows(a["L0_ffn_centroids"].T),
        "w1_0": e1.reshape(EXPERTS, P, DC * FF),
        "w2_0": e2.reshape(EXPERTS, P, FC * D),
        "par_0": np.concatenate([by_expert(a["L0_ffn_ln_g"]), by_expert(a["L0_ffn_ln_b"]), by_expert(a["L0_ffn_b1"])], 2),
        "b2_0": a["L0_ffn_b2"],
        "wa1": np.stack([rows(a[f"L1_attn_w_{n}"].T) for n in "qkvo"], 2),
        "router": rows(a["L1_ffn_router_w"]),
        "router_b": a["L1_ffn_router_b"],
        "w1_1": f1.reshape(EXPERTS, P, DC * 2 * FF),
        "w2_1": f2.reshape(EXPERTS, P, FC * D),
    }
    nc = bacc.Bacc("TRN2", target_bir_lowering=False, num_devices=1)
    args = {}
    for name, array in arrays.items():
        array = np.ascontiguousarray(array)
        arrays[name] = array
        args[name] = nc.dram_tensor(name, array.shape, mybir.dt.from_np(array.dtype), kind="ExternalInput").ap()
    out = nc.dram_tensor("out", (TOKENS, D), F32, kind="ExternalOutput").ap()
    vit_tower(nc, *args.values(), out)
    got = run_bass_kernel_spmd(nc, [arrays], core_ids=[0])
    return got.results[0]["out"].reshape(IMAGES, SEQ, D)
```
